# Optimizing a Trainium2 kernel written in Bass

```python
import numpy as np
import jax
import jax.numpy as jnp

def _softmax(x, axis=-1):
    return jax.nn.softmax(x, axis=axis)

def _gelu(x):
    return jax.nn.gelu(x, approximate=True)

def _silu(x):
    return jax.nn.silu(x)

def _sigmoid(x):
    return jax.nn.sigmoid(x)

def _layernorm(x, axis=-1, eps=1e-05):
    m = jnp.mean(x, axis=axis, keepdims=True)
    v = jnp.var(x, axis=axis, keepdims=True)
    return (x - m) / jnp.sqrt(v + eps)

def _scatter_add(tgt, idx, src, axis=0):
    return tgt.at[idx].add(src)

def _segment_sum(src, seg, n):
    return jax.ops.segment_sum(src, seg, n)
kernel_name = 'mk_prb_d1_jaxref_r4_513f70'

def setup_inputs(seed: int=0):
    np.random.seed(seed)
    _w = jnp.asarray

    def _L0_attn_setup():
        import jax, jax.numpy as jnp
        import numpy as np
        BLOCK = 64
        EPS = 1e-06

        def _silu(x):
            return x * jax.nn.sigmoid(x)
        key = jax.random.key(seed)
        k1, k2, k3, k4 = jax.random.split(key, 4)
        embed_dim, hidden_dim = (512, 512)
        b, n, h = (2, 1024, 16)
        x = jax.random.normal(k1, (b, n, embed_dim), dtype=jnp.float32)
        slope_rate = jax.random.uniform(k2, (h, 1, 1), dtype=jnp.float32, minval=0.01, maxval=1.0)
        W_qkvu = jax.random.normal(k3, (4 * hidden_dim, embed_dim), dtype=jnp.float32) / np.sqrt(embed_dim)
        W_out = jax.random.normal(k4, (embed_dim, hidden_dim), dtype=jnp.float32) / np.sqrt(hidden_dim)
        return {'x': x, 'slope_rate': slope_rate, 'W_qkvu': W_qkvu, 'W_out': W_out}
    _L0_attn_in = _L0_attn_setup()

    def _L0_ffn_setup():
        import jax, jax.numpy as jnp
        import numpy as np
        CAPACITY = 0.125
        HEAD_DIM = 128
        N_HEADS = 16
        N_KV_HEADS = 8
        ROPE_THETA = 10000.0
        EPS = 1e-06

        def _rms_norm(x, w):
            return x * jax.lax.rsqrt(jnp.mean(x * x, axis=-1, keepdims=True) + EPS) * w

        def _rotate_half(t):
            h = t.shape[-1] // 2
            return jnp.concatenate([-t[..., h:], t[..., :h]], axis=-1)
        key = jax.random.key(seed)
        ks = jax.random.split(key, 12)
        B, T, D = (4, 1024, 512)
        I = 2048
        s = 0.02
        return {'hidden_states': jax.random.normal(ks[0], (B, T, D), jnp.float32), 'w_router': jax.random.normal(ks[1], (D,), jnp.float32) * s, 'wq': jax.random.normal(ks[2], (D, N_HEADS * HEAD_DIM), jnp.float32) * s, 'bq': jnp.zeros((N_HEADS * HEAD_DIM,), jnp.float32), 'wk': jax.random.normal(ks[3], (D, N_KV_HEADS * HEAD_DIM), jnp.float32) * s, 'bk': jnp.zeros((N_KV_HEADS * HEAD_DIM,), jnp.float32), 'wv': jax.random.normal(ks[4], (D, N_KV_HEADS * HEAD_DIM), jnp.float32) * s, 'bv': jnp.zeros((N_KV_HEADS * HEAD_DIM,), jnp.float32), 'wo': jax.random.normal(ks[5], (N_HEADS * HEAD_DIM, D), jnp.float32) * s, 'w_gate': jax.random.normal(ks[6], (D, I), jnp.float32) * s, 'w_up': jax.random.normal(ks[7], (D, I), jnp.float32) * s, 'w_down': jax.random.normal(ks[8], (I, D), jnp.float32) * s, 'ln1_w': jnp.ones((D,), jnp.float32), 'ln2_w': jnp.ones((D,), jnp.float32)}
    _L0_ffn_in = _L0_ffn_setup()
    _d = {'L0_attn_x': _L0_attn_in['x'], 'L0_attn_slope_rate': _L0_attn_in['slope_rate'], 'L0_attn_W_qkvu': _L0_attn_in['W_qkvu'], 'L0_attn_W_out': _L0_attn_in['W_out'], 'L0_ffn_w_router': _L0_ffn_in['w_router'], 'L0_ffn_wq': _L0_ffn_in['wq'], 'L0_ffn_bq': _L0_ffn_in['bq'], 'L0_ffn_wk': _L0_ffn_in['wk'], 'L0_ffn_bk': _L0_ffn_in['bk'], 'L0_ffn_wv': _L0_ffn_in['wv'], 'L0_ffn_bv': _L0_ffn_in['bv'], 'L0_ffn_wo': _L0_ffn_in['wo'], 'L0_ffn_w_gate': _L0_ffn_in['w_gate'], 'L0_ffn_w_up': _L0_ffn_in['w_up'], 'L0_ffn_w_down': _L0_ffn_in['w_down'], 'L0_ffn_ln1_w': _L0_ffn_in['ln1_w'], 'L0_ffn_ln2_w': _L0_ffn_in['ln2_w']}
    _x0 = _d['L0_attn_x']
    _d['L0_attn_x'] = jax.random.normal(jax.random.fold_in(jax.random.key(seed), 1), (1, 2048, 512), dtype=_x0.dtype)
    del _x0
    return _d

def reference(L0_attn_x, L0_attn_slope_rate, L0_attn_W_qkvu, L0_attn_W_out, L0_ffn_w_router, L0_ffn_wq, L0_ffn_bq, L0_ffn_wk, L0_ffn_bk, L0_ffn_wv, L0_ffn_bv, L0_ffn_wo, L0_ffn_w_gate, L0_ffn_w_up, L0_ffn_w_down, L0_ffn_ln1_w, L0_ffn_ln2_w):

    def _L0_attn_ref(x, slope_rate, W_qkvu, W_out):
        import jax, jax.numpy as jnp
        import numpy as np
        BLOCK = 64
        EPS = 1e-06

        def _silu(x):
            return x * jax.nn.sigmoid(x)
        b, n, embed_dim = x.shape
        h = slope_rate.shape[0]
        hidden_dim = W_qkvu.shape[0] // 4
        d = hidden_dim // h
        NB = n // BLOCK
        qkvu = x @ W_qkvu.T
        q, k, v, u = jnp.split(qkvu, 4, axis=-1)

        def to_heads(t):
            return t.reshape(b, n, h, d).transpose(0, 2, 1, 3)
        q = _silu(to_heads(q))
        k = _silu(to_heads(k))
        v = to_heads(v)
        s = slope_rate
        arr = jnp.arange(1, BLOCK + 1, dtype=x.dtype)
        q_decay = jnp.exp(-s * arr[:, None])
        k_decay = jnp.exp(-s * (BLOCK - arr[:, None]))
        idx = arr[:, None] - arr[None, :]
        diag_decay = jnp.exp(jnp.where(idx >= 0, -s * idx, -jnp.inf))
        block_decay = jnp.exp(-s * BLOCK)

        def blk(t):
            return t.reshape(b, h, NB, BLOCK, d).transpose(2, 0, 1, 3, 4)
        qb, kb, vb = (blk(q), blk(k), blk(v))

        def step(kv, inp):
            qi, ki, vi = inp
            qkv_none_diag = jnp.einsum('bhmd,bhde->bhme', qi * q_decay, kv)
            qk = jnp.einsum('bhmd,bhsd->bhms', qi, ki) * diag_decay
            qkv_diag = jnp.einsum('bhms,bhse->bhme', qk, vi)
            kv_new = block_decay * kv + jnp.einsum('bhsd,bhse->bhde', ki * k_decay, vi)
            return (kv_new, qkv_none_diag + qkv_diag)
        kv0 = jnp.zeros((b, h, d, d), dtype=jnp.float32)
        _, outs = jax.lax.scan(step, kv0, (qb, kb, vb))
        o = outs.transpose(1, 2, 0, 3, 4).reshape(b, h, n, d)
        o = o.transpose(0, 2, 1, 3).reshape(b, n, hidden_dim)
        o = o * jax.lax.rsqrt(jnp.mean(o * o, axis=-1, keepdims=True) + EPS)
        o = u * o
        return o @ W_out.T

    def _L0_ffn_ref(hidden_states, w_router, wq, bq, wk, bk, wv, bv, wo, w_gate, w_up, w_down, ln1_w, ln2_w):
        import jax, jax.numpy as jnp
        import numpy as np
        CAPACITY = 0.125
        HEAD_DIM = 128
        N_HEADS = 16
        N_KV_HEADS = 8
        ROPE_THETA = 10000.0
        EPS = 1e-06

        def _rms_norm(x, w):
            return x * jax.lax.rsqrt(jnp.mean(x * x, axis=-1, keepdims=True) + EPS) * w

        def _rotate_half(t):
            h = t.shape[-1] // 2
            return jnp.concatenate([-t[..., h:], t[..., :h]], axis=-1)
        B, T, D = hidden_states.shape
        k = max(1, int(T * CAPACITY))
        scores = jnp.einsum('btd,d->bt', hidden_states, w_router)
        _, idx = jax.lax.top_k(scores, k)
        idx = jnp.sort(idx, axis=-1)
        b = jnp.arange(B)[:, None]
        sel = hidden_states[b, idx]
        sel_scores = scores[b, idx]
        S = B * k
        x = sel.reshape(S, D)
        pos = idx.reshape(S)
        inv_freq = 1.0 / ROPE_THETA ** (jnp.arange(0, HEAD_DIM, 2, dtype=jnp.float32) / HEAD_DIM)
        ang = pos.astype(jnp.float32)[:, None] * inv_freq
        cos = jnp.concatenate([jnp.cos(ang), jnp.cos(ang)], axis=-1)[:, None, :]
        sin = jnp.concatenate([jnp.sin(ang), jnp.sin(ang)], axis=-1)[:, None, :]
        h = _rms_norm(x, ln1_w)
        q = (h @ wq + bq).reshape(S, N_HEADS, HEAD_DIM)
        kk = (h @ wk + bk).reshape(S, N_KV_HEADS, HEAD_DIM)
        v = (h @ wv + bv).reshape(S, N_KV_HEADS, HEAD_DIM)
        q = q * cos + _rotate_half(q) * sin
        kk = kk * cos + _rotate_half(kk) * sin
        rep = N_HEADS // N_KV_HEADS
        kk = jnp.repeat(kk, rep, axis=1)
        v = jnp.repeat(v, rep, axis=1)
        att = jnp.einsum('shd,thd->hst', q, kk) / np.sqrt(HEAD_DIM)
        causal = jnp.tril(jnp.ones((S, S), bool))
        att = jnp.where(causal[None], att, jnp.finfo(att.dtype).min)
        att = jax.nn.softmax(att, axis=-1)
        attn_out = jnp.einsum('hst,thd->shd', att, v).reshape(S, N_HEADS * HEAD_DIM) @ wo
        x1 = x + attn_out
        h2 = _rms_norm(x1, ln2_w)
        mlp = jax.nn.silu(h2 @ w_gate) * (h2 @ w_up) @ w_down
        processed = x1 + mlp
        gate = jax.nn.sigmoid(sel_scores).reshape(S, 1)
        gated = gate * processed + (1.0 - gate) * x
        output = hidden_states.at[b, idx].set(gated.reshape(B, k, D))
        return output
    x = L0_attn_x
    xn = _layernorm(x, axis=-1)
    x = x + _L0_attn_ref(xn, L0_attn_slope_rate, L0_attn_W_qkvu, L0_attn_W_out) + _L0_ffn_ref(xn, L0_ffn_w_router, L0_ffn_wq, L0_ffn_bq, L0_ffn_wk, L0_ffn_bk, L0_ffn_wv, L0_ffn_bv, L0_ffn_wo, L0_ffn_w_gate, L0_ffn_w_up, L0_ffn_w_down, L0_ffn_ln1_w, L0_ffn_ln2_w)
    return x

_drawn_inputs = setup_inputs


def setup_inputs(seed=0):
    import zlib

    import numpy as np

    out = dict(_drawn_inputs(seed))
    spreads = {'L0_ffn_bq': (0.0, 0.8),
     'L0_ffn_bk': (0.0, 0.8),
     'L0_ffn_bv': (0.0, 0.749),
     'L0_ffn_ln1_w': (1.0, 0.6),
     'L0_ffn_ln2_w': (1.0, 0.6)}
    factors = {'L0_ffn_w_router': 3.313,
     'L0_ffn_wq': 8.0,
     'L0_ffn_wk': 8.0,
     'L0_ffn_wv': 6.248,
     'L0_ffn_wo': 4.257,
     'L0_ffn_w_gate': 4.976,
     'L0_ffn_w_up': 4.856,
     'L0_ffn_w_down': 4.886}
    for name, (base, spread) in spreads.items():
        noise = np.random.default_rng([zlib.crc32(name.encode()), seed]).standard_normal(out[name].shape)
        drawn = base * np.exp(spread * noise) if base else spread * noise
        out[name] = jnp.asarray(drawn.astype(out[name].dtype))
    for name, factor in factors.items():
        out[name] = (out[name] * factor).astype(out[name].dtype)
    return out
```

```python
import concourse.bass as bass
from concourse import mybir
from contextlib import ExitStack

P = 128
N_TOK, DM = 2048, 512
NH, DH = 16, 32
NK = DM // P
GROUP = 512
G = N_TOK // GROUP
CH = GROUP // P
N_TILES = N_TOK // P
SEL = N_TOK // 8
NS = SEL // P
FH, FKV, FD = 16, 8, 128
FF = 2048
NPROJ = 16


def build(nc, x, WT, WoT, s_hid, s_row, s_head, w_router, wq, bq, wk, bk, wv, bv, wo, w_gate, w_up,
          w_down, ln1, ln2, rope, scores, out):
    f32, f32r, bf16, i32 = mybir.dt.float32, mybir.dt.float32r, mybir.dt.bfloat16, mybir.dt.int32
    ALU, ACT = mybir.AluOpType, mybir.ActivationFunctionType
    V, S, T, Q = nc.vector, nc.scalar, nc.tensor, nc.gpsimd

    x_g = x.rearrange("(g c p) d -> g p c d", c=CH, p=P)
    out_t = out.rearrange("(n p) d -> n p d", p=P)
    WT_v = WT.rearrange("(k p) n -> p k n", p=P)
    WoT_v = WoT.rearrange("(k p) n -> p k n", p=P)
    scores_g = scores.rearrange("(g c p) -> g p c", c=CH, p=P)
    scores_t = scores.rearrange("(n p) -> p n", p=P)

    ctx = ExitStack()
    with ctx:
        def sb(name, shape, dt=f32, c=ctx):
            return c.enter_context(nc.sbuf_tensor(name, shape, dt))

        ident = sb("ident", [P, P])
        tri = sb("tri", [P, P], bf16)
        below = sb("below", [P, P], bf16)
        above = sb("above", [P, P], bf16)
        ones_sq = sb("ones_sq", [P, P], bf16)
        XN = sb("XN", [P, CH, DM])
        small = sb("small", [P, 200])
        taken = [0]

        def col(n):
            taken[0] += n
            assert taken[0] <= 200
            return small[:, taken[0] - n:taken[0]]

        rstd, sd_ln = col(CH), col(CH)
        shid, nshid, bdec = col(NK), col(NK), col(NK)
        shead, nshead = col(NH), col(NH)
        age, eps_ln, eps_rms, ones1, sd_o, r_o = (col(1) for _ in range(6))
        s_col, n_ge, n_gt, n_eq, rank, chosen, place, before = (col(N_TILES) for _ in range(8))
        stats = sb("stats", [P, CH, 6])
        mv = sb("mv", [P, CH, 2])
        score4 = sb("score4", [P, 2, CH])
        chosen_b = sb("chosen_b", [P, N_TILES], bf16)
        tok2 = sb("tok2", [P, N_TILES, 2], bf16)
        idx_f = sb("idx_f", [P, 2 * NS])
        idx = sb("idx", [P, NS], i32)
        wr_b = sb("wr_b", [P, DM])

        slots = sb("slots", [P, SEL], bf16)

        ca = ExitStack()
        Wh, Wl = (sb(n, [P, NK, 4 * DM], f32r, ca) for n in ("Wh", "Wl"))
        Woh, Wol = (sb(n, [P, NK, DM], f32r, ca) for n in ("Woh", "Wol"))
        xTh, xTl = (sb(n, [P, NK, GROUP], f32r, ca) for n in ("xTh", "xTl"))
        X, BASE = (sb(n, [P, CH, DM], f32, ca) for n in ("X", "BASE"))
        KT, QT, UT = (sb(n, [P, NK, GROUP], f32, ca) for n in ("KT", "QT", "UT"))
        VT = sb("VT", [P, CH, DM], f32, ca)
        kh, kl, qh, ql = (sb(n, [P, NK, P], f32r, ca) for n in ("kh", "kl", "qh", "ql"))
        qdec, uo, sq = (sb(n, [P, NK, P], f32, ca) for n in ("qdec", "uo", "sq"))
        uoh, uol = (sb(n, [P, NK, P], f32r, ca) for n in ("uoh", "uol"))
        kdec = sb("kdec", [P, DM], f32, ca)
        DEC = sb("DEC", [P, NH, P], f32, ca)
        QD = sb("QD", [P, NK, P], f32, ca)
        KD = sb("KD", [P, DM], f32, ca)
        A = sb("A", [P, NH, P], f32, ca)
        R = sb("R", [P, 2, DM], f32, ca)
        state, state_dec, kv_new = (sb(n, [P, NK, P], f32, ca) for n in ("state", "state_dec", "kv_new"))
        BM = sb("BM", [P, P], f32, ca)
        ca.close()
        raw_qkvu = [KT, QT, VT, UT]
        raw_wo = A[:].rearrange("p (k h) m -> p k (h m)", k=NK)
        flat_x = X[:].rearrange("p c d -> p (c d)")
        s_bc = XN[:].rearrange("p c d -> p (c d)")
        one_hot = flat_x.bitcast(bf16).rearrange("p (n s) -> p n s", n=N_TILES)
        lag = kv_new[:, 0, :]
        ahead = kv_new[:, 1, :]

        cb = ExitStack()
        raw = [sb(f"raw{i}", [P, 4, DM], f32, cb) for i in range(2)]
        whi = [sb(f"whi{i}", [P, 4, DM], f32r, cb) for i in range(3)]
        wlo = [sb(f"wlo{i}", [P, 4, DM], f32r, cb) for i in range(3)]
        QRh, QRl = (sb(n, [P, FH, SEL], f32r, cb) for n in ("QRh", "QRl"))
        KRh, KRl = (sb(n, [P, FKV, SEL], f32r, cb) for n in ("KRh", "KRl"))
        Vh, Vl = (sb(n, [P, NS, FKV * FD], f32r, cb) for n in ("Vh", "Vl"))
        HT = sb("HT", [P, NK, SEL], f32, cb)
        HTh, HTl = (sb(n, [P, NK, SEL], f32r, cb) for n in ("HTh", "HTl"))
        xsn, hs, ao = (sb(n, [P, NS, DM], f32, cb) for n in ("xsn", "hs", "ao"))
        CS = sb("CS", [P, 2, SEL], f32, cb)
        bvb = sb("bvb", [P, FKV * FD], f32, cb)
        bqk = sb("bqk", [P, FKV + FH], f32, cb)
        ln12 = sb("ln12", [P, 2, NK], f32, cb)
        qb = sb("qb", [P, 2, 2, SEL], f32, cb)
        rope1, rope2 = (sb(n, [P, 2, SEL], f32, cb) for n in ("rope1", "rope2"))
        staged = sb("staged", [P, 2, 2 * SEL], f32, cb)
        causal, SM, PR = (sb(n, [P, 3 * P], f32, cb) for n in ("causal", "SM", "PR"))
        PN = sb("PN", [P, 2, 3 * P], f32, cb)
        PTh, PTl = (sb(n, [P, 2, 3 * P], f32r, cb) for n in ("PTh", "PTl"))
        OTh, OTl = (sb(n, [P, 2, SEL], f32r, cb) for n in ("OTh", "OTl"))
        sg = sb("sg", [P, 2, 2 * SEL], f32, cb)
        fsmall = sb("fsmall", [P, 48], f32, cb)
        cb.close()
        xs, tab = XN[:, 0:NS, :], XN[:, NS, :]
        top, ntop, psum_, pinv = (fsmall[:, 4 * n:4 * n + 4].rearrange("p (a b) -> p a b", a=2) for n in range(4))
        sel_score, gate, sumsq, sd_s, r_s = (fsmall[:, 16 + 2 * n:18 + 2 * n] for n in range(5))
        scrap = staged[:, 0, :]

        def wide(w):
            return lambda i: w.rearrange("(k p) n -> p k n", p=P)[:, :, i * DM:(i + 1) * DM]

        def tall(w):
            return lambda i: w.rearrange("(h p) n -> p h n", p=P)[:, 4 * i:4 * i + 4, :]

        source = {"K": wide(wk), "V": wide(wv), "Q": wide(wq), "O": tall(wo), "G": wide(w_gate), "U": wide(w_up),
                  "D": tall(w_down)}
        order = ["K0", "K1", "V0", "V1", "Q0", "Q1", "O0", "Q2", "O1", "Q3", "O2", "O3",
                 "G0", "U0", "G1", "U1", "D0", "G2", "U2", "D1", "G3", "U3", "D2", "D3"]
        block_of = {k: n for n, k in enumerate(order)}
        units = [(k, p) for k in ("K0", "K1", "V0", "V1", "Q0", "Q1", "Q2", "Q3") for p in range(2)]
        before_heads = 10
        STEPS = FH + 3

        def unit_of_step(h):
            return before_heads + h // 2 if h % 2 == 0 and before_heads + h // 2 < len(units) else None

        def kq_unit(h):
            return 9 + h // 2 if h >= 4 else before_heads

        def kq_count(u):
            return sum(units[n][0][0] != "V" for n in range(u + 1))

        split_after = {2: "O1", 6: "Q3", 7: "O2", 11: "O3", 12: "G0", 15: "U0"}

        B = [ctx.enter_context(nc.psum_tensor(f"bank{i}", [P, 512], f32)) for i in range(8)]

        def tiles4(ap):
            return ap.rearrange("p (k m) -> p k m", k=4)

        def sems(names):
            return [ctx.enter_context(nc.semaphore(n)) for n in names.split()]

        class Chain:

            def __init__(self, eng, done):
                self.eng, self.done, self.n = eng, done, 0

            def link(self, ins):
                self.n += 1
                ins.then_inc(self.done, 1)
                self.eng.wait_ge(self.done, self.n)

        x_in, const_in, scol_in, sbc_in, score_out = sems("x_in const_in scol_in sbc_in score_out")
        w_raw = sems("w_raw_k w_raw_q w_raw_v w_raw_u w_raw_o")
        stored = sems("stored_even stored_odd")
        raw_in = sems("raw_in_even raw_in_odd")
        part_in, picked, scattered = sems("part_in picked scattered")
        consts, slopes_ok, iota_ok, masks_ok, tok_ok, lag_ok = sems("consts slopes_ok iota_ok masks_ok tok_ok lag_ok")
        decays_ok, dec_ok, bm_ok, causal_ok = sems("decays_ok dec_ok bm_ok causal_ok")
        w_hi, w_lo, w_lo_pool = sems("w_hi w_lo w_lo_pool")
        var_ok, sd_ln_ok, xn_ok, score_ok, base_ok = sems("var_ok sd_ln_ok xn_ok score_ok base_ok")
        xt_ps, xt_hi, xt_lo, proj_ps, proj_sb = sems("xt_ps xt_hi xt_lo proj_ps proj_sb")
        k_hi, q_hi, k_lo, q_lo, q_dec, kt_ps, k_dec = sems("k_hi q_hi k_lo q_lo q_dec kt_ps k_dec")
        s_ps, masked, inter_ps, kv_ps, pv_ps = sems("s_ps masked inter_ps kv_ps pv_ps")
        state_dk, state_ok, uo_ok, sq_ok, uo_hi, uo_lo = sems("state_dk state_ok uo_ok sq_ok uo_hi uo_lo")
        rms_ps, sd_o_ok, out_ps, final_ok = sems("rms_ps sd_o_ok out_ps final_ok")
        rank_ok, cnt_ps, oh_ok, idx_ps, idx_ok = sems("rank_ok cnt_ps oh_ok idx_ps idx_ok")
        dve_chain, pool_chain = sems("dve_chain pool_chain")
        fw_hi, fw_lo = sems("fw_hi fw_lo")
        var_s_ok, sd_s_ok, hs_ok, ht_ps, tab_ps = sems("var_s_ok sd_s_ok hs_ok ht_ps tab_ps")
        cs_ok, ht_ok, ht_hi, ht_lo = sems("cs_ok ht_ok ht_hi ht_lo")
        unit_ps, unit_b, staged_ok, unit_hi, unit_lo = sems("unit_ps unit_b staged_ok unit_hi unit_lo")
        sc_ps, sm_ok, exp_ok, pn_ok, pt_ps, pt_hi, pt_lo = sems("sc_ps sm_ok exp_ok pn_ok pt_ps pt_hi pt_lo")
        ot_ps, ot_hi, ot_lo, wo_ps, gate_ok = sems("ot_ps ot_hi ot_lo wo_ps gate_ok")
        g_ps, u_ps, sg_ok, mt_ok, mt_hi, mt_lo = sems("g_ps u_ps sg_ok mt_ok mt_hi mt_lo")
        down_ps, delta_ok = sems("down_ps delta_ok")

        def last_use(b):
            if b < 0:
                return unit_ps, 0
            k, i = order[b][0], int(order[b][1])
            if k in "KVQ":
                return unit_ps, [u for u, (name, _) in enumerate(units) if name == order[b]][-1] + 1
            return {"O": (wo_ps, 4 * i + 4), "G": (g_ps, 2 * i + 2), "U": (u_ps, 2 * i + 2),
                    "D": (down_ps, i + 1)}[k]

        def groups(body):
            for g in range(G):
                body(g, g < G - 1)

        block = ctx.enter_context(nc.Block())

        @block.sync
        def _(sp):
            sp.dma_start(X[:], x_g[0]).then_inc(x_in, 16)
            for n, q in enumerate((1, 0, 2, 3)):
                sp.dma_start(raw_qkvu[n][:], WT_v[:, :, q * DM:(q + 1) * DM]).then_inc(w_raw[n], 16)
            sp.dma_start(raw_wo, WoT_v).then_inc(w_raw[4], 16)

            def body(g, more):
                sp.wait_ge(score_ok, g + 1)
                sp.dma_start(scores_g[g], score4[:, g % 2, :], allow_slow_non_contiguous=True).then_inc(score_out, 16)
                sp.wait_ge(base_ok, CH * (g + 1))
                if more:
                    sp.dma_start(X[:], x_g[g + 1]).then_inc(x_in, 16)
                else:
                    sp.wait_ge(score_out, 16 * G)
                    sp.wait_ge(xt_ps, CH * G)
                    sp.dma_start(s_col, scores_t, allow_slow_non_contiguous=True).then_inc(scol_in, 16)
                    sp.dma_start(s_bc, scores.partition_broadcast(P)).then_inc(sbc_in, 16)
                    sp.wait_ge(proj_ps, NPROJ * G)
                    load_block(0)
                    load_block(1)
                for c in range(CH):
                    N = CH * g + c
                    sp.wait_ge(final_ok, N + 1)
                    sp.dma_start(out_t[N], R[:, c % 2, :]).then_inc(stored[c % 2], 16)

            def load_block(b):
                k = order[b]
                if b >= 2:
                    sp.wait_ge(fw_hi, b - 1), sp.wait_ge(fw_lo, b - 1)
                sp.dma_start(raw[b % 2][:], source[k[0]](int(k[1]))).then_inc(raw_in[b % 2], 16)

            groups(body)
            sp.dma_start(bqk[:, 0:FKV], bk).then_inc(part_in, 16)
            sp.dma_start(bqk[:, FKV:], bq).then_inc(part_in, 16)
            sp.dma_start(ln12[:, 0, :], ln1).then_inc(part_in, 16)
            sp.dma_start(ln12[:, 1, :], ln2).then_inc(part_in, 16)
            sp.dma_start(bvb[:], bv.partition_broadcast(P)).then_inc(part_in, 16)
            for b in range(2, len(order)):
                load_block(b)
            for c in range(2):
                sp.wait_ge(stored[c], 16 * N_TILES // 2)

        @block.scalar
        def _(act):
            for dst, src in ((wr_b[:], w_router.partition_broadcast(P)), (shid, s_hid),
                             (KD[:], s_row.partition_broadcast(P)), (shead, s_head.partition_broadcast(P))):
                act.dma_start(dst, src).then_inc(const_in, 16)

            def weights_hi(n):
                act.wait_ge(w_raw[n], 16)
                q = (1, 0, 2, 3, 0)[n]
                dst, src = (Wh[:, :, q * DM:(q + 1) * DM], raw_qkvu[n][:]) if n < 4 else (Woh[:], raw_wo)
                S.activation(dst, src, ACT.Copy).then_inc(w_hi, 1)

            def ln_sd(g):
                act.wait_ge(var_ok, g + 1)
                act.wait_ge(consts, 1)
                S.activation(sd_ln, mv[:, :, 1], ACT.Sqrt, bias=eps_ln).then_inc(sd_ln_ok, 1)

            def xt_high(g, c):
                act.wait_ge(xt_ps, CH * g + c + 1)
                S.activation(xTh[:, :, c * P:(c + 1) * P], tiles4(B[5][:]), ACT.Copy).then_inc(xt_hi, 1)

            ln_sd(0)
            weights_hi(0)
            for c in range(CH):
                xt_high(0, c)
            weights_hi(1)
            weights_hi(2)
            weights_hi(3)
            weights_hi(4)
            act.wait_ge(iota_ok, 3), act.wait_ge(lag_ok, 1), act.wait_ge(slopes_ok, 1)
            for h in range(NH):
                S.activation(DEC[:, h, :], lag, ACT.Exp, scale=nshead[:, h:h + 1])
            for k in range(NK):
                S.activation(QD[:, k, :], ahead, ACT.Exp, scale=nshid[:, k:k + 1])
            S.activation(bdec, shid, ACT.Exp, scale=-float(P))
            S.activation(KD[:], KD[:], ACT.Exp, scale=age).then_inc(decays_ok, 1)

            def body(g, more):
                for i in range(NPROJ):
                    name, j = "KQVU"[i // 4], i % 4
                    dst = {"K": KT, "Q": QT, "V": VT, "U": UT}[name]
                    act.wait_ge(proj_ps, NPROJ * g + i + 1)
                    if i == 8 and more:
                        ln_sd(g + 1)
                    if j == 0:
                        if name == "K":
                            act.wait_ge(w_lo, 1), act.wait_ge(k_lo, CH * g), act.wait_ge(kt_ps, CH * g)
                            act.wait_ge(k_hi, CH * g)
                        if name == "Q":
                            act.wait_ge(w_lo, 2), act.wait_ge(q_lo, CH * g), act.wait_ge(q_dec, CH * g)
                            act.wait_ge(q_hi, CH * g)
                        if name == "V":
                            act.wait_ge(w_lo_pool, 1), act.wait_ge(pv_ps, CH * g), act.wait_ge(kv_ps, CH * g)
                        if name == "U":
                            act.wait_ge(w_lo_pool, 2), act.wait_ge(uo_ok, CH * g)
                        act.wait_ge(w_hi, 5)
                    S.activation(dst[:, j, :], B[i % 4][:], ACT.Silu if name in "KQ" else ACT.Copy)\
                        .then_inc(proj_sb, 1)

                def split_high(c):
                    N = CH * g + c
                    act.wait_ge(proj_sb, NPROJ * g + 8)
                    act.wait_ge(s_ps, N), act.wait_ge(k_lo, N), act.wait_ge(q_lo, N)
                    S.activation(kh[:], KT[:, :, c * P:(c + 1) * P], ACT.Copy).then_inc(k_hi, 1)
                    S.activation(qh[:], QT[:, :, c * P:(c + 1) * P], ACT.Copy).then_inc(q_hi, 1)

                def rms_sd(c):
                    N = CH * g + c
                    act.wait_ge(rms_ps, N + 1)
                    act.wait_ge(final_ok, N)
                    S.activation(sd_o, B[7][:, 0:1], ACT.Sqrt, scale=1.0 / DM, bias=eps_rms)\
                        .then_inc(sd_o_ok, 1)

                split_high(0)
                for c in range(CH):
                    N = CH * g + c
                    if c + 1 < CH:
                        split_high(c + 1)
                    if c:
                        rms_sd(c - 1)
                    if more:
                        act.wait_ge(proj_ps, NPROJ * (g + 1))
                        xt_high(g + 1, c)
                    act.wait_ge(uo_ok, N + 1)
                    act.wait_ge(rms_ps, N)
                    S.activation(sq[:], tiles4(B[4][:]), ACT.Square).then_inc(sq_ok, 1)
                    act.wait_ge(out_ps, N), act.wait_ge(uo_lo, N)
                    S.activation(uoh[:], uo[:], ACT.Copy).then_inc(uo_hi, 1)
                rms_sd(CH - 1)

            groups(body)

            def block_hi(b):
                act.wait_ge(raw_in[b % 2], 16 * (b // 2 + 1))
                act.wait_ge(*last_use(b - 3))
                S.activation(whi[b % 3][:], raw[b % 2][:], ACT.Copy).then_inc(fw_hi, 1)

            def norm_sd(n, func_input, scale, bias):
                S.activation(sd_s, func_input, ACT.Sqrt, scale=scale, bias=bias).then_inc(sd_s_ok, 1)

            def scaled_transpose(n):
                act.wait_ge(ht_ps, n + 1), act.wait_ge(part_in, 16 * 5)
                for k in range(NK):
                    ins = S.activation(HT[:, k, :], B[k // 2][:, (k % 2) * SEL:(k % 2 + 1) * SEL], ACT.Copy,
                                       scale=ln12[:, n, k:k + 1])
                ins.then_inc(ht_ok, 1)
                act.wait_ge(ht_ok, n + 1)
                if n:
                    act.wait_ge(unit_ps, len(units))
                S.activation(HTh[:], HT[:], ACT.Copy).then_inc(ht_hi, 1)

            def unit_bias(u):
                k, p = units[u]
                if k[0] == "V":
                    return
                act.wait_ge(unit_ps, u + 1)
                if u >= 2:
                    act.wait_ge(staged_ok, u - 1)
                for i in range(2):
                    head = 4 * int(k[1]) + 2 * p + i + (FKV if k[0] == "Q" else 0)
                    ins = S.activation(qb[:, u % 2, i, :], B[u % 2][:, i * SEL:(i + 1) * SEL], ACT.Identity,
                                       bias=bqk[:, head:head + 1])
                ins.then_inc(unit_b, 1)

            def unit_dst(u, part):
                k, p = units[u]
                i = int(k[1])
                if k[0] == "V":
                    return (Vh, Vl)[part][:, p, i * DM:(i + 1) * DM]
                dst = ((KRh, KRl) if k[0] == "K" else (QRh, QRl))[part]
                return dst[:, 4 * i + 2 * p:4 * i + 2 * p + 2, :].rearrange("p h m -> p (h m)")

            def unit_high(u):
                act.wait_ge(staged_ok, u + 1)
                S.activation(unit_dst(u, 0), staged[:, u % 2, :], ACT.Copy).then_inc(unit_hi, 1)

            block_hi(0)
            block_hi(1)
            act.wait_ge(var_s_ok, 1)
            norm_sd(0, mv[:, 0:NS, 1], 1.0, eps_ln)
            act.wait_ge(var_s_ok, 2)
            norm_sd(1, sumsq, 1.0 / DM, eps_rms)
            block_hi(2)
            scaled_transpose(0)
            for u in range(before_heads):
                unit_bias(u)
                if u:
                    unit_high(u - 1)
                if u % 2:
                    block_hi(u // 2 + 3)
            unit_high(before_heads - 1)
            S.activation(gate, sel_score, ACT.Exp, scale=-1.0).then_inc(gate_ok, 1)
            for h in range(STEPS):
                if h < FH:
                    act.wait_ge(sm_ok, h + 1), act.wait_ge(pn_ok, h)
                    for t, cols in ((0, slice(0, P)), (1, slice(P, 3 * P))):
                        ins = S.activation(PR[:, cols], SM[:, cols], ACT.Exp, scale=float(FD) ** -0.5,
                                           bias=ntop[:, h % 2, t:t + 1], accum_out=psum_[:, h % 2, t:t + 1])
                    ins.then_inc(exp_ok, 1)
                if 1 <= h <= FH:
                    act.wait_ge(pt_ps, h)
                    if h >= 3:
                        act.wait_ge(ot_ps, h - 2)
                    S.activation(PTh[:, (h - 1) % 2, :], B[4][:, 0:3 * P], ACT.Copy).then_inc(pt_hi, 1)
                if 2 <= h <= FH + 1:
                    act.wait_ge(ot_ps, h - 1)
                    if h >= 4:
                        act.wait_ge(wo_ps, h - 3)
                    S.activation(OTh[:, (h - 2) % 2, :], B[5][:, 0:SEL], ACT.Copy).then_inc(ot_hi, 1)
                u = unit_of_step(h)
                if u is not None:
                    unit_bias(u)
                    unit_high(u)
                if h in split_after:
                    block_hi(block_of[split_after[h]])
            block_hi(14)
            act.wait_ge(var_s_ok, 3)
            norm_sd(2, sumsq, 1.0 / DM, eps_rms)
            scaled_transpose(1)
            for j in range(4):
                for p in range(2):
                    m = 2 * j + p
                    act.wait_ge(g_ps, m + 1)
                    if m >= 2:
                        act.wait_ge(mt_ok, m - 1)
                    S.activation(sg[:, m % 2, :], B[m % 2][:], ACT.Silu).then_inc(sg_ok, 1)
                block_hi(block_of[f"G{j}"] + 3) if block_of[f"G{j}"] + 3 < len(order) else None
                for p in range(2):
                    m = 2 * j + p
                    act.wait_ge(mt_ok, m + 1)
                    S.activation(QRh[:, 2 * m:2 * m + 2, :].rearrange("p h m -> p (h m)"), staged[:, m % 2, :],
                                 ACT.Copy).then_inc(mt_hi, 1)
                for b in range(block_of[f"G{j}"] + 4, (block_of[f"G{j + 1}"] if j < 3 else len(order)) + 3):
                    if b < len(order):
                        block_hi(b)

        @block.vector
        def _(dve):
            ch = Chain(dve, dve_chain)
            V.memset(eps_ln, 1e-5)
            V.memset(ones1, 1.0)
            V.memset(eps_rms, 1e-6).then_inc(consts, 1)

            def ln_stats(g):
                dve.wait_ge(x_in, 16 * (g + 1))
                dve.wait_ge(xn_ok, CH * g)
                for c in range(CH):
                    ch.link(V.bn_stats(stats[:, c, :], X[:, c, :]))
                for c in range(CH):
                    ins = V.bn_aggr(mv[:, c, :], stats[:, c, :])
                ins.then_inc(var_ok, 1)

            def ln_norm(g):
                dve.wait_ge(sd_ln_ok, g + 1)
                ch.link(V.reciprocal(rstd, sd_ln))
                dve.wait_ge(xt_ps, CH * g), dve.wait_ge(base_ok, CH * g)
                dve.wait_ge(const_in, 64)
                for c in range(CH):
                    V.tensor_scalar(XN[:, c, :], X[:, c, :], mv[:, c, 0:1], rstd[:, c:c + 1], ALU.subtract,
                                    ALU.mult).then_inc(xn_ok, 1)
                if g >= 1:
                    dve.wait_ge(uo_hi, CH * (g - 1)), dve.wait_ge(uo_lo, CH * (g - 1))
                    dve.wait_ge(score_out, 16 * (g - 1))
                for c in range(CH):
                    dve.wait_ge(xn_ok, CH * g + c + 1)
                    ins = V.tensor_tensor_reduce(out=uo[:].rearrange("p k m -> p (k m)"), in0=XN[:, c, :], in1=wr_b[:], scale=1.0, scalar=0.0,
                                                 op0=ALU.mult, op1=ALU.add, accum_out=score4[:, g % 2, c:c + 1])
                    if c < CH - 1:
                        ch.link(ins)
                ins.then_inc(score_ok, 1)
                dve.wait_ge(score_ok, g + 1)

            def xt_low(g, c):
                dve.wait_ge(xt_hi, CH * g + c + 1)
                V.tensor_tensor(xTl[:, :, c * P:(c + 1) * P], tiles4(B[5][:]),
                                xTh[:, :, c * P:(c + 1) * P].bitcast(f32), ALU.subtract).then_inc(xt_lo, 1)

            def weights_lo(n):
                dve.wait_ge(w_hi, n + 1)
                q = (1, 0, 2, 3, 0)[n]
                dst, hi, src = (Wl[:, :, q * DM:(q + 1) * DM], Wh[:, :, q * DM:(q + 1) * DM], raw_qkvu[n][:]) \
                    if n < 4 else (Wol[:], Woh[:], raw_wo)
                V.tensor_tensor(dst, src, hi.bitcast(f32), ALU.subtract).then_inc(w_lo, 1)

            ln_stats(0)
            ln_norm(0)
            weights_lo(0)
            for c in range(CH):
                xt_low(0, c)
            weights_lo(1)
            dve.wait_ge(const_in, 64)
            V.tensor_scalar(nshead, shead, -1.0, None, ALU.mult)
            V.tensor_scalar(nshid, shid, -1.0, None, ALU.mult).then_inc(slopes_ok, 1)
            dve.wait_ge(iota_ok, 3)
            V.tensor_scalar(lag, lag, 0.0, None, ALU.max).then_inc(lag_ok, 1)
            ch.link(V.memset(BM[:], 0.0))
            for r in range(4):
                V.memset(BM[DH * r:DH * r + DH, DH * r:DH * r + DH], 1.0)
            V.memset(state[:], 0.0).then_inc(bm_ok, 1)
            dve.wait_ge(bm_ok, 1)
            weights_lo(4)
            dve.wait_ge(decays_ok, 1), dve.wait_ge(masks_ok, 3)
            V.tensor_tensor(DEC[:], DEC[:], tri[:].unsqueeze(1).to_broadcast([P, NH, P]), ALU.mult)\
                .then_inc(dec_ok, 1)

            def rank_tokens():
                seen = flat_x.bitcast(bf16)[:, 0:N_TOK]
                dve.wait_ge(sbc_in, 16), dve.wait_ge(scol_in, 16)
                ch.link(V.memset(n_ge, 0.0))
                for n in range(N_TILES):
                    me = s_col[:, n:n + 1]
                    if n:
                        ch.link(V.tensor_scalar(seen[:, 0:n * P], s_bc[:, 0:n * P], me, None, ALU.is_ge, ALU.add,
                                                accum_out=n_ge[:, n:n + 1]))
                    ch.link(V.tensor_scalar(seen[:, n * P:], s_bc[:, n * P:], me, None, ALU.is_gt, ALU.add,
                                            accum_out=n_gt[:, n:n + 1]))
                    ch.link(V.scalar_tensor_tensor(out=seen[:, 0:P], in0=s_bc[:, n * P:(n + 1) * P], scalar=me,
                                                   in1=below[:], op0=ALU.is_equal, op1=ALU.mult,
                                                   accum_out=n_eq[:, n:n + 1]))
                ch.link(V.tensor_tensor(rank, n_ge, n_gt, ALU.add))
                ch.link(V.tensor_tensor(rank, rank, n_eq, ALU.add))
                V.tensor_scalar(chosen, rank, float(SEL), None, ALU.is_lt)
                V.tensor_scalar(chosen_b[:], rank, float(SEL), None, ALU.is_lt).then_inc(rank_ok, 1)

            def place_tokens():
                dve.wait_ge(cnt_ps, 1), dve.wait_ge(rank_ok, 1)
                ch.link(V.tensor_copy(n_gt, B[5][:, N_TILES:2 * N_TILES]))
                ch.link(V.tensor_tensor_scan(before, n_gt, n_ge, 0.0, ALU.add, ALU.bypass))
                ch.link(V.tensor_tensor(before, before, n_gt, ALU.subtract))
                ch.link(V.tensor_tensor(place, B[5][:, 0:N_TILES], before, ALU.add))
                ch.link(V.tensor_scalar(n_eq, chosen, -float(N_TOK), float(N_TOK), ALU.mult, ALU.add))
                ch.link(V.tensor_tensor(place, place, n_eq, ALU.add))
                for n in range(N_TILES):
                    ins = V.tensor_scalar(one_hot[:, n, :], slots[:], place[:, n:n + 1], None, ALU.is_equal)
                ins.then_inc(oh_ok, 1)

            def token_indices():
                dve.wait_ge(idx_ps, 1)
                ch.link(V.tensor_copy(idx_f[:], B[5][:, 0:2 * NS]))
                for t in range(NS):
                    ins = V.scalar_tensor_tensor(out=idx[:, t:t + 1], in0=idx_f[:, 2 * t + 1:2 * t + 2],
                                                 scalar=float(P), in1=idx_f[:, 2 * t:2 * t + 1], op0=ALU.mult,
                                                 op1=ALU.add)
                ins.then_inc(idx_ok, 1)

            def body(g, more):
                if more:
                    ln_stats(g + 1)
                    ln_norm(g + 1)
                else:
                    rank_tokens()

                def k_low(c):
                    N = CH * g + c
                    dve.wait_ge(k_hi, N + 1)
                    V.tensor_tensor(kl[:], KT[:, :, c * P:(c + 1) * P], kh[:].bitcast(f32), ALU.subtract)\
                        .then_inc(k_lo, 1)

                def final(c):
                    N = CH * g + c
                    dve.wait_ge(out_ps, N + 1), dve.wait_ge(sd_o_ok, N + 1)
                    ch.link(V.reciprocal(r_o, sd_o))
                    dve.wait_ge(stored[c % 2], 16 * (2 * g + c // 2))
                    dve.wait_ge(base_ok, N + 1)
                    V.scalar_tensor_tensor(out=R[:, c % 2, :], in0=B[7][:], scalar=r_o, in1=BASE[:, c, :],
                                           op0=ALU.mult, op1=ALU.add).then_inc(final_ok, 1)

                k_low(0)
                for c in range(CH):
                    N = CH * g + c
                    dve.wait_ge(kt_ps, N + 1), dve.wait_ge(kv_ps, N)
                    V.tensor_tensor(kdec[:], B[5][:], KD[:], ALU.mult).then_inc(k_dec, 1)
                    dve.wait_ge(s_ps, N + 1), dve.wait_ge(pv_ps, N), dve.wait_ge(dec_ok, 1), dve.wait_ge(w_lo, 3)
                    for r in range(4):
                        V.tensor_tensor(A[:].rearrange("p (j r) m -> p r j m", r=4)[:, r], tiles4(B[r][:]),
                                        DEC[:].rearrange("p (j r) m -> p r j m", r=4)[:, r], ALU.mult)\
                            .then_inc(masked, 1)
                    if c + 1 < CH:
                        k_low(c + 1)
                    dve.wait_ge(kv_ps, N + 1), dve.wait_ge(state_dk, N + 1), dve.wait_ge(bm_ok, 1)
                    ch.link(V.tensor_tensor(kv_new[:], tiles4(B[6][:]),
                                            BM[:].unsqueeze(1).to_broadcast([P, NK, P]), ALU.mult))
                    V.tensor_tensor(state[:], kv_new[:], state_dec[:], ALU.add).then_inc(state_ok, 1)
                    if c:
                        final(c - 1)
                    if more:
                        xt_low(g + 1, c)
                    elif c == 0:
                        place_tokens()
                    elif c == 1:
                        token_indices()
                    dve.wait_ge(pv_ps, N + 1), dve.wait_ge(uo_hi, N), dve.wait_ge(uo_lo, N)
                    V.tensor_tensor(uo[:], tiles4(B[4][:]), UT[:, :, c * P:(c + 1) * P], ALU.mult)\
                        .then_inc(uo_ok, 1)
                final(CH - 1)

            groups(body)

            dve.wait_ge(final_ok, N_TILES), dve.wait_ge(stored[0], 8 * N_TILES), dve.wait_ge(stored[1], 8 * N_TILES)
            dve.wait_ge(picked, 16 * 2 * NS)

            def normed(n, src):
                for t in range(NS):
                    ins = V.tensor_tensor_reduce(out=hs[:, t, :], in0=src[:, t, :], in1=src[:, t, :], scale=1.0,
                                                 scalar=0.0, op0=ALU.mult, op1=ALU.add, accum_out=sumsq[:, t:t + 1])
                ins.then_inc(var_s_ok, 1)
                dve.wait_ge(sd_s_ok, n + 2)
                ch.link(V.reciprocal(r_s, sd_s))
                for t in range(NS):
                    ins = V.tensor_scalar(hs[:, t, :], src[:, t, :], r_s[:, t:t + 1], None, ALU.mult)
                ins.then_inc(hs_ok, 1)

            def low_of(dst, src, high, done):
                V.tensor_tensor(dst, src, high.bitcast(f32), ALU.subtract).then_inc(done, 1)

            for t in range(NS):
                ch.link(V.bn_stats(stats[:, t, :], xs[:, t, :]))
            for t in range(NS):
                ins = V.bn_aggr(mv[:, t, :], stats[:, t, :])
            ins.then_inc(var_s_ok, 1)
            dve.wait_ge(sd_s_ok, 1)
            ch.link(V.reciprocal(r_s, sd_s))
            for t in range(NS):
                ch.link(V.tensor_scalar(xsn[:, t, :], xs[:, t, :], mv[:, t, 0:1], r_s[:, t:t + 1], ALU.subtract,
                                        ALU.mult))
            for t in range(NS):
                ch.link(V.tensor_tensor_reduce(out=hs[:, t, :], in0=xsn[:, t, :], in1=wr_b[:], scale=1.0, scalar=0.0,
                                               op0=ALU.mult, op1=ALU.add, accum_out=sel_score[:, t:t + 1]))
            normed(0, xsn)
            dve.wait_ge(tab_ps, 1)
            V.tensor_copy(CS[:].rearrange("p a m -> p (a m)"), B[2][:]).then_inc(cs_ok, 1)
            dve.wait_ge(ht_hi, 1)
            low_of(HTl[:], HT[:], HTh[:], ht_lo)

            def stage(u):
                k, p = units[u]
                if u >= 2:
                    dve.wait_ge(unit_hi, u - 1), dve.wait_ge(unit_lo, u - 1)
                if k[0] == "V":
                    dve.wait_ge(unit_ps, u + 1), dve.wait_ge(part_in, 16 * 5)
                    i = int(k[1])
                    V.tensor_tensor(staged[:, u % 2, :], B[u % 2][:], bvb[:, i * DM:(i + 1) * DM], ALU.add)\
                        .then_inc(staged_ok, 1)
                    return
                dve.wait_ge(unit_b, kq_count(u)), dve.wait_ge(cs_ok, 1)
                dve.wait_ge(staged_ok, u)
                both = qb[:, u % 2]
                half = P // 2
                V.tensor_tensor(rope1[:], both, CS[:, 0, :].unsqueeze(1).to_broadcast([P, 2, SEL]), ALU.mult)
                for a, b in ((0, half), (half, 0)):
                    ins = V.tensor_tensor(rope2[a:a + half], both[b:b + half],
                                          CS[b:b + half, 1, :].unsqueeze(1).to_broadcast([half, 2, SEL]), ALU.mult)
                ch.link(ins)
                V.tensor_tensor(staged[:, u % 2, :].rearrange("p (a m) -> p a m", a=2), rope1[:], rope2[:],
                                ALU.add).then_inc(staged_ok, 1)

            def unit_low(u):
                k, p = units[u]
                i = int(k[1])
                dve.wait_ge(unit_hi, u + 1)
                if k[0] == "V":
                    low_of(Vl[:, p, i * DM:(i + 1) * DM], staged[:, u % 2, :], Vh[:, p, i * DM:(i + 1) * DM], unit_lo)
                else:
                    hi, lo = (KRh, KRl) if k[0] == "K" else (QRh, QRl)
                    heads = slice(4 * i + 2 * p, 4 * i + 2 * p + 2)
                    low_of(lo[:, heads, :], staged[:, u % 2, :].rearrange("p (a m) -> p a m", a=2), hi[:, heads, :],
                           unit_lo)

            for u in range(before_heads):
                stage(u)
                if u:
                    unit_low(u - 1)
            unit_low(before_heads - 1)
            dve.wait_ge(causal_ok, 3)
            for h in range(STEPS):
                if h < FH:
                    dve.wait_ge(sc_ps, h + 1), dve.wait_ge(exp_ok, h)
                    for t, cols in ((0, slice(0, P)), (1, slice(P, 3 * P))):
                        ins = V.tensor_tensor_reduce(out=SM[:, cols], in0=B[2 + h % 2][:, cols], in1=causal[:, cols],
                                                     scale=1.0, scalar=-3.0e38, op0=ALU.add, op1=ALU.max,
                                                     accum_out=top[:, h % 2, t:t + 1])
                    ch.link(ins)
                    V.tensor_scalar(ntop[:, h % 2, :], top[:, h % 2, :], -(float(FD) ** -0.5), None, ALU.mult)\
                        .then_inc(sm_ok, 1)
                if 1 <= h <= FH:
                    dve.wait_ge(pt_hi, h)
                    if h >= 3:
                        dve.wait_ge(ot_ps, h - 2)
                    low_of(PTl[:, (h - 1) % 2, :], B[4][:, 0:3 * P], PTh[:, (h - 1) % 2, :], pt_lo)
                if h < FH:
                    dve.wait_ge(exp_ok, h + 1)
                    if h >= 2:
                        dve.wait_ge(pt_ps, h - 1)
                    ch.link(V.reciprocal(pinv[:, h % 2, :], psum_[:, h % 2, :]))
                    for t, cols in ((0, slice(0, P)), (1, slice(P, 3 * P))):
                        ins = V.tensor_scalar(PN[:, h % 2, cols], PR[:, cols], pinv[:, h % 2, t:t + 1], None, ALU.mult)
                    ins.then_inc(pn_ok, 1)
                if 2 <= h <= FH + 1:
                    dve.wait_ge(ot_hi, h - 1)
                    if h >= 4:
                        dve.wait_ge(wo_ps, h - 3)
                    low_of(OTl[:, (h - 2) % 2, :], B[5][:, 0:SEL], OTh[:, (h - 2) % 2, :], ot_lo)
                u = unit_of_step(h)
                if u is not None:
                    stage(u)
                    unit_low(u)
            dve.wait_ge(gate_ok, 1)
            ch.link(V.tensor_scalar(gate, gate, 1.0, None, ALU.add))
            ch.link(V.reciprocal(gate, gate))
            dve.wait_ge(wo_ps, FH)
            for t in range(NS):
                ins = V.tensor_copy(ao[:, t, :], B[6 + t][:])
            ch.link(ins)
            for t in range(NS):
                ins = V.tensor_tensor(xs[:, t, :], xsn[:, t, :], ao[:, t, :], ALU.add)
            ch.link(ins)
            normed(1, xs)
            dve.wait_ge(ht_hi, 2)
            low_of(HTl[:], HT[:], HTh[:], ht_lo)
            for j in range(4):
                for p in range(2):
                    m = 2 * j + p
                    dve.wait_ge(sg_ok, m + 1), dve.wait_ge(u_ps, m + 1)
                    if m >= 2:
                        dve.wait_ge(mt_hi, m - 1), dve.wait_ge(mt_lo, m - 1)
                    V.tensor_tensor(staged[:, m % 2, :], sg[:, m % 2, :], B[2 + m % 2][:], ALU.mult)\
                        .then_inc(mt_ok, 1)
                for p in range(2):
                    m = 2 * j + p
                    dve.wait_ge(mt_hi, m + 1)
                    low_of(QRl[:, 2 * m:2 * m + 2, :], staged[:, m % 2, :].rearrange("p (a m) -> p a m", a=2),
                           QRh[:, 2 * m:2 * m + 2, :], mt_lo)
            dve.wait_ge(down_ps, 4)
            for t in range(NS):
                ins = V.tensor_tensor(ao[:, t, :], B[6 + t][:], ao[:, t, :], ALU.add)
            ch.link(ins)
            for t in range(NS):
                V.tensor_scalar(hs[:, t, :], ao[:, t, :], gate[:, t:t + 1], None, ALU.mult).then_inc(delta_ok, 1)

        @block.gpsimd
        def _(pool):
            Q.iota(lag, pattern=[[1, P]], base=0, channel_multiplier=-1, allow_small_or_imprecise_dtypes=True)\
                .then_inc(iota_ok, 1)
            Q.iota(ahead, pattern=[[1, P]], base=1, channel_multiplier=0, allow_small_or_imprecise_dtypes=True)\
                .then_inc(iota_ok, 1)
            Q.iota(age, pattern=[[0, 1]], base=1 - P, channel_multiplier=1, allow_small_or_imprecise_dtypes=True)\
                .then_inc(iota_ok, 1)
            Q.memset(ident[:], 0.0).then_inc(pool_chain, 1)
            Q.memset(tri[:], 1.0).then_inc(pool_chain, 1)
            Q.memset(below[:], 1.0).then_inc(pool_chain, 1)
            Q.memset(above[:], 1.0).then_inc(pool_chain, 1)
            Q.memset(ones_sq[:], 1.0)
            pool.wait_ge(pool_chain, 4)
            Q.affine_select(out=ident[:], in_=ident[:], compare_op=ALU.not_equal, fill=1.0, base=0,
                            pattern=[[-1, P]], channel_multiplier=1).then_inc(masks_ok, 1)
            Q.affine_select(out=tri[:], in_=tri[:], compare_op=ALU.is_ge, fill=0.0, base=0,
                            pattern=[[1, P]], channel_multiplier=-1).then_inc(masks_ok, 1)
            Q.affine_select(out=below[:], in_=below[:], compare_op=ALU.is_gt, fill=0.0, base=0,
                            pattern=[[-1, P]], channel_multiplier=1).then_inc(masks_ok, 1)
            Q.affine_select(out=above[:], in_=above[:], compare_op=ALU.is_gt, fill=0.0, base=0,
                            pattern=[[1, P]], channel_multiplier=-1)
            Q.iota(slots[:], pattern=[[1, SEL]], base=0, channel_multiplier=0, allow_small_or_imprecise_dtypes=True)
            Q.iota(tok2[:, :, 0], pattern=[[0, N_TILES]], base=0, channel_multiplier=1,
                   allow_small_or_imprecise_dtypes=True)
            Q.iota(tok2[:, :, 1], pattern=[[1, N_TILES]], base=0, channel_multiplier=0,
                   allow_small_or_imprecise_dtypes=True).then_inc(tok_ok, 1)

            def base(g, c):
                pool.wait_ge(xn_ok, CH * g + c + 1)
                if g:
                    pool.wait_ge(final_ok, CH * (g - 1) + c + 1)
                Q.tensor_tensor(BASE[:, c, :], X[:, c, :], XN[:, c, :], ALU.add).then_inc(base_ok, 1)

            for n in (2, 3):
                pool.wait_ge(w_hi, n + 1)
                Q.tensor_tensor(Wl[:, :, n * DM:(n + 1) * DM], raw_qkvu[n][:],
                                Wh[:, :, n * DM:(n + 1) * DM].bitcast(f32), ALU.subtract)\
                    .then_inc(w_lo_pool, 1)
            for c in range(CH):
                base(0, c)

            def body(g, more):
                def q_low(c):
                    N = CH * g + c
                    pool.wait_ge(q_hi, N + 1)
                    Q.tensor_tensor(ql[:], QT[:, :, c * P:(c + 1) * P], qh[:].bitcast(f32), ALU.subtract)\
                        .then_inc(q_lo, 1)

                def decayed(c):
                    N = CH * g + c
                    pool.wait_ge(inter_ps, N), pool.wait_ge(decays_ok, 1), pool.wait_ge(proj_sb, NPROJ * g + 8)
                    Q.tensor_tensor(qdec[:], QT[:, :, c * P:(c + 1) * P], QD[:], ALU.mult).then_inc(q_dec, 1)
                    pool.wait_ge(state_ok, N), pool.wait_ge(bm_ok, 1)
                    Q.tensor_tensor(state_dec[:], state[:], bdec.unsqueeze(2).to_broadcast([P, NK, P]), ALU.mult)\
                        .then_inc(state_dk, 1)

                q_low(0)
                decayed(0)
                for c in range(CH):
                    N = CH * g + c
                    if c + 1 < CH:
                        q_low(c + 1)
                        decayed(c + 1)
                    if more and c:
                        base(g + 1, c - 1)
                    pool.wait_ge(uo_hi, N + 1), pool.wait_ge(out_ps, N)
                    Q.tensor_tensor(uol[:], uo[:], uoh[:].bitcast(f32), ALU.subtract).then_inc(uo_lo, 1)
                    if not more and c == CH - 2:
                        gather()
                if more:
                    base(g + 1, CH - 1)

            def gather():
                pool.wait_ge(idx_ok, 1)
                for t in range(NS):
                    for dst, src in ((xs[:, t, :], x), (tab[:, t * 2 * FD:(t + 1) * 2 * FD], rope)):
                        Q.indirect_dma_start(out=dst, out_offset=None, in_=src,
                                             in_offset=bass.IndirectOffsetOnAxis(ap=idx[:, t:t + 1], axis=0))\
                            .then_inc(picked, 16)

            groups(body)

            def block_lo(b):
                pool.wait_ge(fw_hi, b + 1)
                pool.wait_ge(*last_use(b - 3))
                Q.tensor_tensor(wlo[b % 3][:], raw[b % 2][:], whi[b % 3][:].bitcast(f32), ALU.subtract)\
                    .then_inc(fw_lo, 1)

            pool.wait_ge(proj_ps, NPROJ * G)
            block_lo(0)
            block_lo(1)
            pool.wait_ge(final_ok, N_TILES)
            pool.wait_ge(stored[0], 8 * N_TILES), pool.wait_ge(stored[1], 8 * N_TILES)
            Q.memset(causal[:], 0.0).then_inc(causal_ok, 1)
            pool.wait_ge(causal_ok, 1)
            for blk in (0, 2):
                Q.affine_select(out=causal[:, blk * P:(blk + 1) * P], in_=causal[:, blk * P:(blk + 1) * P],
                                compare_op=ALU.is_ge, fill=-1.0e38, base=0, pattern=[[-1, P]], channel_multiplier=1)\
                    .then_inc(causal_ok, 1)
            for b in range(2, len(order)):
                block_lo(b)
            for t in range(NS):
                pool.wait_ge(delta_ok, t + 1)
                Q.indirect_dma_start(out=out, out_offset=bass.IndirectOffsetOnAxis(ap=idx[:, t:t + 1], axis=0),
                                     in_=hs[:, t, :], in_offset=None, compute_op=ALU.add).then_inc(scattered, 16)
            pool.wait_ge(scattered, 16 * NS)

        @block.tensor
        def _(pe):
            def split_matmuls(dst, lhs, rhs, first, last):
                (lh, ll), (rh, rl) = lhs, rhs
                T.matmul(dst, lh, rh, start=first, stop=False)
                T.matmul(dst, lh, rl, start=False, stop=False)
                return T.matmul(dst, ll, rh, start=False, stop=last)

            def transposed(g, c):
                pe.wait_ge(xn_ok, CH * g + c + 1)
                pe.wait_ge(masks_ok, 1)
                for k in range(NK):
                    ins = T.transpose(B[5][:, k * P:(k + 1) * P], XN[:, c, k * P:(k + 1) * P], ident[:])
                ins.then_inc(xt_ps, 1)

            for c in range(CH):
                pe.wait_ge(xt_lo, c)
                transposed(0, c)

            def project(g):
                for i in range(NPROJ):
                    name, j = "KQVU"[i // 4], i % 4
                    lo = {"Q": 0, "K": DM, "V": 2 * DM, "U": 3 * DM}[name]
                    if i == 0:
                        pe.wait_ge(xt_lo, CH * (g + 1))
                    if j == 0 and g == 0:
                        if name in "KQ":
                            pe.wait_ge(w_lo, 1 + i // 4)
                        else:
                            pe.wait_ge(w_lo_pool, i // 4 - 1)
                    if i < 4:
                        pe.wait_ge(masked, 4 * CH * g)
                    else:
                        pe.wait_ge(proj_sb, NPROJ * g + i - 3)
                    for k in range(NK):
                        xt = (xTh[:, k, :], xTl[:, k, :])
                        if name == "V":
                            ins = split_matmuls(B[i % 4][:], [a[:, j * P:(j + 1) * P] for a in xt],
                                                (Wh[:, k, lo:lo + DM], Wl[:, k, lo:lo + DM]), k == 0, k == NK - 1)
                        else:
                            cols = slice(lo + j * P, lo + (j + 1) * P)
                            ins = split_matmuls(B[i % 4][:], (Wh[:, k, cols], Wl[:, k, cols]), xt, k == 0, k == NK - 1)
                    ins.then_inc(proj_ps, 1)

            def body(g, more):
                project(g)

                def rms(c):
                    N = CH * g + c
                    pe.wait_ge(sq_ok, N + 1), pe.wait_ge(final_ok, N), pe.wait_ge(consts, 1)
                    for k in range(NK):
                        ins = T.matmul(B[7][:, 0:1], sq[:, k, :], ones1, start=k == 0, stop=k == NK - 1)
                    ins.then_inc(rms_ps, 1)

                def project_out(c):
                    N = CH * g + c
                    pe.wait_ge(uo_hi, N + 1), pe.wait_ge(uo_lo, N + 1), pe.wait_ge(sd_o_ok, N + 1), pe.wait_ge(w_lo, 3)
                    for k in range(NK):
                        ins = split_matmuls(B[7][:], (uoh[:, k, :], uol[:, k, :]), (Woh[:, k, :], Wol[:, k, :]),
                                            k == 0, k == NK - 1)
                    ins.then_inc(out_ps, 1)

                for c in range(CH):
                    N = CH * g + c
                    pe.wait_ge(proj_sb, NPROJ * g + 4)
                    if c:
                        if more:
                            pe.wait_ge(xt_lo, CH * (g + 1) + c)
                        elif c == 1:
                            pe.wait_ge(oh_ok, 1)
                        elif c == 2:
                            pe.wait_ge(idx_ok, 1)
                        pe.wait_ge(k_dec, N)
                    for k in range(NK):
                        ins = T.transpose(B[5][:, k * P:(k + 1) * P], KT[:, k, c * P:(c + 1) * P], ident[:])
                    ins.then_inc(kt_ps, 1)
                    pe.wait_ge(k_hi, N + 1), pe.wait_ge(q_hi, N + 1), pe.wait_ge(k_lo, N + 1), pe.wait_ge(q_lo, N + 1)
                    pe.wait_ge(masked, 4 * N)
                    if c == 0:
                        pe.wait_ge(proj_sb, NPROJ * (g + 1))
                    for j in range(NK):
                        for n, (ka, qa) in enumerate(((kh, qh), (kh, ql), (kl, qh))):
                            for r in range(4):
                                rows = slice(DH * r, DH * r + DH)
                                ins = T.matmul(B[r][:, j * P:(j + 1) * P], ka[rows, j, :], qa[rows, j, :],
                                               start=n == 0, stop=n == 2)
                    ins.then_inc(s_ps, 1)
                    if c:
                        rms(c - 1)
                    pe.wait_ge(q_dec, N + 1), pe.wait_ge(state_ok, N), pe.wait_ge(bm_ok, 1)
                    pe.wait_ge(uo_ok, N), pe.wait_ge(sq_ok, N)
                    for j in range(NK):
                        ins = T.matmul(B[4][:, j * P:(j + 1) * P], state[:, j, :], qdec[:, j, :], start=j == 0,
                                       stop=False, skip_group_check=True)
                    ins.then_inc(inter_ps, 1)
                    pe.wait_ge(k_dec, N + 1), pe.wait_ge(proj_sb, NPROJ * g + 12)
                    for j in range(NK):
                        cols = slice(j * P, (j + 1) * P)
                        ins = T.matmul(B[6][:, cols], kdec[:, cols], VT[:, c, cols], start=True, stop=True)
                    ins.then_inc(kv_ps, 1)
                    if c:
                        project_out(c - 1)
                    if more:
                        transposed(g + 1, c)
                    elif c == 0:
                        pe.wait_ge(rank_ok, 1), pe.wait_ge(tok_ok, 1)
                        T.matmul(B[5][:, 0:N_TILES], above[:], chosen_b[:], start=True, stop=True)
                        T.matmul(B[5][:, N_TILES:2 * N_TILES], ones_sq[:], chosen_b[:], start=True, stop=True)\
                            .then_inc(cnt_ps, 1)
                    elif c == 1:
                        for t in range(NS):
                            for n in range(N_TILES):
                                ins = T.matmul(B[5][:, 2 * t:2 * t + 2], one_hot[:, n, t * P:(t + 1) * P], tok2[:, n, :],
                                               start=n == 0, stop=n == N_TILES - 1)
                        ins.then_inc(idx_ps, 1)
                    pe.wait_ge(masked, 4 * N + 4)
                    for j in range(NK):
                        for r in range(4):
                            h = 4 * j + r
                            ins = T.matmul(B[4][DH * r:DH * r + DH, j * P:(j + 1) * P], VT[:, c, DH * h:DH * h + DH],
                                           A[:, h, :], start=False, stop=True, skip_group_check=True)
                    ins.then_inc(pv_ps, 1)
                rms(CH - 1)
                project_out(CH - 1)

            groups(body)

            def block_ready(b):
                pe.wait_ge(fw_hi, b + 1), pe.wait_ge(fw_lo, b + 1)

            def hidden_transposed(n):
                pe.wait_ge(hs_ok, n + 1)
                pe.wait_ge(masked, 4 * N_TILES)
                if n == 0:
                    pe.wait_ge(final_ok, N_TILES)
                for k in range(NK):
                    for t in range(NS):
                        at = (k % 2) * SEL + t * P
                        ins = T.transpose(B[k // 2][:, at:at + P], hs[:, t, k * P:(k + 1) * P], ident[:])
                ins.then_inc(ht_ps, 1)

            def pair(bank, b, p):
                for i in range(2):
                    cols = slice((2 * p + i) * P, (2 * p + i + 1) * P)
                    for k in range(NK):
                        ins = split_matmuls(bank[:, i * SEL:(i + 1) * SEL], (whi[b % 3][:, k, cols], wlo[b % 3][:, k, cols]),
                                            (HTh[:, k, :], HTl[:, k, :]), k == 0, k == NK - 1)
                return ins

            def unit(u):
                k, p = units[u]
                b = block_of[k]
                block_ready(b)
                if u >= 2:
                    if units[u - 2][0][0] == "V":
                        pe.wait_ge(staged_ok, u - 1)
                    else:
                        pe.wait_ge(unit_b, kq_count(u - 2))
                if k[0] == "V":
                    for n in range(NK):
                        rows = slice(p * P, (p + 1) * P)
                        ins = split_matmuls(B[u % 2][:], (HTh[:, n, rows], HTl[:, n, rows]),
                                            (whi[b % 3][:, n, :], wlo[b % 3][:, n, :]), n == 0, n == NK - 1)
                else:
                    ins = pair(B[u % 2], b, p)
                ins.then_inc(unit_ps, 1)

            pe.wait_ge(picked, 16 * 2 * NS), pe.wait_ge(masked, 4 * N_TILES)
            for half in range(2):
                for t in range(NS):
                    at = half * SEL + t * P
                    ins = T.transpose(B[2][:, at:at + P], tab[:, t * 2 * FD + half * P:t * 2 * FD + (half + 1) * P],
                                      ident[:])
            ins.then_inc(tab_ps, 1)
            hidden_transposed(0)
            pe.wait_ge(ht_hi, 1), pe.wait_ge(ht_lo, 1)
            for u in range(before_heads):
                unit(u)
            for h in range(STEPS):
                if h < FH:
                    kv = h // (FH // FKV)
                    pe.wait_ge(unit_lo, kq_unit(h)), pe.wait_ge(cs_ok, 1)
                    if h >= 2:
                        pe.wait_ge(sm_ok, h - 1)
                    for rows, width, at in ((slice(0, P), P, 0), (slice(P, SEL), SEL, P)):
                        ins = split_matmuls(B[2 + h % 2][:, at:at + width], (QRh[:, h, rows], QRl[:, h, rows]),
                                            (KRh[:, kv, 0:width], KRl[:, kv, 0:width]), True, True)
                    ins.then_inc(sc_ps, 1)
                if 1 <= h <= FH:
                    pe.wait_ge(pn_ok, h), pe.wait_ge(pt_lo, h - 1)
                    for n in range(3):
                        ins = T.transpose(B[4][:, n * P:(n + 1) * P], PN[:, (h - 1) % 2, n * P:(n + 1) * P], ident[:])
                    ins.then_inc(pt_ps, 1)
                if 2 <= h <= FH + 1:
                    g = h - 2
                    kv = g // (FH // FKV)
                    cols = slice(kv * FD, (kv + 1) * FD)
                    pe.wait_ge(pt_lo, g + 1), pe.wait_ge(ot_lo, g)
                    split_matmuls(B[5][:, 0:SEL], (Vh[:, 0, cols], Vl[:, 0, cols]),
                                  (PTh[:, g % 2, 0:SEL], PTl[:, g % 2, 0:SEL]), True, False)
                    split_matmuls(B[5][:, P:SEL], (Vh[:, 1, cols], Vl[:, 1, cols]),
                                  (PTh[:, g % 2, SEL:], PTl[:, g % 2, SEL:]), False, True).then_inc(ot_ps, 1)
                u = unit_of_step(h)
                if u is not None:
                    unit(u)
                if h >= 3:
                    g = h - 3
                    b = block_of[f"O{g // 4}"]
                    if g % 4 == 0:
                        block_ready(b)
                    pe.wait_ge(ot_lo, g + 1)
                    for t in range(NS):
                        rows = slice(t * P, (t + 1) * P)
                        ins = split_matmuls(B[6 + t][:], (OTh[:, g % 2, rows], OTl[:, g % 2, rows]),
                                            (whi[b % 3][:, g % 4, :], wlo[b % 3][:, g % 4, :]), g == 0, g == FH - 1)
                    ins.then_inc(wo_ps, 1)
            hidden_transposed(1)
            pe.wait_ge(ht_hi, 2), pe.wait_ge(ht_lo, 2)

            def gate_up(j):
                for k, done, first in (("G", g_ps, 0), ("U", u_ps, 2)):
                    b = block_of[f"{k}{j}"]
                    block_ready(b)
                    for p in range(2):
                        m = 2 * j + p
                        if m >= 2:
                            pe.wait_ge(sg_ok if k == "G" else mt_ok, m - 1)
                        ins = pair(B[first + m % 2], b, p)
                        ins.then_inc(done, 1)

            def down(j):
                b = block_of[f"D{j}"]
                block_ready(b)
                pe.wait_ge(mt_hi, 2 * j + 2), pe.wait_ge(mt_lo, 2 * j + 2)
                if j == 0:
                    pe.wait_ge(hs_ok, 2)
                for i in range(4):
                    for t in range(NS):
                        rows = slice(t * P, (t + 1) * P)
                        ins = split_matmuls(B[6 + t][:], (QRh[:, 4 * j + i, rows], QRl[:, 4 * j + i, rows]),
                                            (whi[b % 3][:, i, :], wlo[b % 3][:, i, :]), j == 0 and i == 0,
                                            j == 3 and i == 3)
                ins.then_inc(down_ps, 1)

            for k in order[block_of["G0"]:]:
                if k[0] == "G":
                    gate_up(int(k[1]))
                elif k[0] == "D":
                    down(int(k[1]))


_NAMES = ("w_router", "wq", "bq", "wk", "bk", "wv", "bv", "wo", "w_gate", "w_up", "w_down")


def kernel(**inputs):
    import numpy as np
    import concourse.bacc as bacc
    from concourse.bass_utils import run_bass_kernel_spmd as run

    W = {k: np.asarray(v) for k, v in inputs.items()}
    slopes = W["L0_attn_slope_rate"].reshape(NH)
    per_feature = np.repeat(slopes, DH)
    tile_major = lambda a, n: a.reshape(n, P).T
    freq = (np.float32(1.0) / np.float32(10000.0) ** (np.arange(0, FD, 2, dtype=np.float32) / np.float32(FD)))
    angle = np.arange(N_TOK, dtype=np.float32)[:, None] * freq.astype(np.float32)
    cos, sin = np.cos(angle.astype(np.float64)), np.sin(angle.astype(np.float64))
    rope = np.concatenate([cos, cos, sin, -sin], axis=1).astype(np.float32)
    data = {
        "x": W["L0_attn_x"].reshape(N_TOK, DM), "WT": W["L0_attn_W_qkvu"].T, "WoT": W["L0_attn_W_out"].T,
        "s_hid": tile_major(per_feature, NK), "s_row": per_feature, "s_head": slopes,
        **{n: W["L0_ffn_" + n] for n in _NAMES},
        "ln1": tile_major(W["L0_ffn_ln1_w"], NK), "ln2": tile_major(W["L0_ffn_ln2_w"], NK), "rope": rope,
    }
    data["bq"], data["bk"] = tile_major(data["bq"], FH), tile_major(data["bk"], FKV)
    data = {"in_" + k: np.ascontiguousarray(v) for k, v in data.items()}
    nc = bacc.Bacc("TRN2", target_bir_lowering=False, num_devices=1)
    args = {n[3:]: nc.dram_tensor(n, a.shape, mybir.dt.from_np(a.dtype), kind="ExternalInput").ap()
            for n, a in data.items()}
    scores = nc.dram_tensor("scores", [N_TOK], mybir.dt.float32).ap()
    out = nc.dram_tensor("out", [N_TOK, DM], mybir.dt.float32, kind="ExternalOutput").ap()
    build(nc, scores=scores, out=out, **args)
    r = run(nc, [data], core_ids=[0])
    return r.results[0]["out"].reshape(1, N_TOK, DM)
```

```python
import concourse.bass as bass
from concourse import mybir
from contextlib import ExitStack

P = 128
N_TOK, DM = 2048, 512
NH, DH = 16, 32
NK = DM // P
GROUP = 256
G = N_TOK // GROUP
CH = GROUP // P
N_TILES = N_TOK // P
SEL = N_TOK // 8
NS = SEL // P
FH, FKV, FD = 16, 8, 128
FF = 2048
NPROJ = 8
PER_SLOT = NPROJ // CH
XT_AHEAD = 4
LN_AHEAD = 5
NX = 3
NBASE = 6


def build(nc, x, WT, WoT, s_hid, s_row, s_head, w_router, wq, bq, wk, bk, wv, bv, wo, w_gate, w_up,
          w_down, ln1, ln2, rope, scores, out):
    f32, f32r, bf16, i32 = mybir.dt.float32, mybir.dt.float32r, mybir.dt.bfloat16, mybir.dt.int32
    ALU, ACT = mybir.AluOpType, mybir.ActivationFunctionType
    V, S, T, Q = nc.vector, nc.scalar, nc.tensor, nc.gpsimd

    x_t = x.rearrange("(n p) d -> n p d", p=P)
    out_t = out.rearrange("(n p) d -> n p d", p=P)
    WT_v = WT.rearrange("(k p) n -> p k n", p=P)
    WoT_v = WoT.rearrange("(k p) n -> p k n", p=P)
    scores_t = scores.rearrange("(n p) -> p n", p=P)

    ctx = ExitStack()
    with ctx:
        def sb(name, shape, dt=f32, c=ctx):
            return c.enter_context(nc.sbuf_tensor(name, shape, dt))

        ident = sb("ident", [P, P])
        tri = sb("tri", [P, P], bf16)
        below = sb("below", [P, P], bf16)
        above = sb("above", [P, P], bf16)
        ones_sq = sb("ones_sq", [P, P], bf16)
        XX = sb("XX", [P, 2 * NX, DM])
        small = sb("small", [P, 200])
        taken = [0]

        def col(n):
            taken[0] += n
            assert taken[0] <= 200
            return small[:, taken[0] - n:taken[0]]

        rstd, sd_ln = col(NX), col(NX)
        shid, nshid, bdec = col(NK), col(NK), col(NK)
        shead, nshead = col(NH), col(NH)
        age, eps_ln, eps_rms, ones1, sd_o, r_o = (col(1) for _ in range(6))
        score_all, n_ge, n_gt, n_eq, rank, chosen, place, before = (col(N_TILES) for _ in range(8))
        stats = sb("stats", [P, NX, 6])
        mv = sb("mv", [P, NX, 2])
        chosen_b = sb("chosen_b", [P, N_TILES], bf16)
        tok2 = sb("tok2", [P, N_TILES, 2], bf16)
        idx_f = sb("idx_f", [P, 2 * NS])
        idx = sb("idx", [P, NS], i32)
        wr_b = sb("wr_b", [P, DM])

        slots = sb("slots", [P, SEL], bf16)

        ca = ExitStack()
        Wh, Wl = (sb(n, [P, NK, 4 * DM], f32r, ca) for n in ("Wh", "Wl"))
        Woh, Wol = (sb(n, [P, NK, DM], f32r, ca) for n in ("Woh", "Wol"))
        xTh, xTl = (sb(n, [P, 2, NK, GROUP], f32r, ca) for n in ("xTh", "xTl"))
        KT, QT, UT = (sb(n, [P, 2, NK, GROUP], f32, ca) for n in ("KT", "QT", "UT"))
        VT = sb("VT", [P, 2, CH, DM], f32, ca)
        BASE = sb("BASE", [P, NBASE, DM], f32, ca)
        kh, kl, qh, ql = (sb(n, [P, NK, P], f32r, ca) for n in ("kh", "kl", "qh", "ql"))
        qdec, uo, sq = (sb(n, [P, NK, P], f32, ca) for n in ("qdec", "uo", "sq"))
        uoh, uol = (sb(n, [P, NK, P], f32r, ca) for n in ("uoh", "uol"))
        kdec = sb("kdec", [P, DM], f32, ca)
        DEC = sb("DEC", [P, NH, P], f32, ca)
        QD = sb("QD", [P, NK, P], f32, ca)
        KD = sb("KD", [P, DM], f32, ca)
        A = sb("A", [P, NH, P], f32, ca)
        R = sb("R", [P, 2, DM], f32, ca)
        state, state_dec, kv_new = (sb(n, [P, NK, P], f32, ca) for n in ("state", "state_dec", "kv_new"))
        BM = sb("BM", [P, P], f32, ca)
        ca.close()
        raw_qkvu = [m[:].rearrange("p b k m -> p (b k m)").rearrange("p (k n) -> p k n", k=NK)
                    for m in (KT, QT, VT, UT)]
        raw_wo = A[:].rearrange("p (k h) m -> p k (h m)", k=NK)
        X, XN = XX[:, 0:NX, :], XX[:, NX:, :]
        s_bc = XX[:, 0:4, :].rearrange("p c d -> p (c d)")
        seen = XX[:, 4:6, :].rearrange("p c d -> p (c d)").bitcast(bf16)
        one_hot = s_bc.bitcast(bf16).rearrange("p (n s) -> p n s", n=N_TILES)
        lag = R[:, 0, 0:P]
        ahead = R[:, 0, P:2 * P]

        cb = ExitStack()
        raw = [sb(f"raw{i}", [P, 4, DM], f32, cb) for i in range(2)]
        whi = [sb(f"whi{i}", [P, 4, DM], f32r, cb) for i in range(3)]
        wlo = [sb(f"wlo{i}", [P, 4, DM], f32r, cb) for i in range(3)]
        QRh = sb("QRh", [P, FH, SEL], f32r, cb)
        tab = sb("tab", [P, NS * 2 * FD], f32, cb)
        CS = sb("CS", [P, 2, SEL], f32, cb)
        bvb = sb("bvb", [P, FKV * FD], f32, cb)
        bqk = sb("bqk", [P, FKV + FH], f32, cb)
        ln12 = sb("ln12", [P, 2, NK], f32, cb)
        causal = sb("causal", [P, 3 * P], f32, cb)
        QRl = sb("QRl", [P, FH, SEL], f32r, cb)
        KRh, KRl = (sb(n, [P, FKV, SEL], f32r, cb) for n in ("KRh", "KRl"))
        Vh, Vl = (sb(n, [P, NS, FKV * FD], f32r, cb) for n in ("Vh", "Vl"))
        HT = sb("HT", [P, NK, SEL], f32, cb)
        HTh, HTl = (sb(n, [P, NK, SEL], f32r, cb) for n in ("HTh", "HTl"))
        ao = sb("ao", [P, NS, DM], f32, cb)
        qb = sb("qb", [P, 2, 2, SEL], f32, cb)
        rope1, rope2 = (sb(n, [P, 2, SEL], f32, cb) for n in ("rope1", "rope2"))
        staged = sb("staged", [P, 2, 2 * SEL], f32, cb)
        SM, PR = (sb(n, [P, 3 * P], f32, cb) for n in ("SM", "PR"))
        PN = sb("PN", [P, 2, 3 * P], f32, cb)
        PTh, PTl = (sb(n, [P, 2, 3 * P], f32r, cb) for n in ("PTh", "PTl"))
        OTh, OTl = (sb(n, [P, 2, SEL], f32r, cb) for n in ("OTh", "OTl"))
        sg = sb("sg", [P, 2, 2 * SEL], f32, cb)
        fsmall = sb("fsmall", [P, 48], f32, cb)
        cb.close()
        hs, xsn, xs = XX[:, 0:NS, :], XX[:, NS:2 * NS, :], XX[:, 2 * NS:, :]
        top, ntop, psum_, pinv = (fsmall[:, 4 * n:4 * n + 4].rearrange("p (a b) -> p a b", a=2) for n in range(4))
        sel_score, gate, sumsq, sd_s, r_s = (fsmall[:, 16 + 2 * n:18 + 2 * n] for n in range(5))
        scrap = staged[:, 0, :]

        def wide(w):
            return lambda i: w.rearrange("(k p) n -> p k n", p=P)[:, :, i * DM:(i + 1) * DM]

        def tall(w):
            return lambda i: w.rearrange("(h p) n -> p h n", p=P)[:, 4 * i:4 * i + 4, :]

        source = {"K": wide(wk), "V": wide(wv), "Q": wide(wq), "O": tall(wo), "G": wide(w_gate), "U": wide(w_up),
                  "D": tall(w_down)}
        order = ["K0", "K1", "V0", "V1", "Q0", "Q1", "O0", "Q2", "O1", "Q3", "O2", "O3",
                 "G0", "U0", "G1", "U1", "D0", "G2", "U2", "D1", "G3", "U3", "D2", "D3"]
        block_of = {k: n for n, k in enumerate(order)}
        units = [(k, p) for k in ("K0", "K1", "V0", "V1", "Q0", "Q1", "Q2", "Q3") for p in range(2)]
        before_heads = 10
        STEPS = FH + 3

        def unit_of_step(h):
            return before_heads + h // 2 if h % 2 == 0 and before_heads + h // 2 < len(units) else None

        def kq_unit(h):
            return 9 + h // 2 if h >= 4 else before_heads

        def kq_count(u):
            return sum(units[n][0][0] != "V" for n in range(u + 1))

        rank_in = {(N_TILES - 4, 0): (0, 3), (N_TILES - 4, 1): (3, 6), (N_TILES - 3, 0): (6, 9),
                   (N_TILES - 3, 1): (9, 12), (N_TILES - 2, 0): (12, 14), (N_TILES - 2, 1): (14, N_TILES)}
        split_after = {2: "O1", 6: "Q3", 7: "O2", 11: "O3", 12: "G0", 15: "U0"}

        B = [ctx.enter_context(nc.psum_tensor(f"bank{i}", [P, 512], f32)) for i in range(8)]

        def tiles4(ap):
            return ap.rearrange("p (k m) -> p k m", k=4)

        def sems(names):
            return [ctx.enter_context(nc.semaphore(n)) for n in names.split()]

        class Chain:

            def __init__(self, eng, done):
                self.eng, self.done, self.n = eng, done, 0

            def link(self, ins):
                self.n += 1
                ins.then_inc(self.done, 1)
                self.eng.wait_ge(self.done, self.n)

        x_in = sems("x_in_0 x_in_1 x_in_2")
        const_in, sbc_in, score_out = sems("const_in sbc_in score_out")
        w_raw = sems("w_raw_k w_raw_q w_raw_v w_raw_u w_raw_o")
        stored = sems("stored_even stored_odd")
        raw_in = sems("raw_in_even raw_in_odd")
        part_in, picked, scattered = sems("part_in picked scattered")
        consts, slopes_ok, iota_ok, masks_ok, tok_ok, lag_ok = sems("consts slopes_ok iota_ok masks_ok tok_ok lag_ok")
        decays_ok, dec_ok, bm_ok, causal_ok = sems("decays_ok dec_ok bm_ok causal_ok")
        w_hi, w_lo, w_lo_pool = sems("w_hi w_lo w_lo_pool")
        var_ok, sd_ln_ok, xn_ok, score_ok, base_ok = sems("var_ok sd_ln_ok xn_ok score_ok base_ok")
        xt_ps, xt_hi, xt_lo, proj_ps, proj_sb = sems("xt_ps xt_hi xt_lo proj_ps proj_sb")
        k_hi, q_hi, k_lo, q_lo, q_dec, kt_ps, k_dec = sems("k_hi q_hi k_lo q_lo q_dec kt_ps k_dec")
        s_ps, masked, inter_ps, kv_ps, pv_ps = sems("s_ps masked inter_ps kv_ps pv_ps")
        state_dk, state_ok, uo_ok, sq_ok, uo_hi, uo_lo = sems("state_dk state_ok uo_ok sq_ok uo_hi uo_lo")
        rms_ps, sd_o_ok, out_ps, final_ok = sems("rms_ps sd_o_ok out_ps final_ok")
        rank_ok, cnt_ps, oh_ok, idx_ps, idx_ok = sems("rank_ok cnt_ps oh_ok idx_ps idx_ok")
        dve_chain, pool_chain = sems("dve_chain pool_chain")
        fw_hi, fw_lo = sems("fw_hi fw_lo")
        var_s_ok, sd_s_ok, hs_ok, ht_ps, tab_ps = sems("var_s_ok sd_s_ok hs_ok ht_ps tab_ps")
        cs_ok, ht_ok, ht_hi, ht_lo = sems("cs_ok ht_ok ht_hi ht_lo")
        unit_ps, unit_b, staged_ok, unit_hi, unit_lo = sems("unit_ps unit_b staged_ok unit_hi unit_lo")
        sc_ps, sm_ok, exp_ok, pn_ok, pt_ps, pt_hi, pt_lo = sems("sc_ps sm_ok exp_ok pn_ok pt_ps pt_hi pt_lo")
        ot_ps, ot_hi, ot_lo, wo_ps, gate_ok = sems("ot_ps ot_hi ot_lo wo_ps gate_ok")
        g_ps, u_ps, sg_ok, mt_ok, mt_hi, mt_lo = sems("g_ps u_ps sg_ok mt_ok mt_hi mt_lo")
        down_ps, delta_ok = sems("down_ps delta_ok")

        def last_use(b):
            if b < 0:
                return unit_ps, 0
            k, i = order[b][0], int(order[b][1])
            if k in "KVQ":
                return unit_ps, [u for u, (name, _) in enumerate(units) if name == order[b]][-1] + 1
            return {"O": (wo_ps, 4 * i + 4), "G": (g_ps, 2 * i + 2), "U": (u_ps, 2 * i + 2),
                    "D": (down_ps, i + 1)}[k]

        def proj_tiles(N):
            group = N // CH + 1
            return [NPROJ * group + PER_SLOT * (N % CH) + i for i in range(PER_SLOT)] if group < G else []

        slots_of_chunks = range(-CH, N_TILES)

        block = ctx.enter_context(nc.Block())

        @block.sync
        def _(sp):
            def load_x(M):
                if M >= NX:
                    sp.wait_ge(base_ok, M - NX + 1)
                sp.dma_start(X[:, M % NX, :], x_t[M]).then_inc(x_in[M % NX], 16)

            def load_block(b):
                k = order[b]
                if b >= 2:
                    sp.wait_ge(fw_hi, b - 1), sp.wait_ge(fw_lo, b - 1)
                sp.dma_start(raw[b % 2][:], source[k[0]](int(k[1]))).then_inc(raw_in[b % 2], 16)

            def store(N):
                sp.wait_ge(final_ok, N + 1)
                sp.dma_start(out_t[N], R[:, N % 2, :]).then_inc(stored[N % 2], 16)

            for M in range(NX):
                load_x(M)
            for n, q in enumerate((1, 0, 2, 3)):
                sp.dma_start(raw_qkvu[n], WT_v[:, :, q * DM:(q + 1) * DM]).then_inc(w_raw[n], 16)
            sp.dma_start(raw_wo, WoT_v).then_inc(w_raw[4], 16)
            load_x(NX), load_x(NX + 1)

            for N in slots_of_chunks:
                M = N + LN_AHEAD
                if N >= 2:
                    store(N - 2)
                if M < N_TILES:
                    if M + 2 < N_TILES and M + 2 > NX + 1:
                        load_x(M + 2)
                    if M % 4 == 3:
                        sp.wait_ge(score_ok, M + 1)
                        sp.dma_start(scores_t[:, M - 3:M + 1], score_all[:, M - 3:M + 1],
                                     allow_slow_non_contiguous=True).then_inc(score_out, 16)
                if N == N_TILES - XT_AHEAD:
                    sp.wait_ge(score_out, 16 * N_TILES // 4)
                    sp.wait_ge(xt_ps, N_TILES), sp.wait_ge(base_ok, N_TILES)
                    sp.dma_start(s_bc, scores.partition_broadcast(P)).then_inc(sbc_in, 16)
                if N == N_TILES - CH:
                    sp.wait_ge(proj_ps, NPROJ * G)
                    load_block(0)
                    load_block(1)
                    sp.dma_start(bqk[:, 0:FKV], bk).then_inc(part_in, 16)
                    sp.dma_start(bqk[:, FKV:], bq).then_inc(part_in, 16)
                    sp.dma_start(ln12[:, 0, :], ln1).then_inc(part_in, 16)
                    sp.dma_start(ln12[:, 1, :], ln2).then_inc(part_in, 16)
                    sp.dma_start(bvb[:], bv.partition_broadcast(P)).then_inc(part_in, 16)
                    load_block(2)
            store(N_TILES - 2)
            load_block(3)
            store(N_TILES - 1)
            for b in range(4, len(order)):
                load_block(b)
            for c in range(2):
                sp.wait_ge(stored[c], 16 * N_TILES // 2)

        @block.scalar
        def _(act):
            for dst, src in ((wr_b[:], w_router.partition_broadcast(P)), (shid, s_hid),
                             (KD[:], s_row.partition_broadcast(P)), (shead, s_head.partition_broadcast(P))):
                act.dma_start(dst, src).then_inc(const_in, 16)

            def weights_hi(n):
                act.wait_ge(w_raw[n], 16)
                q = (1, 0, 2, 3, 0)[n]
                dst, src = (Wh[:, :, q * DM:(q + 1) * DM], raw_qkvu[n]) if n < 4 else (Woh[:], raw_wo)
                S.activation(dst, src, ACT.Copy).then_inc(w_hi, 1)

            def ln_sd(first, count):
                act.wait_ge(var_ok, first + count), act.wait_ge(consts, 1)
                s = first % NX
                S.activation(sd_ln[:, s:s + count], mv[:, s:s + count, 1], ACT.Sqrt, bias=eps_ln)\
                    .then_inc(sd_ln_ok, count)

            def xt_high(M):
                act.wait_ge(xt_ps, M + 1)
                act.wait_ge(proj_ps, NPROJ * max(M // CH - 1, 0))
                S.activation(xTh[:, M // CH % 2, :, M % CH * P:(M % CH + 1) * P], tiles4(B[5][:]), ACT.Copy)\
                    .then_inc(xt_hi, 1)

            def evacuate(tile):
                g, i = tile // NPROJ, tile % NPROJ
                name, j = "KQVU"[i // 2], i % 2
                act.wait_ge(proj_ps, tile + 1)
                if j == 0:
                    used = CH * max(g - 1, 0)
                    if name == "K":
                        act.wait_ge(w_lo, 1), act.wait_ge(k_lo, used), act.wait_ge(kt_ps, used), act.wait_ge(k_hi, used)
                    if name == "Q":
                        act.wait_ge(w_lo, 2), act.wait_ge(q_lo, used), act.wait_ge(q_dec, used), act.wait_ge(q_hi, used)
                    if name == "V":
                        act.wait_ge(w_lo_pool, 1), act.wait_ge(pv_ps, used), act.wait_ge(kv_ps, used)
                    if name == "U":
                        act.wait_ge(w_lo_pool, 2), act.wait_ge(uo_ok, used)
                if name == "V":
                    dst = VT[:, g % 2, j, :]
                else:
                    dst = {"K": KT, "Q": QT, "U": UT}[name][:, g % 2, 2 * j:2 * j + 2, :].rearrange("p k m -> p (k m)")
                S.activation(dst, B[2 + tile % 2][:], ACT.Silu if name in "KQ" else ACT.Copy).then_inc(proj_sb, 1)

            def split_high(N):
                act.wait_ge(proj_sb, NPROJ * (N // CH) + 4)
                act.wait_ge(s_ps, 2 * N), act.wait_ge(k_lo, N), act.wait_ge(q_lo, N)
                cols = slice(N % CH * P, (N % CH + 1) * P)
                S.activation(kh[:], KT[:, N // CH % 2, :, cols], ACT.Copy).then_inc(k_hi, 1)
                S.activation(qh[:], QT[:, N // CH % 2, :, cols], ACT.Copy).then_inc(q_hi, 1)

            def rms_sd(N):
                act.wait_ge(rms_ps, N + 1)
                act.wait_ge(final_ok, N)
                S.activation(sd_o, B[7][:, 0:1], ACT.Sqrt, scale=1.0 / DM, bias=eps_rms).then_inc(sd_o_ok, 1)

            def decay_tables(part):
                act.wait_ge(iota_ok, 3), act.wait_ge(lag_ok, 1), act.wait_ge(slopes_ok, 1), act.wait_ge(w_hi, 5)
                act.wait_ge(w_lo, 3)
                for h in range(part * NH // 2, (part + 1) * NH // 2):
                    S.activation(DEC[:, h, :], lag, ACT.Exp, scale=nshead[:, h:h + 1])
                if part:
                    for k in range(NK):
                        S.activation(QD[:, k, :], ahead, ACT.Exp, scale=nshid[:, k:k + 1])
                    S.activation(bdec, shid, ACT.Exp, scale=-float(P))
                    S.activation(KD[:], KD[:], ACT.Exp, scale=age).then_inc(decays_ok, 1)

            def block_hi(b):
                act.wait_ge(raw_in[b % 2], 16 * (b // 2 + 1))
                act.wait_ge(*last_use(b - 3))
                S.activation(whi[b % 3][:], raw[b % 2][:], ACT.Copy).then_inc(fw_hi, 1)

            ln_sd(0, NX)
            weights_hi(0)
            xt_high(0)
            xt_high(1)
            weights_hi(1)
            for N in slots_of_chunks:
                tiles = proj_tiles(N)
                M = N + LN_AHEAD
                if tiles:
                    evacuate(tiles[0])
                if N == -2:
                    weights_hi(2)
                if N == -1:
                    evacuate(tiles[1])
                    evacuate(tiles[2])
                if N >= 1:
                    rms_sd(N - 1)
                if M < N_TILES:
                    ln_sd(M, 1)
                if tiles and N != -1:
                    evacuate(tiles[1])
                if -1 <= N < N_TILES - 1:
                    split_high(N + 1)
                if N == -2:
                    weights_hi(3)
                if N + XT_AHEAD < N_TILES:
                    xt_high(N + XT_AHEAD)
                if tiles and N != -1:
                    evacuate(tiles[2])
                if N == -2:
                    weights_hi(4)
                if N == -1:
                    decay_tables(0)
                if N >= 0:
                    act.wait_ge(uo_ok, N + 1)
                    act.wait_ge(rms_ps, N)
                    S.activation(sq[:], tiles4(B[4][:]), ACT.Square).then_inc(sq_ok, 1)
                    act.wait_ge(out_ps, N), act.wait_ge(uo_lo, N)
                    S.activation(uoh[:], uo[:], ACT.Copy).then_inc(uo_hi, 1)
                if tiles:
                    evacuate(tiles[3])
                if N == -1:
                    decay_tables(1)
                if N == N_TILES - 2:
                    block_hi(0)
                    block_hi(1)
            rms_sd(N_TILES - 1)

            def norm_sd(n, func_input, scale, bias):
                S.activation(sd_s, func_input, ACT.Sqrt, scale=scale, bias=bias).then_inc(sd_s_ok, 1)

            def scaled_transpose(n):
                act.wait_ge(ht_ps, n + 1), act.wait_ge(part_in, 16 * 5)
                for k in range(NK):
                    ins = S.activation(HT[:, k, :], B[k // 2][:, (k % 2) * SEL:(k % 2 + 1) * SEL], ACT.Copy,
                                       scale=ln12[:, n, k:k + 1])
                ins.then_inc(ht_ok, 1)
                act.wait_ge(ht_ok, n + 1)
                if n:
                    act.wait_ge(unit_ps, len(units))
                S.activation(HTh[:], HT[:], ACT.Copy).then_inc(ht_hi, 1)

            def unit_bias(u):
                k, p = units[u]
                if k[0] == "V":
                    return
                act.wait_ge(unit_ps, u + 1)
                if u >= 2:
                    act.wait_ge(staged_ok, u - 1)
                for i in range(2):
                    head = 4 * int(k[1]) + 2 * p + i + (FKV if k[0] == "Q" else 0)
                    ins = S.activation(qb[:, u % 2, i, :], B[u % 2][:, i * SEL:(i + 1) * SEL], ACT.Identity,
                                       bias=bqk[:, head:head + 1])
                ins.then_inc(unit_b, 1)

            def unit_dst(u, part):
                k, p = units[u]
                i = int(k[1])
                if k[0] == "V":
                    return (Vh, Vl)[part][:, p, i * DM:(i + 1) * DM]
                dst = ((KRh, KRl) if k[0] == "K" else (QRh, QRl))[part]
                return dst[:, 4 * i + 2 * p:4 * i + 2 * p + 2, :].rearrange("p h m -> p (h m)")

            def unit_high(u):
                act.wait_ge(staged_ok, u + 1)
                S.activation(unit_dst(u, 0), staged[:, u % 2, :], ACT.Copy).then_inc(unit_hi, 1)

            act.wait_ge(var_s_ok, 1)
            norm_sd(0, mv[:, 0:NS, 1], 1.0, eps_ln)
            act.wait_ge(var_s_ok, 2)
            norm_sd(1, sumsq, 1.0 / DM, eps_rms)
            block_hi(2)
            scaled_transpose(0)
            for u in range(before_heads):
                unit_bias(u)
                if u:
                    unit_high(u - 1)
                if u % 2:
                    block_hi(u // 2 + 3)
            unit_high(before_heads - 1)
            S.activation(gate, sel_score, ACT.Exp, scale=-1.0).then_inc(gate_ok, 1)
            for h in range(STEPS):
                if h < FH:
                    act.wait_ge(sm_ok, h + 1), act.wait_ge(pn_ok, h)
                    for t, cols in ((0, slice(0, P)), (1, slice(P, 3 * P))):
                        ins = S.activation(PR[:, cols], SM[:, cols], ACT.Exp, scale=float(FD) ** -0.5,
                                           bias=ntop[:, h % 2, t:t + 1], accum_out=psum_[:, h % 2, t:t + 1])
                    ins.then_inc(exp_ok, 1)
                if 1 <= h <= FH:
                    act.wait_ge(pt_ps, h)
                    if h >= 3:
                        act.wait_ge(ot_ps, h - 2)
                    S.activation(PTh[:, (h - 1) % 2, :], B[4][:, 0:3 * P], ACT.Copy).then_inc(pt_hi, 1)
                if 2 <= h <= FH + 1:
                    act.wait_ge(ot_ps, h - 1)
                    if h >= 4:
                        act.wait_ge(wo_ps, h - 3)
                    S.activation(OTh[:, (h - 2) % 2, :], B[5][:, 0:SEL], ACT.Copy).then_inc(ot_hi, 1)
                u = unit_of_step(h)
                if u is not None:
                    unit_bias(u)
                    unit_high(u)
                if h in split_after:
                    block_hi(block_of[split_after[h]])
            block_hi(14)
            act.wait_ge(var_s_ok, 3)
            norm_sd(2, sumsq, 1.0 / DM, eps_rms)
            scaled_transpose(1)
            for j in range(4):
                for p in range(2):
                    m = 2 * j + p
                    act.wait_ge(g_ps, m + 1)
                    if m >= 2:
                        act.wait_ge(mt_ok, m - 1)
                    S.activation(sg[:, m % 2, :], B[m % 2][:], ACT.Silu).then_inc(sg_ok, 1)
                block_hi(block_of[f"G{j}"] + 3) if block_of[f"G{j}"] + 3 < len(order) else None
                for p in range(2):
                    m = 2 * j + p
                    act.wait_ge(mt_ok, m + 1)
                    S.activation(QRh[:, 2 * m:2 * m + 2, :].rearrange("p h m -> p (h m)"), staged[:, m % 2, :],
                                 ACT.Copy).then_inc(mt_hi, 1)
                for b in range(block_of[f"G{j}"] + 4, (block_of[f"G{j + 1}"] if j < 3 else len(order)) + 3):
                    if b < len(order):
                        block_hi(b)

        @block.vector
        def _(dve):
            ch = Chain(dve, dve_chain)
            V.memset(eps_ln, 1e-5)
            V.memset(ones1, 1.0)
            V.memset(eps_rms, 1e-6).then_inc(consts, 1)

            def ln_stats(M):
                s = M % NX
                dve.wait_ge(x_in[s], 16 * (M // NX + 1))
                dve.wait_ge(xn_ok, max(M - NX + 1, 0))
                ch.link(V.bn_stats(stats[:, s, :], X[:, s, :]))
                V.bn_aggr(mv[:, s, :], stats[:, s, :]).then_inc(var_ok, 1)

            def ln_norm(M):
                s = M % NX
                dve.wait_ge(sd_ln_ok, M + 1)
                ch.link(V.reciprocal(rstd[:, s:s + 1], sd_ln[:, s:s + 1]))
                if M >= NX:
                    dve.wait_ge(xt_ps, M - NX + 1), dve.wait_ge(base_ok, M - NX + 1)
                V.tensor_scalar(XN[:, s, :], X[:, s, :], mv[:, s, 0:1], rstd[:, s:s + 1], ALU.subtract,
                                ALU.mult).then_inc(xn_ok, 1)

            def router(M):
                dve.wait_ge(const_in, 64), dve.wait_ge(xn_ok, M + 1)
                V.tensor_tensor_reduce(out=kv_new[:].rearrange("p k m -> p (k m)"), in0=XN[:, M % NX, :], in1=wr_b[:],
                                       scale=1.0, scalar=0.0, op0=ALU.mult, op1=ALU.add,
                                       accum_out=score_all[:, M:M + 1]).then_inc(score_ok, 1)

            def xt_low(M):
                at = slice(M % CH * P, (M % CH + 1) * P)
                dve.wait_ge(xt_hi, M + 1)
                V.tensor_tensor(xTl[:, M // CH % 2, :, at], tiles4(B[5][:]), xTh[:, M // CH % 2, :, at].bitcast(f32),
                                ALU.subtract).then_inc(xt_lo, 1)

            def weights_lo(n):
                dve.wait_ge(w_hi, n + 1)
                q = (1, 0, 2, 3, 0)[n]
                dst, hi, src = (Wl[:, :, q * DM:(q + 1) * DM], Wh[:, :, q * DM:(q + 1) * DM], raw_qkvu[n]) \
                    if n < 4 else (Wol[:], Woh[:], raw_wo)
                V.tensor_tensor(dst, src, hi.bitcast(f32), ALU.subtract).then_inc(w_lo, 1)

            def rank_tokens(first, last):
                if first == 0:
                    dve.wait_ge(sbc_in, 16), dve.wait_ge(score_ok, N_TILES)
                    ch.link(V.memset(n_ge, 0.0))
                for n in range(first, last):
                    me = score_all[:, n:n + 1]
                    if n:
                        ch.link(V.tensor_scalar(seen[:, 0:n * P], s_bc[:, 0:n * P], me, None, ALU.is_ge, ALU.add,
                                                accum_out=n_ge[:, n:n + 1]))
                    ch.link(V.tensor_scalar(seen[:, n * P:], s_bc[:, n * P:], me, None, ALU.is_gt, ALU.add,
                                            accum_out=n_gt[:, n:n + 1]))
                    ch.link(V.scalar_tensor_tensor(out=seen[:, 0:P], in0=s_bc[:, n * P:(n + 1) * P], scalar=me,
                                                   in1=below[:], op0=ALU.is_equal, op1=ALU.mult,
                                                   accum_out=n_eq[:, n:n + 1]))
                if last < N_TILES:
                    return
                ch.link(V.tensor_tensor(rank, n_ge, n_gt, ALU.add))
                ch.link(V.tensor_tensor(rank, rank, n_eq, ALU.add))
                V.tensor_scalar(chosen, rank, float(SEL), None, ALU.is_lt)
                V.tensor_scalar(chosen_b[:], rank, float(SEL), None, ALU.is_lt).then_inc(rank_ok, 1)

            def place_tokens():
                dve.wait_ge(cnt_ps, 1), dve.wait_ge(rank_ok, 1)
                ch.link(V.tensor_copy(n_gt, B[5][:, N_TILES:2 * N_TILES]))
                ch.link(V.tensor_tensor_scan(before, n_gt, n_ge, 0.0, ALU.add, ALU.bypass))
                ch.link(V.tensor_tensor(before, before, n_gt, ALU.subtract))
                ch.link(V.tensor_tensor(place, B[5][:, 0:N_TILES], before, ALU.add))
                ch.link(V.tensor_scalar(n_eq, chosen, -float(N_TOK), float(N_TOK), ALU.mult, ALU.add))
                ch.link(V.tensor_tensor(place, place, n_eq, ALU.add))
                for n in range(N_TILES):
                    ins = V.tensor_scalar(one_hot[:, n, :], slots[:], place[:, n:n + 1], None, ALU.is_equal)
                ins.then_inc(oh_ok, 1)

            def token_indices():
                dve.wait_ge(idx_ps, 1)
                ch.link(V.tensor_copy(idx_f[:], B[5][:, 0:2 * NS]))
                for t in range(NS):
                    ins = V.scalar_tensor_tensor(out=idx[:, t:t + 1], in0=idx_f[:, 2 * t + 1:2 * t + 2],
                                                 scalar=float(P), in1=idx_f[:, 2 * t:2 * t + 1], op0=ALU.mult,
                                                 op1=ALU.add)
                ins.then_inc(idx_ok, 1)

            def k_low(N):
                dve.wait_ge(k_hi, N + 1)
                V.tensor_tensor(kl[:], KT[:, N // CH % 2, :, N % CH * P:(N % CH + 1) * P], kh[:].bitcast(f32),
                                ALU.subtract).then_inc(k_lo, 1)

            def mask(N, half):
                dve.wait_ge(s_ps, 2 * N + half + 1), dve.wait_ge(pv_ps, N), dve.wait_ge(dec_ok, 1)
                for b in range(2):
                    r = 2 * half + b
                    V.tensor_tensor(A[:].rearrange("p (j r) m -> p r j m", r=4)[:, r], tiles4(B[b][:]),
                                    DEC[:].rearrange("p (j r) m -> p r j m", r=4)[:, r], ALU.mult).then_inc(masked, 1)

            def new_state(N):
                dve.wait_ge(kv_ps, N + 1), dve.wait_ge(state_dk, N + 1), dve.wait_ge(bm_ok, 1)
                dve.wait_ge(score_ok, min(N + LN_AHEAD + 1, N_TILES))
                ch.link(V.tensor_tensor(kv_new[:], tiles4(B[6][:]), BM[:].unsqueeze(1).to_broadcast([P, NK, P]),
                                        ALU.mult))
                V.tensor_tensor(state[:], kv_new[:], state_dec[:], ALU.add).then_inc(state_ok, 1)

            def final(N):
                dve.wait_ge(out_ps, N + 1), dve.wait_ge(sd_o_ok, N + 1)
                ch.link(V.reciprocal(r_o, sd_o))
                dve.wait_ge(stored[N % 2], 16 * (N // 2))
                dve.wait_ge(base_ok, N + 1)
                V.scalar_tensor_tensor(out=R[:, N % 2, :], in0=B[7][:], scalar=r_o, in1=BASE[:, N % NBASE, :],
                                       op0=ALU.mult, op1=ALU.add).then_inc(final_ok, 1)

            for M in range(NX):
                ln_stats(M)
            for M in range(NX):
                ln_norm(M)
            weights_lo(0)
            xt_low(0)
            xt_low(1)
            weights_lo(1)
            dve.wait_ge(const_in, 64)
            V.tensor_scalar(nshead, shead, -1.0, None, ALU.mult)
            V.tensor_scalar(nshid, shid, -1.0, None, ALU.mult).then_inc(slopes_ok, 1)
            dve.wait_ge(iota_ok, 3)
            V.tensor_scalar(lag, lag, 0.0, None, ALU.max).then_inc(lag_ok, 1)
            for M in range(NX):
                router(M)
                dve.wait_ge(score_ok, M + 1)
            ch.link(V.memset(BM[:], 0.0))
            for r in range(4):
                V.memset(BM[DH * r:DH * r + DH, DH * r:DH * r + DH], 1.0)
            V.memset(state[:], 0.0).then_inc(bm_ok, 1)
            dve.wait_ge(bm_ok, 1)
            for N in slots_of_chunks:
                M = N + LN_AHEAD
                if M < N_TILES:
                    ln_stats(M)
                if (N, 0) in rank_in:
                    rank_tokens(*rank_in[N, 0])
                if N >= 0:
                    mask(N, 0)
                    dve.wait_ge(kt_ps, N + 1), dve.wait_ge(kv_ps, N)
                    V.tensor_tensor(kdec[:], B[5][:], KD[:], ALU.mult).then_inc(k_dec, 1)
                if (N, 1) in rank_in:
                    rank_tokens(*rank_in[N, 1])
                if M < N_TILES:
                    ln_norm(M)
                    dve.wait_ge(state_ok, max(N, 0))
                    router(M)
                    if N < 0:
                        dve.wait_ge(score_ok, M + 1)
                if N >= 0:
                    mask(N, 1)
                    if N >= 1:
                        final(N - 1)
                    new_state(N)
                if -1 <= N < N_TILES - 1:
                    k_low(N + 1)
                if N + XT_AHEAD < N_TILES:
                    xt_low(N + XT_AHEAD)
                if N == -2:
                    weights_lo(4)
                if N == -1:
                    dve.wait_ge(decays_ok, 1), dve.wait_ge(masks_ok, 3)
                    V.tensor_tensor(DEC[:], DEC[:], tri[:].unsqueeze(1).to_broadcast([P, NH, P]), ALU.mult)\
                        .then_inc(dec_ok, 1)
                if N == N_TILES - 1:
                    place_tokens()
                if N >= 0:
                    at = slice(N % CH * P, (N % CH + 1) * P)
                    dve.wait_ge(pv_ps, N + 1), dve.wait_ge(uo_hi, N), dve.wait_ge(uo_lo, N)
                    V.tensor_tensor(uo[:], tiles4(B[4][:]), UT[:, N // CH % 2, :, at], ALU.mult).then_inc(uo_ok, 1)
            token_indices()
            final(N_TILES - 1)

            dve.wait_ge(final_ok, N_TILES), dve.wait_ge(stored[0], 8 * N_TILES), dve.wait_ge(stored[1], 8 * N_TILES)
            dve.wait_ge(picked, 16 * 2 * NS)

            def normed(n, src):
                for t in range(NS):
                    ins = V.tensor_tensor_reduce(out=hs[:, t, :], in0=src[:, t, :], in1=src[:, t, :], scale=1.0,
                                                 scalar=0.0, op0=ALU.mult, op1=ALU.add, accum_out=sumsq[:, t:t + 1])
                ins.then_inc(var_s_ok, 1)
                dve.wait_ge(sd_s_ok, n + 2)
                ch.link(V.reciprocal(r_s, sd_s))
                for t in range(NS):
                    ins = V.tensor_scalar(hs[:, t, :], src[:, t, :], r_s[:, t:t + 1], None, ALU.mult)
                ins.then_inc(hs_ok, 1)

            def low_of(dst, src, high, done):
                V.tensor_tensor(dst, src, high.bitcast(f32), ALU.subtract).then_inc(done, 1)

            for t in range(NS):
                ch.link(V.bn_stats(stats[:, t, :], xs[:, t, :]))
            for t in range(NS):
                ins = V.bn_aggr(mv[:, t, :], stats[:, t, :])
            ins.then_inc(var_s_ok, 1)
            dve.wait_ge(sd_s_ok, 1)
            ch.link(V.reciprocal(r_s, sd_s))
            for t in range(NS):
                ch.link(V.tensor_scalar(xsn[:, t, :], xs[:, t, :], mv[:, t, 0:1], r_s[:, t:t + 1], ALU.subtract,
                                        ALU.mult))
            for t in range(NS):
                ch.link(V.tensor_tensor_reduce(out=hs[:, t, :], in0=xsn[:, t, :], in1=wr_b[:], scale=1.0, scalar=0.0,
                                               op0=ALU.mult, op1=ALU.add, accum_out=sel_score[:, t:t + 1]))
            normed(0, xsn)
            dve.wait_ge(tab_ps, 1)
            V.tensor_copy(CS[:].rearrange("p a m -> p (a m)"), B[2][:]).then_inc(cs_ok, 1)
            dve.wait_ge(ht_hi, 1)
            low_of(HTl[:], HT[:], HTh[:], ht_lo)

            def stage(u):
                k, p = units[u]
                if u >= 2:
                    dve.wait_ge(unit_hi, u - 1), dve.wait_ge(unit_lo, u - 1)
                if k[0] == "V":
                    dve.wait_ge(unit_ps, u + 1), dve.wait_ge(part_in, 16 * 5)
                    i = int(k[1])
                    V.tensor_tensor(staged[:, u % 2, :], B[u % 2][:], bvb[:, i * DM:(i + 1) * DM], ALU.add)\
                        .then_inc(staged_ok, 1)
                    return
                dve.wait_ge(unit_b, kq_count(u)), dve.wait_ge(cs_ok, 1)
                dve.wait_ge(staged_ok, u)
                both = qb[:, u % 2]
                half = P // 2
                V.tensor_tensor(rope1[:], both, CS[:, 0, :].unsqueeze(1).to_broadcast([P, 2, SEL]), ALU.mult)
                for a, b in ((0, half), (half, 0)):
                    ins = V.tensor_tensor(rope2[a:a + half], both[b:b + half],
                                          CS[b:b + half, 1, :].unsqueeze(1).to_broadcast([half, 2, SEL]), ALU.mult)
                ch.link(ins)
                V.tensor_tensor(staged[:, u % 2, :].rearrange("p (a m) -> p a m", a=2), rope1[:], rope2[:],
                                ALU.add).then_inc(staged_ok, 1)

            def unit_low(u):
                k, p = units[u]
                i = int(k[1])
                dve.wait_ge(unit_hi, u + 1)
                if k[0] == "V":
                    low_of(Vl[:, p, i * DM:(i + 1) * DM], staged[:, u % 2, :], Vh[:, p, i * DM:(i + 1) * DM], unit_lo)
                else:
                    hi, lo = (KRh, KRl) if k[0] == "K" else (QRh, QRl)
                    heads = slice(4 * i + 2 * p, 4 * i + 2 * p + 2)
                    low_of(lo[:, heads, :], staged[:, u % 2, :].rearrange("p (a m) -> p a m", a=2), hi[:, heads, :],
                           unit_lo)

            for u in range(before_heads):
                stage(u)
                if u:
                    unit_low(u - 1)
            unit_low(before_heads - 1)
            dve.wait_ge(causal_ok, 3)
            for h in range(STEPS):
                if h < FH:
                    dve.wait_ge(sc_ps, h + 1), dve.wait_ge(exp_ok, h)
                    for t, cols in ((0, slice(0, P)), (1, slice(P, 3 * P))):
                        ins = V.tensor_tensor_reduce(out=SM[:, cols], in0=B[2 + h % 2][:, cols], in1=causal[:, cols],
                                                     scale=1.0, scalar=-3.0e38, op0=ALU.add, op1=ALU.max,
                                                     accum_out=top[:, h % 2, t:t + 1])
                    ch.link(ins)
                    V.tensor_scalar(ntop[:, h % 2, :], top[:, h % 2, :], -(float(FD) ** -0.5), None, ALU.mult)\
                        .then_inc(sm_ok, 1)
                if 1 <= h <= FH:
                    dve.wait_ge(pt_hi, h)
                    if h >= 3:
                        dve.wait_ge(ot_ps, h - 2)
                    low_of(PTl[:, (h - 1) % 2, :], B[4][:, 0:3 * P], PTh[:, (h - 1) % 2, :], pt_lo)
                if h < FH:
                    dve.wait_ge(exp_ok, h + 1)
                    if h >= 2:
                        dve.wait_ge(pt_ps, h - 1)
                    ch.link(V.reciprocal(pinv[:, h % 2, :], psum_[:, h % 2, :]))
                    for t, cols in ((0, slice(0, P)), (1, slice(P, 3 * P))):
                        ins = V.tensor_scalar(PN[:, h % 2, cols], PR[:, cols], pinv[:, h % 2, t:t + 1], None, ALU.mult)
                    ins.then_inc(pn_ok, 1)
                if 2 <= h <= FH + 1:
                    dve.wait_ge(ot_hi, h - 1)
                    if h >= 4:
                        dve.wait_ge(wo_ps, h - 3)
                    low_of(OTl[:, (h - 2) % 2, :], B[5][:, 0:SEL], OTh[:, (h - 2) % 2, :], ot_lo)
                u = unit_of_step(h)
                if u is not None:
                    stage(u)
                    unit_low(u)
            dve.wait_ge(gate_ok, 1)
            ch.link(V.tensor_scalar(gate, gate, 1.0, None, ALU.add))
            ch.link(V.reciprocal(gate, gate))
            dve.wait_ge(wo_ps, FH)
            for t in range(NS):
                ins = V.tensor_copy(ao[:, t, :], B[6 + t][:])
            ch.link(ins)
            for t in range(NS):
                ins = V.tensor_tensor(xs[:, t, :], xsn[:, t, :], ao[:, t, :], ALU.add)
            ch.link(ins)
            normed(1, xs)
            dve.wait_ge(ht_hi, 2)
            low_of(HTl[:], HT[:], HTh[:], ht_lo)
            for j in range(4):
                for p in range(2):
                    m = 2 * j + p
                    dve.wait_ge(sg_ok, m + 1), dve.wait_ge(u_ps, m + 1)
                    if m >= 2:
                        dve.wait_ge(mt_hi, m - 1), dve.wait_ge(mt_lo, m - 1)
                    V.tensor_tensor(staged[:, m % 2, :], sg[:, m % 2, :], B[2 + m % 2][:], ALU.mult)\
                        .then_inc(mt_ok, 1)
                for p in range(2):
                    m = 2 * j + p
                    dve.wait_ge(mt_hi, m + 1)
                    low_of(QRl[:, 2 * m:2 * m + 2, :], staged[:, m % 2, :].rearrange("p (a m) -> p a m", a=2),
                           QRh[:, 2 * m:2 * m + 2, :], mt_lo)
            dve.wait_ge(down_ps, 4)
            for t in range(NS):
                ins = V.tensor_tensor(ao[:, t, :], B[6 + t][:], ao[:, t, :], ALU.add)
            ch.link(ins)
            for t in range(NS):
                V.tensor_scalar(hs[:, t, :], ao[:, t, :], gate[:, t:t + 1], None, ALU.mult).then_inc(delta_ok, 1)

        @block.gpsimd
        def _(pool):
            Q.iota(lag, pattern=[[1, P]], base=0, channel_multiplier=-1, allow_small_or_imprecise_dtypes=True)\
                .then_inc(iota_ok, 1)
            Q.iota(ahead, pattern=[[1, P]], base=1, channel_multiplier=0, allow_small_or_imprecise_dtypes=True)\
                .then_inc(iota_ok, 1)
            Q.iota(age, pattern=[[0, 1]], base=1 - P, channel_multiplier=1, allow_small_or_imprecise_dtypes=True)\
                .then_inc(iota_ok, 1)
            Q.memset(ident[:], 0.0).then_inc(pool_chain, 1)
            Q.memset(tri[:], 1.0).then_inc(pool_chain, 1)
            Q.memset(below[:], 1.0).then_inc(pool_chain, 1)
            Q.memset(above[:], 1.0).then_inc(pool_chain, 1)
            Q.memset(ones_sq[:], 1.0)
            pool.wait_ge(pool_chain, 4)
            Q.affine_select(out=ident[:], in_=ident[:], compare_op=ALU.not_equal, fill=1.0, base=0,
                            pattern=[[-1, P]], channel_multiplier=1).then_inc(masks_ok, 1)
            Q.affine_select(out=tri[:], in_=tri[:], compare_op=ALU.is_ge, fill=0.0, base=0,
                            pattern=[[1, P]], channel_multiplier=-1).then_inc(masks_ok, 1)
            Q.affine_select(out=below[:], in_=below[:], compare_op=ALU.is_gt, fill=0.0, base=0,
                            pattern=[[-1, P]], channel_multiplier=1).then_inc(masks_ok, 1)
            Q.affine_select(out=above[:], in_=above[:], compare_op=ALU.is_gt, fill=0.0, base=0,
                            pattern=[[1, P]], channel_multiplier=-1)
            Q.iota(slots[:], pattern=[[1, SEL]], base=0, channel_multiplier=0, allow_small_or_imprecise_dtypes=True)
            Q.iota(tok2[:, :, 0], pattern=[[0, N_TILES]], base=0, channel_multiplier=1,
                   allow_small_or_imprecise_dtypes=True)
            Q.iota(tok2[:, :, 1], pattern=[[1, N_TILES]], base=0, channel_multiplier=0,
                   allow_small_or_imprecise_dtypes=True).then_inc(tok_ok, 1)

            def base(M):
                pool.wait_ge(xn_ok, M + 1)
                pool.wait_ge(final_ok, max(M - NBASE + 1, 0))
                Q.tensor_tensor(BASE[:, M % NBASE, :], X[:, M % NX, :], XN[:, M % NX, :], ALU.add)\
                    .then_inc(base_ok, 1)

            def weights_lo(n):
                pool.wait_ge(w_hi, n + 1)
                Q.tensor_tensor(Wl[:, :, n * DM:(n + 1) * DM], raw_qkvu[n], Wh[:, :, n * DM:(n + 1) * DM].bitcast(f32),
                                ALU.subtract).then_inc(w_lo_pool, 1)

            def q_low(N):
                pool.wait_ge(q_hi, N + 1)
                Q.tensor_tensor(ql[:], QT[:, N // CH % 2, :, N % CH * P:(N % CH + 1) * P], qh[:].bitcast(f32),
                                ALU.subtract).then_inc(q_lo, 1)

            def q_decayed(N):
                pool.wait_ge(inter_ps, N), pool.wait_ge(decays_ok, 1), pool.wait_ge(proj_sb, NPROJ * (N // CH) + 4)
                Q.tensor_tensor(qdec[:], QT[:, N // CH % 2, :, N % CH * P:(N % CH + 1) * P], QD[:], ALU.mult)\
                    .then_inc(q_dec, 1)

            def state_decayed(N):
                pool.wait_ge(state_ok, N), pool.wait_ge(bm_ok, 1)
                Q.tensor_tensor(state_dec[:], state[:], bdec.unsqueeze(2).to_broadcast([P, NK, P]), ALU.mult)\
                    .then_inc(state_dk, 1)

            def uo_low(N):
                pool.wait_ge(uo_hi, N + 1), pool.wait_ge(out_ps, N)
                Q.tensor_tensor(uol[:], uo[:], uoh[:].bitcast(f32), ALU.subtract).then_inc(uo_lo, 1)

            def gather():
                pool.wait_ge(idx_ok, 1)
                for t in range(NS):
                    for dst, src in ((xs[:, t, :], x), (tab[:, t * 2 * FD:(t + 1) * 2 * FD], rope)):
                        Q.indirect_dma_start(out=dst, out_offset=None, in_=src,
                                             in_offset=bass.IndirectOffsetOnAxis(ap=idx[:, t:t + 1], axis=0))\
                            .then_inc(picked, 16)

            def block_lo(b):
                pool.wait_ge(fw_hi, b + 1)
                pool.wait_ge(*last_use(b - 3))
                Q.tensor_tensor(wlo[b % 3][:], raw[b % 2][:], whi[b % 3][:].bitcast(f32), ALU.subtract)\
                    .then_inc(fw_lo, 1)

            base(0)
            base(1)
            for N in slots_of_chunks:
                if N == -2:
                    weights_lo(2)
                    weights_lo(3)
                if N >= 1:
                    uo_low(N - 1)
                if -1 <= N < N_TILES - 1:
                    if N == -1:
                        q_low(N + 1)
                    q_decayed(N + 1)
                    if N >= 0:
                        q_low(N + 1)
                    state_decayed(N + 1)
                if N + XT_AHEAD < N_TILES:
                    base(N + XT_AHEAD)
                if N == N_TILES - 2:
                    block_lo(0)
                    block_lo(1)
            uo_low(N_TILES - 1)
            gather()

            Q.memset(causal[:], 0.0).then_inc(causal_ok, 1)
            pool.wait_ge(causal_ok, 1)
            for blk in (0, 2):
                Q.affine_select(out=causal[:, blk * P:(blk + 1) * P], in_=causal[:, blk * P:(blk + 1) * P],
                                compare_op=ALU.is_ge, fill=-1.0e38, base=0, pattern=[[-1, P]], channel_multiplier=1)\
                    .then_inc(causal_ok, 1)
            for b in range(2, len(order)):
                block_lo(b)
            for t in range(NS):
                pool.wait_ge(delta_ok, t + 1)
                Q.indirect_dma_start(out=out, out_offset=bass.IndirectOffsetOnAxis(ap=idx[:, t:t + 1], axis=0),
                                     in_=hs[:, t, :], in_offset=None, compute_op=ALU.add).then_inc(scattered, 16)
            pool.wait_ge(scattered, 16 * NS)

        @block.tensor
        def _(pe):
            def split_matmuls(dst, lhs, rhs, first, last):
                (lh, ll), (rh, rl) = lhs, rhs
                T.matmul(dst, lh, rh, start=first, stop=False)
                T.matmul(dst, lh, rl, start=False, stop=False)
                return T.matmul(dst, ll, rh, start=False, stop=last)

            def transposed(M):
                pe.wait_ge(xn_ok, M + 1), pe.wait_ge(masks_ok, 1)
                pe.wait_ge(xt_lo, M), pe.wait_ge(k_dec, max(M - XT_AHEAD + 1, 0))
                for k in range(NK):
                    ins = T.transpose(B[5][:, k * P:(k + 1) * P], XN[:, M % NX, k * P:(k + 1) * P], ident[:])
                ins.then_inc(xt_ps, 1)

            def nothing(step):
                pass

            def project(tile, beside=nothing):
                g, i = tile // NPROJ, tile % NPROJ
                name, j = "KQVU"[i // 2], i % 2
                lo = {"Q": 0, "K": DM, "V": 2 * DM, "U": 3 * DM}[name]
                if i == 0:
                    pe.wait_ge(xt_lo, CH * (g + 1))
                if g == 0 and j == 0:
                    if name in "KQ":
                        pe.wait_ge(w_lo, 1 + i // 2)
                    else:
                        pe.wait_ge(w_lo_pool, i // 2 - 1)
                if tile >= 2:
                    pe.wait_ge(proj_sb, tile - 1)
                bank = B[2 + tile % 2]
                steps = 3 * NK
                for step in range(steps):
                    if name == "V":
                        k, n = step // 3, step % 3
                        xt, w = ((xTh, Wh), (xTh, Wl), (xTl, Wh))[n]
                        ins = T.matmul(bank[:], xt[:, g % 2, k, j * P:(j + 1) * P], w[:, k, lo:lo + DM],
                                       start=step == 0, stop=step == steps - 1)
                    else:
                        for m in (2 * step, 2 * step + 1):
                            half, k, n = m // steps, m % steps // 3, m % 3
                            cols = slice(lo + (2 * j + half) * P, lo + (2 * j + half + 1) * P)
                            w, xt = ((Wh, xTh), (Wh, xTl), (Wl, xTh))[n]
                            ins = T.matmul(bank[:, half * GROUP:(half + 1) * GROUP], w[:, k, cols], xt[:, g % 2, k, :],
                                           start=m % steps == 0, stop=m % steps == steps - 1)
                    if step == steps - 1:
                        ins.then_inc(proj_ps, 1)
                    beside(step)

            def score(N, half, step):
                if step == 0:
                    if half == 0:
                        pe.wait_ge(k_hi, N + 1), pe.wait_ge(q_hi, N + 1)
                        pe.wait_ge(k_lo, N + 1), pe.wait_ge(q_lo, N + 1)
                    pe.wait_ge(masked, 4 * N + 2 * half)
                j, n = step // 3, step % 3
                ka, qa = ((kh, qh), (kh, ql), (kl, qh))[n]
                for b in range(2):
                    r = 2 * half + b
                    rows = slice(DH * r, DH * r + DH)
                    ins = T.matmul(B[b][:, j * P:(j + 1) * P], ka[rows, j, :], qa[rows, j, :], start=n == 0,
                                   stop=n == 2)
                if step == 3 * NK - 1:
                    ins.then_inc(s_ps, 1)

            def rms(N, step):
                if step == 2:
                    pe.wait_ge(sq_ok, N + 1), pe.wait_ge(final_ok, N), pe.wait_ge(consts, 1)
                if step % 3 == 2:
                    k = step // 3
                    ins = T.matmul(B[7][:, 0:1], sq[:, k, :], ones1, start=k == 0, stop=k == NK - 1)
                    if k == NK - 1:
                        ins.then_inc(rms_ps, 1)

            def score_and_rms(N, step):
                if N < N_TILES:
                    score(N, 0, step)
                if N >= 1:
                    rms(N - 1, step)

            def project_out(N):
                pe.wait_ge(uo_hi, N + 1), pe.wait_ge(uo_lo, N + 1), pe.wait_ge(sd_o_ok, N + 1), pe.wait_ge(w_lo, 3)
                for k in range(NK):
                    ins = split_matmuls(B[7][:], (uoh[:, k, :], uol[:, k, :]), (Woh[:, k, :], Wol[:, k, :]),
                                        k == 0, k == NK - 1)
                ins.then_inc(out_ps, 1)

            def inside(N, step):
                if step == 2:
                    pe.wait_ge(masked, 4 * N + 4)
                if step % 3 == 2:
                    j = step // 3
                    for r in range(4):
                        h = 4 * j + r
                        ins = T.matmul(B[4][DH * r:DH * r + DH, j * P:(j + 1) * P],
                                       VT[:, N // CH % 2, N % CH, DH * h:DH * h + DH], A[:, h, :], start=False,
                                       stop=True, skip_group_check=True)
                    if j == NK - 1:
                        ins.then_inc(pv_ps, 1)

            transposed(0)
            transposed(1)
            for N in slots_of_chunks:
                tiles = proj_tiles(N)
                if N < 0:
                    project(tiles[0])
                    project(tiles[1])
                    transposed(N + XT_AHEAD)
                    project(tiles[2])
                    project(tiles[3])
                    continue
                buf = N // CH % 2
                if tiles:
                    project(tiles[0], lambda step: score_and_rms(N, step))
                else:
                    for step in range(3 * NK):
                        score_and_rms(N, step)
                pe.wait_ge(xt_lo, min(N + XT_AHEAD, N_TILES))
                for k in range(NK):
                    ins = T.transpose(B[5][:, k * P:(k + 1) * P], KT[:, buf, k, N % CH * P:(N % CH + 1) * P], ident[:])
                ins.then_inc(kt_ps, 1)
                pe.wait_ge(q_dec, N + 1), pe.wait_ge(state_ok, N), pe.wait_ge(bm_ok, 1)
                pe.wait_ge(uo_ok, N), pe.wait_ge(sq_ok, N)
                for j in range(NK):
                    ins = T.matmul(B[4][:, j * P:(j + 1) * P], state[:, j, :], qdec[:, j, :], start=j == 0,
                                   stop=False, skip_group_check=True)
                ins.then_inc(inter_ps, 1)
                if tiles:
                    project(tiles[1], lambda step: score(N, 1, step))
                else:
                    for step in range(3 * NK):
                        score(N, 1, step)
                if N >= 1:
                    project_out(N - 1)
                pe.wait_ge(k_dec, N + 1), pe.wait_ge(proj_sb, NPROJ * (N // CH) + 6)
                for j in range(NK):
                    cols = slice(j * P, (j + 1) * P)
                    ins = T.matmul(B[6][:, cols], kdec[:, cols], VT[:, buf, N % CH, cols], start=True, stop=True)
                ins.then_inc(kv_ps, 1)
                if N + XT_AHEAD < N_TILES:
                    transposed(N + XT_AHEAD)
                if N == N_TILES - 1:
                    pe.wait_ge(rank_ok, 1), pe.wait_ge(tok_ok, 1)
                    T.matmul(B[5][:, 0:N_TILES], above[:], chosen_b[:], start=True, stop=True)
                    T.matmul(B[5][:, N_TILES:2 * N_TILES], ones_sq[:], chosen_b[:], start=True, stop=True)\
                        .then_inc(cnt_ps, 1)
                if tiles:
                    project(tiles[2], lambda step: inside(N, step))
                    project(tiles[3])
                else:
                    for step in range(3 * NK):
                        inside(N, step)
            pe.wait_ge(oh_ok, 1)
            for t in range(NS):
                for n in range(N_TILES):
                    ins = T.matmul(B[5][:, 2 * t:2 * t + 2], one_hot[:, n, t * P:(t + 1) * P], tok2[:, n, :],
                                   start=n == 0, stop=n == N_TILES - 1)
            ins.then_inc(idx_ps, 1)
            for step in range(3 * NK):
                score_and_rms(N_TILES, step)
            project_out(N_TILES - 1)

            def block_ready(b):
                pe.wait_ge(fw_hi, b + 1), pe.wait_ge(fw_lo, b + 1)

            def hidden_transposed(n):
                pe.wait_ge(hs_ok, n + 1)
                pe.wait_ge(masked, 4 * N_TILES)
                if n == 0:
                    pe.wait_ge(final_ok, N_TILES)
                for k in range(NK):
                    for t in range(NS):
                        at = (k % 2) * SEL + t * P
                        ins = T.transpose(B[k // 2][:, at:at + P], hs[:, t, k * P:(k + 1) * P], ident[:])
                ins.then_inc(ht_ps, 1)

            def pair(bank, b, p):
                for i in range(2):
                    cols = slice((2 * p + i) * P, (2 * p + i + 1) * P)
                    for k in range(NK):
                        ins = split_matmuls(bank[:, i * SEL:(i + 1) * SEL], (whi[b % 3][:, k, cols], wlo[b % 3][:, k, cols]),
                                            (HTh[:, k, :], HTl[:, k, :]), k == 0, k == NK - 1)
                return ins

            def unit(u):
                k, p = units[u]
                b = block_of[k]
                block_ready(b)
                if u >= 2:
                    if units[u - 2][0][0] == "V":
                        pe.wait_ge(staged_ok, u - 1)
                    else:
                        pe.wait_ge(unit_b, kq_count(u - 2))
                if k[0] == "V":
                    for n in range(NK):
                        rows = slice(p * P, (p + 1) * P)
                        ins = split_matmuls(B[u % 2][:], (HTh[:, n, rows], HTl[:, n, rows]),
                                            (whi[b % 3][:, n, :], wlo[b % 3][:, n, :]), n == 0, n == NK - 1)
                else:
                    ins = pair(B[u % 2], b, p)
                ins.then_inc(unit_ps, 1)

            pe.wait_ge(picked, 16 * 2 * NS), pe.wait_ge(masked, 4 * N_TILES)
            for half in range(2):
                for t in range(NS):
                    at = half * SEL + t * P
                    ins = T.transpose(B[2][:, at:at + P], tab[:, t * 2 * FD + half * P:t * 2 * FD + (half + 1) * P],
                                      ident[:])
            ins.then_inc(tab_ps, 1)
            hidden_transposed(0)
            pe.wait_ge(ht_hi, 1), pe.wait_ge(ht_lo, 1)
            for u in range(before_heads):
                unit(u)
            for h in range(STEPS):
                if h < FH:
                    kv = h // (FH // FKV)
                    pe.wait_ge(unit_lo, kq_unit(h)), pe.wait_ge(cs_ok, 1)
                    if h >= 2:
                        pe.wait_ge(sm_ok, h - 1)
                    for rows, width, at in ((slice(0, P), P, 0), (slice(P, SEL), SEL, P)):
                        ins = split_matmuls(B[2 + h % 2][:, at:at + width], (QRh[:, h, rows], QRl[:, h, rows]),
                                            (KRh[:, kv, 0:width], KRl[:, kv, 0:width]), True, True)
                    ins.then_inc(sc_ps, 1)
                if 1 <= h <= FH:
                    pe.wait_ge(pn_ok, h), pe.wait_ge(pt_lo, h - 1)
                    for n in range(3):
                        ins = T.transpose(B[4][:, n * P:(n + 1) * P], PN[:, (h - 1) % 2, n * P:(n + 1) * P], ident[:])
                    ins.then_inc(pt_ps, 1)
                if 2 <= h <= FH + 1:
                    g = h - 2
                    kv = g // (FH // FKV)
                    cols = slice(kv * FD, (kv + 1) * FD)
                    pe.wait_ge(pt_lo, g + 1), pe.wait_ge(ot_lo, g)
                    split_matmuls(B[5][:, 0:SEL], (Vh[:, 0, cols], Vl[:, 0, cols]),
                                  (PTh[:, g % 2, 0:SEL], PTl[:, g % 2, 0:SEL]), True, False)
                    split_matmuls(B[5][:, P:SEL], (Vh[:, 1, cols], Vl[:, 1, cols]),
                                  (PTh[:, g % 2, SEL:], PTl[:, g % 2, SEL:]), False, True).then_inc(ot_ps, 1)
                u = unit_of_step(h)
                if u is not None:
                    unit(u)
                if h >= 3:
                    g = h - 3
                    b = block_of[f"O{g // 4}"]
                    if g % 4 == 0:
                        block_ready(b)
                    pe.wait_ge(ot_lo, g + 1)
                    for t in range(NS):
                        rows = slice(t * P, (t + 1) * P)
                        ins = split_matmuls(B[6 + t][:], (OTh[:, g % 2, rows], OTl[:, g % 2, rows]),
                                            (whi[b % 3][:, g % 4, :], wlo[b % 3][:, g % 4, :]), g == 0, g == FH - 1)
                    ins.then_inc(wo_ps, 1)
            hidden_transposed(1)
            pe.wait_ge(ht_hi, 2), pe.wait_ge(ht_lo, 2)

            def gate_up(j):
                for k, done, first in (("G", g_ps, 0), ("U", u_ps, 2)):
                    b = block_of[f"{k}{j}"]
                    block_ready(b)
                    for p in range(2):
                        m = 2 * j + p
                        if m >= 2:
                            pe.wait_ge(sg_ok if k == "G" else mt_ok, m - 1)
                        ins = pair(B[first + m % 2], b, p)
                        ins.then_inc(done, 1)

            def down(j):
                b = block_of[f"D{j}"]
                block_ready(b)
                pe.wait_ge(mt_hi, 2 * j + 2), pe.wait_ge(mt_lo, 2 * j + 2)
                if j == 0:
                    pe.wait_ge(hs_ok, 2)
                for i in range(4):
                    for t in range(NS):
                        rows = slice(t * P, (t + 1) * P)
                        ins = split_matmuls(B[6 + t][:], (QRh[:, 4 * j + i, rows], QRl[:, 4 * j + i, rows]),
                                            (whi[b % 3][:, i, :], wlo[b % 3][:, i, :]), j == 0 and i == 0,
                                            j == 3 and i == 3)
                ins.then_inc(down_ps, 1)

            for k in order[block_of["G0"]:]:
                if k[0] == "G":
                    gate_up(int(k[1]))
                elif k[0] == "D":
                    down(int(k[1]))


_NAMES = ("w_router", "wq", "bq", "wk", "bk", "wv", "bv", "wo", "w_gate", "w_up", "w_down")


def kernel(**inputs):
    import numpy as np
    import concourse.bacc as bacc
    from concourse.bass_utils import run_bass_kernel_spmd as run

    W = {k: np.asarray(v) for k, v in inputs.items()}
    slopes = W["L0_attn_slope_rate"].reshape(NH)
    per_feature = np.repeat(slopes, DH)
    tile_major = lambda a, n: a.reshape(n, P).T
    freq = (np.float32(1.0) / np.float32(10000.0) ** (np.arange(0, FD, 2, dtype=np.float32) / np.float32(FD)))
    angle = np.arange(N_TOK, dtype=np.float32)[:, None] * freq.astype(np.float32)
    cos, sin = np.cos(angle.astype(np.float64)), np.sin(angle.astype(np.float64))
    rope = np.concatenate([cos, cos, sin, -sin], axis=1).astype(np.float32)
    data = {
        "x": W["L0_attn_x"].reshape(N_TOK, DM), "WT": W["L0_attn_W_qkvu"].T, "WoT": W["L0_attn_W_out"].T,
        "s_hid": tile_major(per_feature, NK), "s_row": per_feature, "s_head": slopes,
        **{n: W["L0_ffn_" + n] for n in _NAMES},
        "ln1": tile_major(W["L0_ffn_ln1_w"], NK), "ln2": tile_major(W["L0_ffn_ln2_w"], NK), "rope": rope,
    }
    data["bq"], data["bk"] = tile_major(data["bq"], FH), tile_major(data["bk"], FKV)
    data = {"in_" + k: np.ascontiguousarray(v) for k, v in data.items()}
    nc = bacc.Bacc("TRN2", target_bir_lowering=False, num_devices=1)
    args = {n[3:]: nc.dram_tensor(n, a.shape, mybir.dt.from_np(a.dtype), kind="ExternalInput").ap()
            for n, a in data.items()}
    scores = nc.dram_tensor("scores", [N_TOK], mybir.dt.float32).ap()
    out = nc.dram_tensor("out", [N_TOK, DM], mybir.dt.float32, kind="ExternalOutput").ap()
    build(nc, scores=scores, out=out, **args)
    r = run(nc, [data], core_ids=[0])
    return r.results[0]["out"].reshape(1, N_TOK, DM)
```

```python
import concourse.bass as bass
from concourse import mybir
from contextlib import ExitStack

P = 128
N_TOK, DM = 2048, 512
NH, DH = 16, 32
NK = DM // P
GROUP = 256
G = N_TOK // GROUP
CH = GROUP // P
N_TILES = N_TOK // P
SEL = N_TOK // 8
NS = SEL // P
FH, FKV, FD = 16, 8, 128
FF = 2048
NPROJ = 8
PER_SLOT = NPROJ // CH
XT_AHEAD = 4
LN_AHEAD = 5
NX = 3
NBASE = 6


def build(nc, x, WT, WoT, s_hid, s_row, s_head, w_router, wq, bq, wk, bk, wv, bv, wo, w_gate, w_up,
          w_down, ln1, ln2, rope, scores, out):
    f32, f32r, bf16, i32 = mybir.dt.float32, mybir.dt.float32r, mybir.dt.bfloat16, mybir.dt.int32
    ALU, ACT = mybir.AluOpType, mybir.ActivationFunctionType
    V, S, T, Q = nc.vector, nc.scalar, nc.tensor, nc.gpsimd

    x_t = x.rearrange("(n p) d -> n p d", p=P)
    out_t = out.rearrange("(n p) d -> n p d", p=P)
    WT_v = WT.rearrange("(k p) n -> p k n", p=P)
    WoT_v = WoT.rearrange("(k p) n -> p k n", p=P)
    scores_t = scores.rearrange("(n p) -> p n", p=P)

    ctx = ExitStack()
    with ctx:
        def sb(name, shape, dt=f32, c=ctx):
            return c.enter_context(nc.sbuf_tensor(name, shape, dt))

        ident = sb("ident", [P, P])
        tri = sb("tri", [P, P], bf16)
        below = sb("below", [P, P], bf16)
        above = sb("above", [P, P], bf16)
        ones_sq = sb("ones_sq", [P, P], bf16)
        XX = sb("XX", [P, 2 * NX, DM])
        small = sb("small", [P, 200])
        taken = [0]

        def col(n):
            taken[0] += n
            assert taken[0] <= 200
            return small[:, taken[0] - n:taken[0]]

        rstd, sd_ln = col(NX), col(NX)
        shid, nshid, bdec = col(NK), col(NK), col(NK)
        shead, nshead = col(NH), col(NH)
        age, eps_ln, eps_rms, ones1, sd_o, r_o = (col(1) for _ in range(6))
        score_all, n_ge, n_gt, n_eq, rank, chosen, place, before = (col(N_TILES) for _ in range(8))
        stats = sb("stats", [P, NX, 6])
        mv = sb("mv", [P, NX, 2])
        chosen_b = sb("chosen_b", [P, N_TILES], bf16)
        tok2 = sb("tok2", [P, N_TILES, 2], bf16)
        idx_f = sb("idx_f", [P, 2 * NS])
        idx = sb("idx", [P, NS], i32)
        wr_b = sb("wr_b", [P, DM])
        fsmall = sb("fsmall", [P, 48])

        slots = sb("slots", [P, SEL], bf16)

        ca = ExitStack()
        Wh, Wl = (sb(n, [P, NK, 4 * DM], f32r, ca) for n in ("Wh", "Wl"))
        Woh, Wol = (sb(n, [P, NK, DM], f32r, ca) for n in ("Woh", "Wol"))
        xTh, xTl = (sb(n, [P, 2, NK, GROUP], f32r, ca) for n in ("xTh", "xTl"))
        KT, QT, UT = (sb(n, [P, 2, NK, GROUP], f32, ca) for n in ("KT", "QT", "UT"))
        VT = sb("VT", [P, 2, CH, DM], f32, ca)
        BASE = sb("BASE", [P, NBASE, DM], f32, ca)
        kh, kl = (sb(n, [P, NK, P], f32r, ca) for n in ("kh", "kl"))
        QBh, QBl = (sb(n, [P, 2, 4, P], f32r, ca) for n in ("QBh", "QBl"))
        qdec, uo, sq = (sb(n, [P, NK, P], f32, ca) for n in ("qdec", "uo", "sq"))
        uoh, uol = (sb(n, [P, NK, P], f32r, ca) for n in ("uoh", "uol"))
        kdec = sb("kdec", [P, DM], f32, ca)
        DEC = sb("DEC", [P, NH, P], f32, ca)
        QD = sb("QD", [P, NK, P], f32, ca)
        KD = sb("KD", [P, DM], f32, ca)
        A = sb("A", [P, NH, P], f32, ca)
        state, state_dec, kv_new = (sb(n, [P, NK, P], f32, ca) for n in ("state", "state_dec", "kv_new"))
        BM = sb("BM", [P, P], f32, ca)
        ca.close()
        raw_qkvu = [m[:].rearrange("p b k m -> p (b k m)").rearrange("p (k n) -> p k n", k=NK)
                    for m in (KT, QT, VT, UT)]
        raw_wo = A[:].rearrange("p (k h) m -> p k (h m)", k=NK)
        X, XN = XX[:, 0:NX, :], XX[:, NX:, :]
        s_bc = XX[:, 0:4, :].rearrange("p c d -> p (c d)")
        seen = XX[:, 4:6, :].rearrange("p c d -> p (c d)").bitcast(bf16)
        one_hot = s_bc.bitcast(bf16).rearrange("p (n s) -> p n s", n=N_TILES)
        lag = BASE[:, NBASE - 1, 0:P]
        ahead = BASE[:, NBASE - 1, P:2 * P]

        cb = ExitStack()
        raw = [sb(f"raw{i}", [P, 4, DM], f32, cb) for i in range(2)]
        whi = [sb(f"whi{i}", [P, 4, DM], f32r, cb) for i in range(3)]
        wlo = [sb(f"wlo{i}", [P, 4, DM], f32r, cb) for i in range(3)]
        QRh = sb("QRh", [P, FH, SEL], f32r, cb)
        tab = sb("tab", [P, NS * 2 * FD], f32, cb)
        CS = sb("CS", [P, 2, SEL], f32, cb)
        bvb = sb("bvb", [P, FKV * FD], f32, cb)
        bqk = sb("bqk", [P, FKV + FH], f32, cb)
        ln12 = sb("ln12", [P, 2, NK], f32, cb)
        causal = sb("causal", [P, 3 * P], f32, cb)
        QRl = sb("QRl", [P, FH, SEL], f32r, cb)
        KRh, KRl = (sb(n, [P, FKV, SEL], f32r, cb) for n in ("KRh", "KRl"))
        Vh, Vl = (sb(n, [P, NS, FKV * FD], f32r, cb) for n in ("Vh", "Vl"))
        HTh, HTl = (sb(n, [P, NK, SEL], f32r, cb) for n in ("HTh", "HTl"))
        ao = sb("ao", [P, NS, DM], f32, cb)
        qb = sb("qb", [P, 2, 2, SEL], f32, cb)
        rope1, rope2 = (sb(n, [P, 2, SEL], f32, cb) for n in ("rope1", "rope2"))
        staged = sb("staged", [P, 2, 2 * SEL], f32, cb)
        SM, PR = (sb(n, [P, 3 * P], f32, cb) for n in ("SM", "PR"))
        PN = sb("PN", [P, 2, 3 * P], f32, cb)
        PTh, PTl = (sb(n, [P, 2, 3 * P], f32r, cb) for n in ("PTh", "PTl"))
        OTh, OTl = (sb(n, [P, 2, SEL], f32r, cb) for n in ("OTh", "OTl"))
        sg = sb("sg", [P, 2, 2 * SEL], f32, cb)
        cb.close()
        hs, xsn, xs = XX[:, 0:NS, :], XX[:, NS:2 * NS, :], XX[:, 2 * NS:, :]
        top, ntop, psum_, pinv = (fsmall[:, 4 * n:4 * n + 4].rearrange("p (a b) -> p a b", a=2) for n in range(4))
        sel_score, gate, sumsq, sd_s, r_s = (fsmall[:, 16 + 2 * n:18 + 2 * n] for n in range(5))
        scrap = staged[:, 0, :]

        def wide(w):
            return lambda i: w.rearrange("(k p) n -> p k n", p=P)[:, :, i * DM:(i + 1) * DM]

        def tall(w):
            return lambda i: w.rearrange("(h p) n -> p h n", p=P)[:, 4 * i:4 * i + 4, :]

        source = {"K": wide(wk), "V": wide(wv), "Q": wide(wq), "O": tall(wo), "G": wide(w_gate), "U": wide(w_up),
                  "D": tall(w_down)}
        order = ["K0", "K1", "Q0", "V0", "V1", "Q1", "O0", "Q2", "O1", "Q3", "O2", "O3",
                 "G0", "U0", "G1", "U1", "D0", "G2", "U2", "D1", "G3", "U3", "D2", "D3"]
        block_of = {k: n for n, k in enumerate(order)}
        units = [(k, p) for k in ("K0", "K1", "Q0", "V0", "V1", "Q1", "Q2", "Q3") for p in range(2)]
        before_heads = 8
        STEPS = FH + 3

        units_of_step = {0: (8, 9), 1: (10,), 2: (11,), 4: (12,), 6: (13,), 9: (14,), 11: (15,)}

        def kq_unit(h):
            return 9 + h // 2 if h >= 4 else 6

        def kq_count(u):
            return sum(units[n][0][0] != "V" for n in range(u + 1))

        rank_in = {(N_TILES - 4, 0): (0, 3), (N_TILES - 4, 1): (3, 6), (N_TILES - 3, 0): (6, 9),
                   (N_TILES - 3, 1): (9, 12), (N_TILES - 2, 0): (12, 14), (N_TILES - 2, 1): (14, N_TILES)}
        split_after = {0: "Q2", 2: "O1", 6: "Q3", 7: "O2", 10: "O3", 12: "G0", 15: "U0"}

        B = [ctx.enter_context(nc.psum_tensor(f"bank{i}", [P, 512], f32)) for i in range(8)]

        def xt_bank(M):
            return B[6] if M == 1 else B[5]

        def tiles4(ap):
            return ap.rearrange("p (k m) -> p k m", k=4)

        def sems(names):
            return [ctx.enter_context(nc.semaphore(n)) for n in names.split()]

        class Chain:

            def __init__(self, eng, done):
                self.eng, self.done, self.n = eng, done, 0

            def link(self, ins):
                self.n += 1
                ins.then_inc(self.done, 1)
                self.eng.wait_ge(self.done, self.n)

        x_in = sems("x_in_0 x_in_1 x_in_2")
        const_in, sbc_in, score_out = sems("const_in sbc_in score_out")
        w_raw = sems("w_raw_k w_raw_q w_raw_v w_raw_u w_raw_o")
        stored = sems("stored_even stored_odd")
        raw_in = sems("raw_in_even raw_in_odd")
        part_in, picked, scattered = sems("part_in picked scattered")
        consts, slopes_ok, iota_ok, masks_ok, tok_ok, lag_ok = sems("consts slopes_ok iota_ok masks_ok tok_ok lag_ok")
        decays_ok, dec_ok, bm_ok, causal_ok = sems("decays_ok dec_ok bm_ok causal_ok")
        w_hi, w_lo, w_lo_pool = sems("w_hi w_lo w_lo_pool")
        var_ok, sd_ln_ok, xn_ok, score_ok, base_ok = sems("var_ok sd_ln_ok xn_ok score_ok base_ok")
        xt_ps, xt_hi, xt_lo, proj_ps, proj_sb = sems("xt_ps xt_hi xt_lo proj_ps proj_sb")
        k_hi, q_hi, k_lo, q_lo, q_dec, kt_ps, k_dec = sems("k_hi q_hi k_lo q_lo q_dec kt_ps k_dec")
        s_ps, masked, inter_ps, kv_ps, kv_masked, pv_ps = sems("s_ps masked inter_ps kv_ps kv_masked pv_ps")
        state_dk, state_ok, uo_ok, sq_ok, uo_hi, uo_lo = sems("state_dk state_ok uo_ok sq_ok uo_hi uo_lo")
        rms_ps, sd_o_ok, out_ps, final_ok = sems("rms_ps sd_o_ok out_ps final_ok")
        rank_ok, cnt_ps, oh_ok, idx_ps, idx_ok = sems("rank_ok cnt_ps oh_ok idx_ps idx_ok")
        dve_chain, pool_chain = sems("dve_chain pool_chain")
        fw_hi, fw_lo = sems("fw_hi fw_lo")
        var_s_ok, sd_s_ok, hs_ok, ht_ps, tab_ps = sems("var_s_ok sd_s_ok hs_ok ht_ps tab_ps")
        cs_ok, ht_hi, ht_lo = sems("cs_ok ht_hi ht_lo")
        unit_ps, unit_b, staged_ok, unit_hi, unit_lo = sems("unit_ps unit_b staged_ok unit_hi unit_lo")
        sc_ps, sm_ok, exp_ok, pn_ok, pt_ps, pt_hi, pt_lo = sems("sc_ps sm_ok exp_ok pn_ok pt_ps pt_hi pt_lo")
        ot_ps, ot_hi, ot_lo, wo_ps, gate_ok = sems("ot_ps ot_hi ot_lo wo_ps gate_ok")
        g_ps, u_ps, sg_ok, mt_ok, mt_hi, mt_lo = sems("g_ps u_ps sg_ok mt_ok mt_hi mt_lo")
        down_ps, delta_ok = sems("down_ps delta_ok")

        def last_use(b):
            if b < 0:
                return unit_ps, 0
            k, i = order[b][0], int(order[b][1])
            if k in "KVQ":
                return unit_ps, [u for u, (name, _) in enumerate(units) if name == order[b]][-1] + 1
            return {"O": (wo_ps, 4 * i + 4), "G": (g_ps, 2 * i + 2), "U": (u_ps, 2 * i + 2),
                    "D": (down_ps, i + 1)}[k]

        def proj_tiles(N):
            group = N // CH + 1
            return [NPROJ * group + PER_SLOT * (N % CH) + i for i in range(PER_SLOT)] if group < G else []

        slots_of_chunks = range(-CH, N_TILES)

        block = ctx.enter_context(nc.Block())

        @block.sync
        def _(sp):
            def load_x(M):
                if M >= NX:
                    sp.wait_ge(base_ok, M - NX + 1)
                sp.dma_start(X[:, M % NX, :], x_t[M]).then_inc(x_in[M % NX], 16)

            def load_block(b):
                k = order[b]
                if b >= 2:
                    sp.wait_ge(fw_hi, b - 1), sp.wait_ge(fw_lo, b - 1)
                sp.dma_start(raw[b % 2][:], source[k[0]](int(k[1]))).then_inc(raw_in[b % 2], 16)

            def store(N):
                sp.wait_ge(final_ok, N + 1)
                sp.dma_start(out_t[N], BASE[:, N % NBASE, :]).then_inc(stored[N % 2], 16)

            load_x(0)
            load_x(1)
            for n, q in enumerate((1, 0, 2, 3)):
                sp.dma_start(raw_qkvu[n], WT_v[:, :, q * DM:(q + 1) * DM]).then_inc(w_raw[n], 16)
                if n == 0:
                    load_x(2)
                    for dst, src in ((wr_b[:], w_router.partition_broadcast(P)), (shid, s_hid),
                                     (KD[:], s_row.partition_broadcast(P)), (shead, s_head.partition_broadcast(P))):
                        sp.dma_start(dst, src).then_inc(const_in, 16)
            sp.dma_start(raw_wo, WoT_v).then_inc(w_raw[4], 16)
            load_x(NX), load_x(NX + 1)

            for N in slots_of_chunks:
                M = N + LN_AHEAD
                if N >= 2:
                    store(N - 2)
                if M < N_TILES:
                    if M + 2 < N_TILES and M + 2 > NX + 1:
                        load_x(M + 2)
                    if M % 4 == 3:
                        sp.wait_ge(score_ok, M + 1)
                        sp.dma_start(scores_t[:, M - 3:M + 1], score_all[:, M - 3:M + 1],
                                     allow_slow_non_contiguous=True).then_inc(score_out, 16)
                if N == N_TILES - XT_AHEAD:
                    sp.wait_ge(score_out, 16 * N_TILES // 4)
                    sp.wait_ge(xt_ps, N_TILES), sp.wait_ge(base_ok, N_TILES)
                    sp.dma_start(s_bc, scores.partition_broadcast(P)).then_inc(sbc_in, 16)
                if N == N_TILES - CH:
                    sp.wait_ge(proj_ps, NPROJ * G)
                    load_block(0)
                    load_block(1)
                    sp.dma_start(bqk[:, 0:FKV], bk).then_inc(part_in, 16)
                    sp.dma_start(bqk[:, FKV:], bq).then_inc(part_in, 16)
                    sp.dma_start(ln12[:, 0, :], ln1).then_inc(part_in, 16)
                    sp.dma_start(ln12[:, 1, :], ln2).then_inc(part_in, 16)
                    sp.dma_start(bvb[:], bv.partition_broadcast(P)).then_inc(part_in, 16)
                    load_block(2)
            store(N_TILES - 2)
            load_block(3)
            store(N_TILES - 1)
            for b in range(4, len(order)):
                load_block(b)
            for c in range(2):
                sp.wait_ge(stored[c], 16 * N_TILES // 2)

        @block.scalar
        def _(act):
            def weights_hi(n):
                act.wait_ge(w_raw[n], 16)
                q = (1, 0, 2, 3, 0)[n]
                dst, src = (Wh[:, :, q * DM:(q + 1) * DM], raw_qkvu[n]) if n < 4 else (Woh[:], raw_wo)
                S.activation(dst, src, ACT.Copy).then_inc(w_hi, 1)

            def ln_sd(first, count):
                act.wait_ge(var_ok, first + count), act.wait_ge(consts, 1)
                s = first % NX
                S.activation(sd_ln[:, s:s + count], mv[:, s:s + count, 1], ACT.Sqrt, bias=eps_ln)\
                    .then_inc(sd_ln_ok, count)

            def xt_high(M):
                act.wait_ge(xt_ps, M + 1)
                act.wait_ge(proj_ps, NPROJ * max(M // CH - 1, 0))
                bank = xt_bank(M)
                S.activation(xTh[:, M // CH % 2, :, M % CH * P:(M % CH + 1) * P], tiles4(bank[:]), ACT.Copy)\
                    .then_inc(xt_hi, 1)

            def evacuate(tile):
                g, i = tile // NPROJ, tile % NPROJ
                name, j = "KQVU"[i // 2], i % 2
                act.wait_ge(proj_ps, tile + 1)
                if j == 0:
                    used = CH * max(g - 1, 0)
                    if name == "K":
                        act.wait_ge(w_lo, 1), act.wait_ge(k_lo, used), act.wait_ge(kt_ps, used), act.wait_ge(k_hi, used)
                    if name == "Q":
                        act.wait_ge(w_lo, 2), act.wait_ge(q_lo, 2 * used), act.wait_ge(q_dec, used)
                        act.wait_ge(q_hi, 2 * used)
                    if name == "V":
                        act.wait_ge(w_lo_pool, 1), act.wait_ge(pv_ps, used), act.wait_ge(kv_ps, used)
                    if name == "U":
                        act.wait_ge(w_lo_pool, 2), act.wait_ge(uo_ok, used)
                if name == "V":
                    dst = VT[:, g % 2, j, :]
                else:
                    dst = {"K": KT, "Q": QT, "U": UT}[name][:, g % 2, 2 * j:2 * j + 2, :].rearrange("p k m -> p (k m)")
                S.activation(dst, B[2 + tile % 2][:], ACT.Silu if name in "KQ" else ACT.Copy).then_inc(proj_sb, 1)

            def k_high(N):
                act.wait_ge(proj_sb, NPROJ * (N // CH) + 2)
                act.wait_ge(s_ps, 2 * N), act.wait_ge(k_lo, N)
                cols = slice(N % CH * P, (N % CH + 1) * P)
                S.activation(kh[:], KT[:, N // CH % 2, :, cols], ACT.Copy).then_inc(k_hi, 1)

            def q_high(N, half):
                act.wait_ge(proj_sb, NPROJ * (N // CH) + 4), act.wait_ge(bm_ok, 1)
                act.wait_ge(s_ps, 2 * N + half), act.wait_ge(q_lo, 2 * N + half)
                cols = slice(N % CH * P, (N % CH + 1) * P)
                for r in range(4):
                    rows = slice(DH * r, DH * r + DH)
                    ins = S.activation(QBh[rows, :, r, :], QT[rows, N // CH % 2, 2 * half:2 * half + 2, cols], ACT.Copy)
                ins.then_inc(q_hi, 1)

            def rms_sd(N):
                act.wait_ge(rms_ps, N + 1)
                act.wait_ge(final_ok, N)
                S.activation(sd_o, B[7][:, 0:1], ACT.Sqrt, scale=1.0 / DM, bias=eps_rms).then_inc(sd_o_ok, 1)

            def decay_tables(part):
                act.wait_ge(iota_ok, 3), act.wait_ge(lag_ok, 1), act.wait_ge(slopes_ok, 1)
                for h in range(part * NH // 2, (part + 1) * NH // 2):
                    S.activation(DEC[:, h, :], lag, ACT.Exp, scale=nshead[:, h:h + 1])
                if part:
                    for k in range(NK):
                        S.activation(QD[:, k, :], ahead, ACT.Exp, scale=nshid[:, k:k + 1])
                    S.activation(bdec, shid, ACT.Exp, scale=-float(P))
                    S.activation(KD[:], KD[:], ACT.Exp, scale=age).then_inc(decays_ok, 1)

            def block_hi(b):
                act.wait_ge(raw_in[b % 2], 16 * (b // 2 + 1))
                act.wait_ge(*last_use(b - 3))
                S.activation(whi[b % 3][:], raw[b % 2][:], ACT.Copy).then_inc(fw_hi, 1)

            act.wait_ge(consts, 1)
            S.activation(sd_ln[:, NX - 1:NX], eps_ln, ACT.Sqrt)
            ln_sd(0, CH)
            xt_high(0)
            xt_high(1)
            weights_hi(0)
            ln_sd(CH, 1)
            weights_hi(1)
            for N in slots_of_chunks:
                tiles = proj_tiles(N)
                M = N + LN_AHEAD
                if N >= 0:
                    q_high(N, 1)
                if tiles:
                    evacuate(tiles[0])
                if N == -2:
                    weights_hi(2)
                if N == -1:
                    ln_sd(M, 1)
                    k_high(0)
                    q_high(0, 0)
                    evacuate(tiles[1])
                    xt_high(N + XT_AHEAD)
                    decay_tables(0)
                    evacuate(tiles[2])
                    decay_tables(1)
                if N >= 1:
                    rms_sd(N - 1)
                if M < N_TILES and N != -1:
                    ln_sd(M, 1)
                if tiles and N != -1:
                    evacuate(tiles[1])
                if 0 <= N < N_TILES - 1:
                    k_high(N + 1)
                    q_high(N + 1, 0)
                if N == -2:
                    weights_hi(3)
                if N + XT_AHEAD < N_TILES and N != -1:
                    xt_high(N + XT_AHEAD)
                if tiles and N != -1:
                    evacuate(tiles[2])
                if N == -2:
                    weights_hi(4)
                if N >= N_TILES - CH:
                    block_hi(N - (N_TILES - CH))
                if N >= 0:
                    act.wait_ge(uo_ok, N + 1)
                    act.wait_ge(rms_ps, N)
                    S.activation(sq[:], tiles4(B[4][:]), ACT.Square).then_inc(sq_ok, 1)
                    act.wait_ge(out_ps, N), act.wait_ge(uo_lo, N)
                    S.activation(uoh[:], uo[:], ACT.Copy).then_inc(uo_hi, 1)
                if tiles:
                    evacuate(tiles[3])
            def norm_sd(n, func_input, scale, bias):
                S.activation(sd_s, func_input, ACT.Sqrt, scale=scale, bias=bias).then_inc(sd_s_ok, 1)

            def hidden_high(n):
                act.wait_ge(ht_ps, n + 1), act.wait_ge(part_in, 16 * 5)
                if n:
                    act.wait_ge(unit_ps, len(units))
                else:
                    act.wait_ge(final_ok, N_TILES)
                for k in range(NK):
                    ins = S.activation(HTh[:, k, :], B[k // 2][:, (k % 2) * SEL:(k % 2 + 1) * SEL], ACT.Copy,
                                       scale=ln12[:, n, k:k + 1])
                    if k % 2:
                        ins.then_inc(ht_hi, 1)

            def unit_bias(u):
                k, p = units[u]
                if k[0] == "V":
                    return
                act.wait_ge(unit_ps, u + 1)
                if u >= 2:
                    act.wait_ge(staged_ok, u - 1)
                for i in range(2):
                    head = 4 * int(k[1]) + 2 * p + i + (FKV if k[0] == "Q" else 0)
                    ins = S.activation(qb[:, u % 2, i, :], B[u % 2][:, i * SEL:(i + 1) * SEL], ACT.Identity,
                                       bias=bqk[:, head:head + 1])
                ins.then_inc(unit_b, 1)

            def unit_dst(u, part):
                k, p = units[u]
                i = int(k[1])
                if k[0] == "V":
                    return (Vh, Vl)[part][:, p, i * DM:(i + 1) * DM]
                dst = ((KRh, KRl) if k[0] == "K" else (QRh, QRl))[part]
                return dst[:, 4 * i + 2 * p:4 * i + 2 * p + 2, :].rearrange("p h m -> p (h m)")

            def unit_high(u):
                act.wait_ge(staged_ok, u + 1)
                S.activation(unit_dst(u, 0), staged[:, u % 2, :], ACT.Copy).then_inc(unit_hi, 1)

            act.wait_ge(var_s_ok, 1)
            norm_sd(0, mv[:, 0:NS, 1], 1.0, eps_ln)
            rms_sd(N_TILES - 1)
            act.wait_ge(var_s_ok, 2)
            norm_sd(1, sumsq, 1.0 / DM, eps_rms)
            hidden_high(0)
            block_hi(2)
            for u in range(before_heads):
                unit_bias(u)
                if u:
                    unit_high(u - 1)
                if u % 2:
                    block_hi(u // 2 + 3)
            unit_high(before_heads - 1)
            S.activation(gate, sel_score, ACT.Exp, scale=-1.0).then_inc(gate_ok, 1)
            for h in range(STEPS):
                for u in units_of_step.get(h - 1, ()):
                    unit_high(u)
                if h < FH:
                    act.wait_ge(sm_ok, h + 1), act.wait_ge(pn_ok, h)
                    for t, cols in ((0, slice(0, P)), (1, slice(P, 3 * P))):
                        ins = S.activation(PR[:, cols], SM[:, cols], ACT.Exp, scale=float(FD) ** -0.5,
                                           bias=ntop[:, h % 2, t:t + 1], accum_out=psum_[:, h % 2, t:t + 1])
                    ins.then_inc(exp_ok, 1)
                if 1 <= h <= FH:
                    act.wait_ge(pt_ps, h)
                    if h >= 3:
                        act.wait_ge(ot_ps, h - 2)
                    S.activation(PTh[:, (h - 1) % 2, :], B[4][:, 0:3 * P], ACT.Copy).then_inc(pt_hi, 1)
                if 2 <= h <= FH + 1:
                    act.wait_ge(ot_ps, h - 1)
                    if h >= 4:
                        act.wait_ge(wo_ps, h - 3)
                    S.activation(OTh[:, (h - 2) % 2, :], B[5][:, 0:SEL], ACT.Copy).then_inc(ot_hi, 1)
                for u in units_of_step.get(h, ()):
                    unit_bias(u)
                if h in split_after:
                    block_hi(block_of[split_after[h]])
            block_hi(14)
            act.wait_ge(var_s_ok, 3)
            norm_sd(2, sumsq, 1.0 / DM, eps_rms)
            hidden_high(1)
            for j in range(4):
                for p in range(2):
                    m = 2 * j + p
                    act.wait_ge(g_ps, m + 1)
                    if m >= 2:
                        act.wait_ge(mt_ok, m - 1)
                    S.activation(sg[:, m % 2, :], B[m % 2][:], ACT.Silu).then_inc(sg_ok, 1)
                block_hi(block_of[f"G{j}"] + 3) if block_of[f"G{j}"] + 3 < len(order) else None
                for p in range(2):
                    m = 2 * j + p
                    act.wait_ge(mt_ok, m + 1)
                    S.activation(QRh[:, 2 * m:2 * m + 2, :].rearrange("p h m -> p (h m)"), staged[:, m % 2, :],
                                 ACT.Copy).then_inc(mt_hi, 1)
                for b in range(block_of[f"G{j}"] + 4, (block_of[f"G{j + 1}"] if j < 3 else len(order)) + 3):
                    if b < len(order):
                        block_hi(b)

        @block.vector
        def _(dve):
            ch = Chain(dve, dve_chain)
            V.memset(eps_ln, 1e-5)
            V.memset(ones1, 1.0)
            V.memset(eps_rms, 1e-6).then_inc(consts, 1)

            def ln_stats(M):
                s = M % NX
                dve.wait_ge(x_in[s], 16 * (M // NX + 1))
                dve.wait_ge(xn_ok, max(M - NX + 1, 0))
                ch.link(V.bn_stats(stats[:, s, :], X[:, s, :]))
                V.bn_aggr(mv[:, s, :], stats[:, s, :]).then_inc(var_ok, 1)

            def ln_norm(M):
                s = M % NX
                dve.wait_ge(sd_ln_ok, M + 1)
                ch.link(V.reciprocal(rstd[:, s:s + 1], sd_ln[:, s:s + 1]))
                if M >= NX:
                    dve.wait_ge(xt_ps, M - NX + 1), dve.wait_ge(base_ok, M - NX + 1)
                V.tensor_scalar(XN[:, s, :], X[:, s, :], mv[:, s, 0:1], rstd[:, s:s + 1], ALU.subtract,
                                ALU.mult).then_inc(xn_ok, 1)

            def router(M):
                dve.wait_ge(const_in, 64), dve.wait_ge(xn_ok, M + 1)
                V.tensor_tensor_reduce(out=kv_new[:].rearrange("p k m -> p (k m)"), in0=XN[:, M % NX, :], in1=wr_b[:],
                                       scale=1.0, scalar=0.0, op0=ALU.mult, op1=ALU.add,
                                       accum_out=score_all[:, M:M + 1]).then_inc(score_ok, 1)

            def xt_low(M):
                at = slice(M % CH * P, (M % CH + 1) * P)
                dve.wait_ge(xt_hi, M + 1)
                V.tensor_tensor(xTl[:, M // CH % 2, :, at], tiles4(xt_bank(M)[:]), xTh[:, M // CH % 2, :, at].bitcast(f32),
                                ALU.subtract).then_inc(xt_lo, 1)

            def weights_lo(n):
                dve.wait_ge(w_hi, n + 1)
                q = (1, 0, 2, 3, 0)[n]
                dst, hi, src = (Wl[:, :, q * DM:(q + 1) * DM], Wh[:, :, q * DM:(q + 1) * DM], raw_qkvu[n]) \
                    if n < 4 else (Wol[:], Woh[:], raw_wo)
                V.tensor_tensor(dst, src, hi.bitcast(f32), ALU.subtract).then_inc(w_lo, 1)

            def rank_tokens(first, last):
                if first == 0:
                    dve.wait_ge(sbc_in, 16), dve.wait_ge(score_ok, N_TILES)
                    ch.link(V.memset(n_ge, 0.0))
                for n in range(first, last):
                    me = score_all[:, n:n + 1]
                    if n:
                        ch.link(V.tensor_scalar(seen[:, 0:n * P], s_bc[:, 0:n * P], me, None, ALU.is_ge, ALU.add,
                                                accum_out=n_ge[:, n:n + 1]))
                    ch.link(V.tensor_scalar(seen[:, n * P:], s_bc[:, n * P:], me, None, ALU.is_gt, ALU.add,
                                            accum_out=n_gt[:, n:n + 1]))
                    ch.link(V.scalar_tensor_tensor(out=seen[:, 0:P], in0=s_bc[:, n * P:(n + 1) * P], scalar=me,
                                                   in1=below[:], op0=ALU.is_equal, op1=ALU.mult,
                                                   accum_out=n_eq[:, n:n + 1]))
                if last < N_TILES:
                    return
                ch.link(V.tensor_tensor(rank, n_ge, n_gt, ALU.add))
                ch.link(V.tensor_tensor(rank, rank, n_eq, ALU.add))
                V.tensor_scalar(chosen, rank, float(SEL), None, ALU.is_lt)
                V.tensor_scalar(chosen_b[:], rank, float(SEL), None, ALU.is_lt).then_inc(rank_ok, 1)

            def place_tokens():
                dve.wait_ge(cnt_ps, 1), dve.wait_ge(rank_ok, 1)
                ch.link(V.tensor_copy(n_gt, B[5][:, N_TILES:2 * N_TILES]))
                ch.link(V.tensor_tensor_scan(before, n_gt, n_ge, 0.0, ALU.add, ALU.bypass))
                ch.link(V.tensor_tensor(before, before, n_gt, ALU.subtract))
                ch.link(V.tensor_tensor(place, B[5][:, 0:N_TILES], before, ALU.add))
                ch.link(V.tensor_scalar(n_eq, chosen, -float(N_TOK), float(N_TOK), ALU.mult, ALU.add))
                ch.link(V.tensor_tensor(place, place, n_eq, ALU.add))
                for n in range(N_TILES):
                    ins = V.tensor_scalar(one_hot[:, n, :], slots[:], place[:, n:n + 1], None, ALU.is_equal)
                ins.then_inc(oh_ok, 1)

            def token_indices():
                dve.wait_ge(idx_ps, 1)
                ch.link(V.tensor_copy(idx_f[:], B[5][:, 0:2 * NS]))
                for t in range(NS):
                    ins = V.scalar_tensor_tensor(out=idx[:, t:t + 1], in0=idx_f[:, 2 * t + 1:2 * t + 2],
                                                 scalar=float(P), in1=idx_f[:, 2 * t:2 * t + 1], op0=ALU.mult,
                                                 op1=ALU.add)
                ins.then_inc(idx_ok, 1)

            def q_low(N, half):
                dve.wait_ge(q_hi, 2 * N + half + 1), dve.wait_ge(s_ps, 2 * N + half)
                cols = slice(N % CH * P, (N % CH + 1) * P)
                for r in range(4):
                    rows = slice(DH * r, DH * r + DH)
                    ins = V.tensor_tensor(QBl[rows, :, r, :], QT[rows, N // CH % 2, 2 * half:2 * half + 2, cols],
                                          QBh[rows, :, r, :].bitcast(f32), ALU.subtract)
                ins.then_inc(q_lo, 1)

            def mask(N, half):
                dve.wait_ge(s_ps, 2 * N + half + 1), dve.wait_ge(pv_ps, N), dve.wait_ge(dec_ok, 1)
                for b in range(2):
                    heads = slice(8 * half + 4 * b, 8 * half + 4 * b + 4)
                    V.tensor_tensor(A[:, heads, :], tiles4(B[b][:]), DEC[:, heads, :], ALU.mult).then_inc(masked, 1)

            def state_part(N):
                dve.wait_ge(kv_ps, N + 1), dve.wait_ge(bm_ok, 1)
                dve.wait_ge(score_ok, min(N + LN_AHEAD + 1, N_TILES)), dve.wait_ge(state_ok, N)
                V.tensor_tensor(kv_new[:], tiles4(B[6][:]), BM[:].unsqueeze(1).to_broadcast([P, NK, P]), ALU.mult)\
                    .then_inc(kv_masked, 1)

            def final(N):
                dve.wait_ge(out_ps, N + 1), dve.wait_ge(sd_o_ok, N + 1)
                ch.link(V.reciprocal(r_o, sd_o))
                dve.wait_ge(base_ok, N + 1)
                V.scalar_tensor_tensor(out=BASE[:, N % NBASE, :], in0=B[7][:], scalar=r_o, in1=BASE[:, N % NBASE, :],
                                       op0=ALU.mult, op1=ALU.add).then_inc(final_ok, 1)

            for M in range(CH):
                ln_stats(M)
            for M in range(CH):
                ln_norm(M)
            for M in range(CH):
                xt_low(M)
            ln_stats(CH)
            weights_lo(0)
            ln_norm(CH)
            weights_lo(1)
            dve.wait_ge(const_in, 64)
            V.tensor_scalar(nshead, shead, -1.0, None, ALU.mult)
            V.tensor_scalar(nshid, shid, -1.0, None, ALU.mult).then_inc(slopes_ok, 1)
            dve.wait_ge(iota_ok, 3)
            V.tensor_scalar(lag, lag, 0.0, None, ALU.max).then_inc(lag_ok, 1)
            for M in range(NX):
                router(M)
                dve.wait_ge(score_ok, M + 1)
            ch.link(V.memset(BM[:], 0.0))
            for r in range(4):
                V.memset(BM[DH * r:DH * r + DH, DH * r:DH * r + DH], 1.0)
            V.memset(QBh[:].bitcast(f32), 0.0)
            V.memset(QBl[:].bitcast(f32), 0.0)
            V.memset(state[:], 0.0).then_inc(bm_ok, 1)
            dve.wait_ge(bm_ok, 1)
            for N in slots_of_chunks:
                M = N + LN_AHEAD
                if M < N_TILES:
                    ln_stats(M)
                if (N, 0) in rank_in:
                    rank_tokens(*rank_in[N, 0])
                if N == N_TILES - 1:
                    place_tokens()
                if N >= 0:
                    mask(N, 0)
                if 0 <= N < N_TILES - 1:
                    dve.wait_ge(kt_ps, N + 1), dve.wait_ge(kv_ps, N)
                    V.tensor_tensor(kdec[:], B[5][:], KD[:], ALU.mult).then_inc(k_dec, 1)
                if N >= 0:
                    q_low(N, 1)
                if N == -1:
                    q_low(0, 0)
                if (N, 1) in rank_in:
                    rank_tokens(*rank_in[N, 1])
                if N == N_TILES - 1:
                    token_indices()
                if M < N_TILES:
                    ln_norm(M)
                    dve.wait_ge(state_ok, max(N, 0))
                    router(M)
                    if N < 0:
                        dve.wait_ge(score_ok, M + 1)
                if N >= 0:
                    mask(N, 1)
                    if N >= 1:
                        final(N - 1)
                    if N < N_TILES - 1:
                        q_low(N + 1, 0)
                        state_part(N)
                if N + XT_AHEAD < N_TILES:
                    xt_low(N + XT_AHEAD)
                if N == -2:
                    weights_lo(4)
                if N == -1:
                    dve.wait_ge(decays_ok, 1), dve.wait_ge(masks_ok, 3)
                    V.tensor_tensor(DEC[:], DEC[:], tri[:].unsqueeze(1).to_broadcast([P, NH, P]), ALU.mult)\
                        .then_inc(dec_ok, 1)
                if N >= 0:
                    at = slice(N % CH * P, (N % CH + 1) * P)
                    dve.wait_ge(pv_ps, N + 1), dve.wait_ge(uo_hi, N), dve.wait_ge(uo_lo, N)
                    V.tensor_tensor(uo[:], tiles4(B[4][:]), UT[:, N // CH % 2, :, at], ALU.mult).then_inc(uo_ok, 1)

            dve.wait_ge(picked, 16 * 2 * NS)

            def normed(n, src):
                for t in range(NS):
                    ins = V.tensor_tensor_reduce(out=hs[:, t, :], in0=src[:, t, :], in1=src[:, t, :], scale=1.0,
                                                 scalar=0.0, op0=ALU.mult, op1=ALU.add, accum_out=sumsq[:, t:t + 1])
                ins.then_inc(var_s_ok, 1)
                dve.wait_ge(sd_s_ok, n + 2)
                ch.link(V.reciprocal(r_s, sd_s))
                for t in range(NS):
                    ins = V.tensor_scalar(hs[:, t, :], src[:, t, :], r_s[:, t:t + 1], None, ALU.mult)
                ins.then_inc(hs_ok, 1)

            def hidden_low(n):
                for k in range(NK):
                    dve.wait_ge(ht_hi, NK // 2 * n + k // 2 + 1)
                    V.scalar_tensor_tensor(out=HTl[:, k, :], in0=B[k // 2][:, (k % 2) * SEL:(k % 2 + 1) * SEL],
                                           scalar=ln12[:, n, k:k + 1], in1=HTh[:, k, :].bitcast(f32), op0=ALU.mult,
                                           op1=ALU.subtract).then_inc(ht_lo, 1)

            def low_of(dst, src, high, done):
                V.tensor_tensor(dst, src, high.bitcast(f32), ALU.subtract).then_inc(done, 1)

            for t in range(NS):
                ch.link(V.bn_stats(stats[:, t, :], xs[:, t, :]))
            for t in range(NS):
                ins = V.bn_aggr(mv[:, t, :], stats[:, t, :])
            ins.then_inc(var_s_ok, 1)
            dve.wait_ge(sd_s_ok, 1)
            ch.link(V.reciprocal(r_s, sd_s))
            for t in range(NS):
                ch.link(V.tensor_scalar(xsn[:, t, :], xs[:, t, :], mv[:, t, 0:1], r_s[:, t:t + 1], ALU.subtract,
                                        ALU.mult))
            normed(0, xsn)
            final(N_TILES - 1)
            for t in range(NS):
                ch.link(V.tensor_tensor_reduce(out=ao[:, t, :], in0=xsn[:, t, :], in1=wr_b[:], scale=1.0, scalar=0.0,
                                               op0=ALU.mult, op1=ALU.add, accum_out=sel_score[:, t:t + 1]))
            dve.wait_ge(tab_ps, 1)
            V.tensor_copy(CS[:].rearrange("p a m -> p (a m)"), B[2][:]).then_inc(cs_ok, 1)
            dve.wait_ge(final_ok, N_TILES), dve.wait_ge(stored[0], 8 * N_TILES), dve.wait_ge(stored[1], 8 * N_TILES)
            hidden_low(0)

            def stage(u):
                k, p = units[u]
                if u >= 2:
                    dve.wait_ge(unit_hi, u - 1), dve.wait_ge(unit_lo, u - 1)
                if k[0] == "V":
                    dve.wait_ge(unit_ps, u + 1), dve.wait_ge(part_in, 16 * 5)
                    i = int(k[1])
                    V.tensor_tensor(staged[:, u % 2, :], B[u % 2][:], bvb[:, i * DM:(i + 1) * DM], ALU.add)\
                        .then_inc(staged_ok, 1)
                    return
                dve.wait_ge(unit_b, kq_count(u)), dve.wait_ge(cs_ok, 1)
                dve.wait_ge(staged_ok, u)
                both = qb[:, u % 2]
                half = P // 2
                V.tensor_tensor(rope1[:], both, CS[:, 0, :].unsqueeze(1).to_broadcast([P, 2, SEL]), ALU.mult)
                for a, b in ((0, half), (half, 0)):
                    ins = V.tensor_tensor(rope2[a:a + half], both[b:b + half],
                                          CS[b:b + half, 1, :].unsqueeze(1).to_broadcast([half, 2, SEL]), ALU.mult)
                ch.link(ins)
                V.tensor_tensor(staged[:, u % 2, :].rearrange("p (a m) -> p a m", a=2), rope1[:], rope2[:],
                                ALU.add).then_inc(staged_ok, 1)

            def unit_low(u):
                k, p = units[u]
                i = int(k[1])
                dve.wait_ge(unit_hi, u + 1)
                if k[0] == "V":
                    low_of(Vl[:, p, i * DM:(i + 1) * DM], staged[:, u % 2, :], Vh[:, p, i * DM:(i + 1) * DM], unit_lo)
                else:
                    hi, lo = (KRh, KRl) if k[0] == "K" else (QRh, QRl)
                    heads = slice(4 * i + 2 * p, 4 * i + 2 * p + 2)
                    low_of(lo[:, heads, :], staged[:, u % 2, :].rearrange("p (a m) -> p a m", a=2), hi[:, heads, :],
                           unit_lo)

            for u in range(before_heads):
                stage(u)
                if u:
                    unit_low(u - 1)
            unit_low(before_heads - 1)
            dve.wait_ge(causal_ok, 3)
            for h in range(STEPS):
                if h < FH:
                    dve.wait_ge(sc_ps, h + 1), dve.wait_ge(exp_ok, h)
                    for t, cols in ((0, slice(0, P)), (1, slice(P, 3 * P))):
                        ins = V.tensor_tensor_reduce(out=SM[:, cols], in0=B[2 + h % 2][:, cols], in1=causal[:, cols],
                                                     scale=1.0, scalar=-3.0e38, op0=ALU.add, op1=ALU.max,
                                                     accum_out=top[:, h % 2, t:t + 1])
                    ch.link(ins)
                    V.tensor_scalar(ntop[:, h % 2, :], top[:, h % 2, :], -(float(FD) ** -0.5), None, ALU.mult)\
                        .then_inc(sm_ok, 1)
                for u in units_of_step.get(h - 1, ()):
                    unit_low(u)
                if h < FH:
                    dve.wait_ge(exp_ok, h + 1)
                    if h >= 2:
                        dve.wait_ge(pt_ps, h - 1)
                    ch.link(V.reciprocal(pinv[:, h % 2, :], psum_[:, h % 2, :]))
                    for t, cols in ((0, slice(0, P)), (1, slice(P, 3 * P))):
                        ins = V.tensor_scalar(PN[:, h % 2, cols], PR[:, cols], pinv[:, h % 2, t:t + 1], None, ALU.mult)
                    ins.then_inc(pn_ok, 1)
                if 1 <= h <= FH:
                    dve.wait_ge(pt_hi, h)
                    if h >= 3:
                        dve.wait_ge(ot_ps, h - 2)
                    low_of(PTl[:, (h - 1) % 2, :], B[4][:, 0:3 * P], PTh[:, (h - 1) % 2, :], pt_lo)
                if 2 <= h <= FH + 1:
                    dve.wait_ge(ot_hi, h - 1)
                    if h >= 4:
                        dve.wait_ge(wo_ps, h - 3)
                    low_of(OTl[:, (h - 2) % 2, :], B[5][:, 0:SEL], OTh[:, (h - 2) % 2, :], ot_lo)
                for u in units_of_step.get(h, ()):
                    stage(u)
            dve.wait_ge(gate_ok, 1)
            ch.link(V.tensor_scalar(gate, gate, 1.0, None, ALU.add))
            ch.link(V.reciprocal(gate, gate))
            dve.wait_ge(wo_ps, FH)
            for t in range(NS):
                ins = V.tensor_copy(ao[:, t, :], B[6 + t][:])
            ch.link(ins)
            for t in range(NS):
                ins = V.tensor_tensor(xs[:, t, :], xsn[:, t, :], ao[:, t, :], ALU.add)
            ch.link(ins)
            normed(1, xs)
            hidden_low(1)
            for j in range(4):
                for p in range(2):
                    m = 2 * j + p
                    dve.wait_ge(sg_ok, m + 1), dve.wait_ge(u_ps, m + 1)
                    if m >= 2:
                        dve.wait_ge(mt_hi, m - 1), dve.wait_ge(mt_lo, m - 1)
                    V.tensor_tensor(staged[:, m % 2, :], sg[:, m % 2, :], B[2 + m % 2][:], ALU.mult)\
                        .then_inc(mt_ok, 1)
                for p in range(2):
                    m = 2 * j + p
                    dve.wait_ge(mt_hi, m + 1)
                    low_of(QRl[:, 2 * m:2 * m + 2, :], staged[:, m % 2, :].rearrange("p (a m) -> p a m", a=2),
                           QRh[:, 2 * m:2 * m + 2, :], mt_lo)
            dve.wait_ge(down_ps, 4)
            for t in range(NS):
                ins = V.tensor_tensor(ao[:, t, :], B[6 + t][:], ao[:, t, :], ALU.add)
            ch.link(ins)
            for t in range(NS):
                V.tensor_scalar(hs[:, t, :], ao[:, t, :], gate[:, t:t + 1], None, ALU.mult).then_inc(delta_ok, 1)

        @block.gpsimd
        def _(pool):
            Q.iota(lag, pattern=[[1, P]], base=0, channel_multiplier=-1, allow_small_or_imprecise_dtypes=True)\
                .then_inc(iota_ok, 1)
            Q.iota(ahead, pattern=[[1, P]], base=1, channel_multiplier=0, allow_small_or_imprecise_dtypes=True)\
                .then_inc(iota_ok, 1)
            Q.iota(age, pattern=[[0, 1]], base=1 - P, channel_multiplier=1, allow_small_or_imprecise_dtypes=True)\
                .then_inc(iota_ok, 1)
            Q.memset(ident[:], 0.0).then_inc(pool_chain, 1)
            Q.memset(tri[:], 1.0).then_inc(pool_chain, 1)
            Q.memset(below[:], 1.0).then_inc(pool_chain, 1)
            Q.memset(above[:], 1.0).then_inc(pool_chain, 1)
            Q.memset(ones_sq[:], 1.0)
            pool.wait_ge(pool_chain, 4)
            Q.affine_select(out=ident[:], in_=ident[:], compare_op=ALU.not_equal, fill=1.0, base=0,
                            pattern=[[-1, P]], channel_multiplier=1).then_inc(masks_ok, 1)
            Q.affine_select(out=tri[:], in_=tri[:], compare_op=ALU.is_ge, fill=0.0, base=0,
                            pattern=[[1, P]], channel_multiplier=-1).then_inc(masks_ok, 1)
            Q.affine_select(out=below[:], in_=below[:], compare_op=ALU.is_gt, fill=0.0, base=0,
                            pattern=[[-1, P]], channel_multiplier=1).then_inc(masks_ok, 1)
            Q.affine_select(out=above[:], in_=above[:], compare_op=ALU.is_gt, fill=0.0, base=0,
                            pattern=[[1, P]], channel_multiplier=-1)
            Q.iota(slots[:], pattern=[[1, SEL]], base=0, channel_multiplier=0, allow_small_or_imprecise_dtypes=True)
            Q.iota(tok2[:, :, 0], pattern=[[0, N_TILES]], base=0, channel_multiplier=1,
                   allow_small_or_imprecise_dtypes=True)
            Q.iota(tok2[:, :, 1], pattern=[[1, N_TILES]], base=0, channel_multiplier=0,
                   allow_small_or_imprecise_dtypes=True).then_inc(tok_ok, 1)

            def base(M):
                pool.wait_ge(xn_ok, M + 1)
                if M >= NBASE:
                    pool.wait_ge(stored[M % 2], 16 * ((M - NBASE) // 2 + 1))
                elif M == NBASE - 1:
                    pool.wait_ge(decays_ok, 1)
                Q.tensor_tensor(BASE[:, M % NBASE, :], X[:, M % NX, :], XN[:, M % NX, :], ALU.add)\
                    .then_inc(base_ok, 1)

            def weights_lo(n):
                pool.wait_ge(w_hi, n + 1)
                Q.tensor_tensor(Wl[:, :, n * DM:(n + 1) * DM], raw_qkvu[n], Wh[:, :, n * DM:(n + 1) * DM].bitcast(f32),
                                ALU.subtract).then_inc(w_lo_pool, 1)

            def q_decayed(N):
                pool.wait_ge(inter_ps, N), pool.wait_ge(decays_ok, 1), pool.wait_ge(proj_sb, NPROJ * (N // CH) + 4)
                Q.tensor_tensor(qdec[:], QT[:, N // CH % 2, :, N % CH * P:(N % CH + 1) * P], QD[:], ALU.mult)\
                    .then_inc(q_dec, 1)

            def state_decayed(N):
                pool.wait_ge(state_ok, N), pool.wait_ge(bm_ok, 1)
                Q.tensor_tensor(state_dec[:], state[:], bdec.unsqueeze(2).to_broadcast([P, NK, P]), ALU.mult)\
                    .then_inc(state_dk, 1)

            def new_state(N):
                pool.wait_ge(kv_masked, N + 1), pool.wait_ge(state_dk, N + 1)
                Q.tensor_tensor(state[:], kv_new[:], state_dec[:], ALU.add).then_inc(state_ok, 1)

            def k_low(N):
                pool.wait_ge(k_hi, N + 1)
                Q.tensor_tensor(kl[:], KT[:, N // CH % 2, :, N % CH * P:(N % CH + 1) * P], kh[:].bitcast(f32),
                                ALU.subtract).then_inc(k_lo, 1)

            def uo_low(N):
                pool.wait_ge(uo_hi, N + 1), pool.wait_ge(out_ps, N)
                Q.tensor_tensor(uol[:], uo[:], uoh[:].bitcast(f32), ALU.subtract).then_inc(uo_lo, 1)

            def gather():
                pool.wait_ge(idx_ok, 1)
                for t in range(NS):
                    for dst, src in ((xs[:, t, :], x), (tab[:, t * 2 * FD:(t + 1) * 2 * FD], rope)):
                        Q.indirect_dma_start(out=dst, out_offset=None, in_=src,
                                             in_offset=bass.IndirectOffsetOnAxis(ap=idx[:, t:t + 1], axis=0))\
                            .then_inc(picked, 16)

            def block_lo(b):
                pool.wait_ge(fw_hi, b + 1)
                pool.wait_ge(*last_use(b - 3))
                Q.tensor_tensor(wlo[b % 3][:], raw[b % 2][:], whi[b % 3][:].bitcast(f32), ALU.subtract)\
                    .then_inc(fw_lo, 1)

            base(0)
            base(1)
            for N in slots_of_chunks:
                if N == -2:
                    weights_lo(2)
                    weights_lo(3)
                if N >= 1:
                    uo_low(N - 1)
                if N >= 0 and N < N_TILES - 1:
                    q_decayed(N + 1)
                if -1 <= N < N_TILES - 1:
                    k_low(N + 1)
                if N == -1:
                    q_decayed(0)
                if N + XT_AHEAD < N_TILES:
                    base(N + XT_AHEAD)
                if N >= 0 and N < N_TILES - 1:
                    new_state(N)
                if -1 <= N < N_TILES - 1:
                    state_decayed(N + 1)
                if N == N_TILES - 2:
                    block_lo(0)
                if N == N_TILES - 1:
                    gather()
            uo_low(N_TILES - 1)
            block_lo(1)

            Q.memset(causal[:], 0.0).then_inc(causal_ok, 1)
            pool.wait_ge(causal_ok, 1)
            for blk in (0, 2):
                Q.affine_select(out=causal[:, blk * P:(blk + 1) * P], in_=causal[:, blk * P:(blk + 1) * P],
                                compare_op=ALU.is_ge, fill=-1.0e38, base=0, pattern=[[-1, P]], channel_multiplier=1)\
                    .then_inc(causal_ok, 1)
            for b in range(2, len(order)):
                block_lo(b)
            for t in range(NS):
                pool.wait_ge(delta_ok, t + 1)
                Q.indirect_dma_start(out=out, out_offset=bass.IndirectOffsetOnAxis(ap=idx[:, t:t + 1], axis=0),
                                     in_=hs[:, t, :], in_offset=None, compute_op=ALU.add).then_inc(scattered, 16)
            pool.wait_ge(scattered, 16 * NS)

        @block.tensor
        def _(pe):
            def split_matmuls(dst, lhs, rhs, first, last):
                (lh, ll), (rh, rl) = lhs, rhs
                T.matmul(dst, lh, rh, start=first, stop=False)
                T.matmul(dst, lh, rl, start=False, stop=False)
                return T.matmul(dst, ll, rh, start=False, stop=last)

            def transposed(M):
                pe.wait_ge(xn_ok, M + 1), pe.wait_ge(masks_ok, 1)
                if M >= 2:
                    pe.wait_ge(xt_lo, M), pe.wait_ge(k_dec, max(M - XT_AHEAD + 1, 0))
                for k in range(NK):
                    ins = T.transpose(xt_bank(M)[:, k * P:(k + 1) * P], XN[:, M % NX, k * P:(k + 1) * P], ident[:])
                ins.then_inc(xt_ps, 1)

            def nothing(step):
                pass

            def project(tile, beside=nothing):
                g, i = tile // NPROJ, tile % NPROJ
                name, j = "KQVU"[i // 2], i % 2
                lo = {"Q": 0, "K": DM, "V": 2 * DM, "U": 3 * DM}[name]
                if i == 0:
                    pe.wait_ge(xt_lo, CH * (g + 1))
                if g == 0 and j == 0:
                    if name in "KQ":
                        pe.wait_ge(w_lo, 1 + i // 2)
                    else:
                        pe.wait_ge(w_lo_pool, i // 2 - 1)
                if tile >= 2:
                    pe.wait_ge(proj_sb, tile - 1)
                bank = B[2 + tile % 2]
                steps = 3 * NK
                for step in range(steps):
                    if name == "V":
                        k, n = step // 3, step % 3
                        xt, w = ((xTh, Wh), (xTh, Wl), (xTl, Wh))[n]
                        ins = T.matmul(bank[:], xt[:, g % 2, k, j * P:(j + 1) * P], w[:, k, lo:lo + DM],
                                       start=step == 0, stop=step == steps - 1)
                    else:
                        for m in (2 * step, 2 * step + 1):
                            half, k, n = m // steps, m % steps // 3, m % 3
                            cols = slice(lo + (2 * j + half) * P, lo + (2 * j + half + 1) * P)
                            w, xt = ((Wh, xTh), (Wh, xTl), (Wl, xTh))[n]
                            ins = T.matmul(bank[:, half * GROUP:(half + 1) * GROUP], w[:, k, cols], xt[:, g % 2, k, :],
                                           start=m % steps == 0, stop=m % steps == steps - 1)
                    if step == steps - 1:
                        ins.then_inc(proj_ps, 1)
                    beside(step)

            def score(N, half):
                pe.wait_ge(k_hi, N + 1), pe.wait_ge(q_hi, 2 * N + half + 1)
                pe.wait_ge(k_lo, N + 1), pe.wait_ge(q_lo, 2 * N + half + 1)
                pe.wait_ge(masked, 4 * N + 2 * half)
                for b in range(2):
                    j = 2 * half + b
                    ins = split_matmuls(B[b][:], (kh[:, j, :], kl[:, j, :]),
                                        [q[:, b].rearrange("p r m -> p (r m)") for q in (QBh, QBl)], True, True)
                ins.then_inc(s_ps, 1)

            def rms(N, step):
                if step == 2:
                    pe.wait_ge(sq_ok, N + 1), pe.wait_ge(final_ok, N), pe.wait_ge(consts, 1)
                if step % 3 == 2:
                    k = step // 3
                    ins = T.matmul(B[7][:, 0:1], sq[:, k, :], ones1, start=k == 0, stop=k == NK - 1)
                    if k == NK - 1:
                        ins.then_inc(rms_ps, 1)

            def project_out(N):
                pe.wait_ge(uo_hi, N + 1), pe.wait_ge(uo_lo, N + 1), pe.wait_ge(sd_o_ok, N + 1), pe.wait_ge(w_lo, 3)
                for k in range(NK):
                    ins = split_matmuls(B[7][:], (uoh[:, k, :], uol[:, k, :]), (Woh[:, k, :], Wol[:, k, :]),
                                        k == 0, k == NK - 1)
                ins.then_inc(out_ps, 1)

            def inside(N, step):
                if step == 2:
                    pe.wait_ge(masked, 4 * N + 4)
                if step % 3 == 2:
                    j = step // 3
                    for r in range(4):
                        h = 4 * j + r
                        ins = T.matmul(B[4][DH * r:DH * r + DH, j * P:(j + 1) * P],
                                       VT[:, N // CH % 2, N % CH, DH * h:DH * h + DH], A[:, h, :], start=False,
                                       stop=True, skip_group_check=True)
                    if j == NK - 1:
                        ins.then_inc(pv_ps, 1)

            transposed(0)
            transposed(1)
            for N in slots_of_chunks:
                tiles = proj_tiles(N)
                if N < 0:
                    project(tiles[0])
                    project(tiles[1])
                    transposed(N + XT_AHEAD)
                    project(tiles[2])
                    project(tiles[3])
                    continue
                buf = N // CH % 2
                score(N, 0)
                if N == 0:
                    project(tiles[0])
                elif tiles:
                    project(tiles[0], lambda step: rms(N - 1, step))
                else:
                    for step in range(3 * NK):
                        rms(N - 1, step)
                if N < N_TILES - 1:
                    pe.wait_ge(xt_lo, min(N + XT_AHEAD, N_TILES))
                    for k in range(NK):
                        ins = T.transpose(B[5][:, k * P:(k + 1) * P], KT[:, buf, k, N % CH * P:(N % CH + 1) * P],
                                          ident[:])
                    ins.then_inc(kt_ps, 1)
                pe.wait_ge(q_dec, N + 1), pe.wait_ge(state_ok, N), pe.wait_ge(bm_ok, 1)
                pe.wait_ge(uo_ok, N), pe.wait_ge(sq_ok, N)
                for j in range(NK):
                    ins = T.matmul(B[4][:, j * P:(j + 1) * P], state[:, j, :], qdec[:, j, :], start=j == 0,
                                   stop=False, skip_group_check=True)
                ins.then_inc(inter_ps, 1)
                if N == N_TILES - 1:
                    pe.wait_ge(oh_ok, 1)
                    for t in range(NS):
                        for n in range(N_TILES):
                            ins = T.matmul(B[5][:, 2 * t:2 * t + 2], one_hot[:, n, t * P:(t + 1) * P], tok2[:, n, :],
                                           start=n == 0, stop=n == N_TILES - 1)
                    ins.then_inc(idx_ps, 1)
                if tiles:
                    project(tiles[1])
                score(N, 1)
                if N >= 1:
                    project_out(N - 1)
                pe.wait_ge(proj_sb, NPROJ * (N // CH) + 6)
                if N < N_TILES - 1:
                    pe.wait_ge(k_dec, N + 1), pe.wait_ge(kv_masked, N)
                    for j in range(NK):
                        cols = slice(j * P, (j + 1) * P)
                        ins = T.matmul(B[6][:, cols], kdec[:, cols], VT[:, buf, N % CH, cols], start=True, stop=True)
                    ins.then_inc(kv_ps, 1)
                if N + XT_AHEAD < N_TILES:
                    transposed(N + XT_AHEAD)
                if tiles:
                    project(tiles[2], lambda step: inside(N, step))
                    project(tiles[3])
                else:
                    for step in range(3 * NK):
                        inside(N, step)
                if N == N_TILES - 2:
                    pe.wait_ge(rank_ok, 1), pe.wait_ge(tok_ok, 1), pe.wait_ge(k_dec, N + 1)
                    T.matmul(B[5][:, 0:N_TILES], above[:], chosen_b[:], start=True, stop=True)
                    T.matmul(B[5][:, N_TILES:2 * N_TILES], ones_sq[:], chosen_b[:], start=True, stop=True)\
                        .then_inc(cnt_ps, 1)
            for step in range(3 * NK):
                rms(N_TILES - 1, step)
            project_out(N_TILES - 1)

            def block_ready(b):
                pe.wait_ge(fw_hi, b + 1), pe.wait_ge(fw_lo, b + 1)

            def hidden_transposed(n):
                pe.wait_ge(hs_ok, n + 1)
                pe.wait_ge(masked, 4 * N_TILES)
                if n == 0:
                    pe.wait_ge(final_ok, N_TILES)
                for k in range(NK):
                    for t in range(NS):
                        at = (k % 2) * SEL + t * P
                        ins = T.transpose(B[k // 2][:, at:at + P], hs[:, t, k * P:(k + 1) * P], ident[:])
                ins.then_inc(ht_ps, 1)

            def pair(bank, b, p):
                for i in range(2):
                    cols = slice((2 * p + i) * P, (2 * p + i + 1) * P)
                    for k in range(NK):
                        ins = split_matmuls(bank[:, i * SEL:(i + 1) * SEL], (whi[b % 3][:, k, cols], wlo[b % 3][:, k, cols]),
                                            (HTh[:, k, :], HTl[:, k, :]), k == 0, k == NK - 1)
                return ins

            def unit(u):
                k, p = units[u]
                b = block_of[k]
                block_ready(b)
                if u >= 2:
                    if units[u - 2][0][0] == "V":
                        pe.wait_ge(staged_ok, u - 1)
                    else:
                        pe.wait_ge(unit_b, kq_count(u - 2))
                if k[0] == "V":
                    for n in range(NK):
                        rows = slice(p * P, (p + 1) * P)
                        ins = split_matmuls(B[u % 2][:], (HTh[:, n, rows], HTl[:, n, rows]),
                                            (whi[b % 3][:, n, :], wlo[b % 3][:, n, :]), n == 0, n == NK - 1)
                else:
                    ins = pair(B[u % 2], b, p)
                ins.then_inc(unit_ps, 1)

            pe.wait_ge(picked, 16 * 2 * NS), pe.wait_ge(masked, 4 * N_TILES)
            for half in range(2):
                for t in range(NS):
                    at = half * SEL + t * P
                    ins = T.transpose(B[2][:, at:at + P], tab[:, t * 2 * FD + half * P:t * 2 * FD + (half + 1) * P],
                                      ident[:])
            ins.then_inc(tab_ps, 1)
            hidden_transposed(0)
            pe.wait_ge(ht_hi, NK // 2), pe.wait_ge(ht_lo, NK)
            for u in range(before_heads):
                unit(u)
            for h in range(STEPS):
                if h < FH:
                    kv = h // (FH // FKV)
                    pe.wait_ge(unit_lo, kq_unit(h)), pe.wait_ge(cs_ok, 1)
                    if h >= 2:
                        pe.wait_ge(sm_ok, h - 1)
                    for rows, width, at in ((slice(0, P), P, 0), (slice(P, SEL), SEL, P)):
                        ins = split_matmuls(B[2 + h % 2][:, at:at + width], (QRh[:, h, rows], QRl[:, h, rows]),
                                            (KRh[:, kv, 0:width], KRl[:, kv, 0:width]), True, True)
                    ins.then_inc(sc_ps, 1)
                for u in units_of_step.get(h, ()):
                    unit(u)
                if h == 2:
                    pe.wait_ge(unit_lo, before_heads + 2)
                if 1 <= h <= FH:
                    pe.wait_ge(pn_ok, h), pe.wait_ge(pt_lo, h - 1)
                    for n in range(3):
                        ins = T.transpose(B[4][:, n * P:(n + 1) * P], PN[:, (h - 1) % 2, n * P:(n + 1) * P], ident[:])
                    ins.then_inc(pt_ps, 1)
                if 2 <= h <= FH + 1:
                    g = h - 2
                    kv = g // (FH // FKV)
                    cols = slice(kv * FD, (kv + 1) * FD)
                    pe.wait_ge(pt_lo, g + 1), pe.wait_ge(ot_lo, g)
                    split_matmuls(B[5][:, 0:SEL], (Vh[:, 0, cols], Vl[:, 0, cols]),
                                  (PTh[:, g % 2, 0:SEL], PTl[:, g % 2, 0:SEL]), True, False)
                    split_matmuls(B[5][:, P:SEL], (Vh[:, 1, cols], Vl[:, 1, cols]),
                                  (PTh[:, g % 2, SEL:], PTl[:, g % 2, SEL:]), False, True).then_inc(ot_ps, 1)
                if h >= 3:
                    g = h - 3
                    b = block_of[f"O{g // 4}"]
                    if g % 4 == 0:
                        block_ready(b)
                    pe.wait_ge(ot_lo, g + 1)
                    for t in range(NS):
                        rows = slice(t * P, (t + 1) * P)
                        ins = split_matmuls(B[6 + t][:], (OTh[:, g % 2, rows], OTl[:, g % 2, rows]),
                                            (whi[b % 3][:, g % 4, :], wlo[b % 3][:, g % 4, :]), g == 0, g == FH - 1)
                    ins.then_inc(wo_ps, 1)
            hidden_transposed(1)
            pe.wait_ge(ht_hi, NK), pe.wait_ge(ht_lo, 2 * NK)

            def gate_up(j):
                for k, done, first in (("G", g_ps, 0), ("U", u_ps, 2)):
                    b = block_of[f"{k}{j}"]
                    block_ready(b)
                    for p in range(2):
                        m = 2 * j + p
                        if m >= 2:
                            pe.wait_ge(sg_ok if k == "G" else mt_ok, m - 1)
                        ins = pair(B[first + m % 2], b, p)
                        ins.then_inc(done, 1)

            def down(j):
                b = block_of[f"D{j}"]
                block_ready(b)
                pe.wait_ge(mt_hi, 2 * j + 2), pe.wait_ge(mt_lo, 2 * j + 2)
                if j == 0:
                    pe.wait_ge(hs_ok, 2)
                for i in range(4):
                    for t in range(NS):
                        rows = slice(t * P, (t + 1) * P)
                        ins = split_matmuls(B[6 + t][:], (QRh[:, 4 * j + i, rows], QRl[:, 4 * j + i, rows]),
                                            (whi[b % 3][:, i, :], wlo[b % 3][:, i, :]), j == 0 and i == 0,
                                            j == 3 and i == 3)
                ins.then_inc(down_ps, 1)

            for k in order[block_of["G0"]:]:
                if k[0] == "G":
                    gate_up(int(k[1]))
                elif k[0] == "D":
                    down(int(k[1]))


_NAMES = ("w_router", "wq", "bq", "wk", "bk", "wv", "bv", "wo", "w_gate", "w_up", "w_down")


def kernel(**inputs):
    import numpy as np
    import concourse.bacc as bacc
    from concourse.bass_utils import run_bass_kernel_spmd as run

    W = {k: np.asarray(v) for k, v in inputs.items()}
    slopes = W["L0_attn_slope_rate"].reshape(NH)
    per_feature = np.repeat(slopes, DH)
    tile_major = lambda a, n: a.reshape(n, P).T
    freq = (np.float32(1.0) / np.float32(10000.0) ** (np.arange(0, FD, 2, dtype=np.float32) / np.float32(FD)))
    angle = np.arange(N_TOK, dtype=np.float32)[:, None] * freq.astype(np.float32)
    cos, sin = np.cos(angle.astype(np.float64)), np.sin(angle.astype(np.float64))
    rope = np.concatenate([cos, cos, sin, -sin], axis=1).astype(np.float32)
    data = {
        "x": W["L0_attn_x"].reshape(N_TOK, DM), "WT": W["L0_attn_W_qkvu"].T, "WoT": W["L0_attn_W_out"].T,
        "s_hid": tile_major(per_feature, NK), "s_row": per_feature, "s_head": slopes,
        **{n: W["L0_ffn_" + n] for n in _NAMES},
        "ln1": tile_major(W["L0_ffn_ln1_w"], NK), "ln2": tile_major(W["L0_ffn_ln2_w"], NK), "rope": rope,
    }
    data["bq"], data["bk"] = tile_major(data["bq"], FH), tile_major(data["bk"], FKV)
    data = {"in_" + k: np.ascontiguousarray(v) for k, v in data.items()}
    nc = bacc.Bacc("TRN2", target_bir_lowering=False, num_devices=1)
    args = {n[3:]: nc.dram_tensor(n, a.shape, mybir.dt.from_np(a.dtype), kind="ExternalInput").ap()
            for n, a in data.items()}
    scores = nc.dram_tensor("scores", [N_TOK], mybir.dt.float32).ap()
    out = nc.dram_tensor("out", [N_TOK, DM], mybir.dt.float32, kind="ExternalOutput").ap()
    build(nc, scores=scores, out=out, **args)
    r = run(nc, [data], core_ids=[0])
    return r.results[0]["out"].reshape(1, N_TOK, DM)
```
